# Optimizing a Trainium2 kernel written in Bass

```python
import numpy as np
import jax
import jax.numpy as jnp

def _softmax(x, axis=-1):
    return jax.nn.softmax(x, axis=axis)

def _gelu(x):
    return jax.nn.gelu(x, approximate=True)

def _silu(x):
    return jax.nn.silu(x)

def _sigmoid(x):
    return jax.nn.sigmoid(x)

def _layernorm(x, axis=-1, eps=1e-05):
    m = jnp.mean(x, axis=axis, keepdims=True)
    v = jnp.var(x, axis=axis, keepdims=True)
    return (x - m) / jnp.sqrt(v + eps)

def _scatter_add(tgt, idx, src, axis=0):
    return tgt.at[idx].add(src)

def _segment_sum(src, seg, n):
    return jax.ops.segment_sum(src, seg, n)
kernel_name = 'mk_adaln_d2_jaxref_r8_97a993'

def setup_inputs(seed: int=0):
    np.random.seed(seed)
    _w = jnp.asarray

    def _L0_attn_setup():
        import jax, jax.numpy as jnp
        import numpy as np
        HEADS = 16
        DIM_HEAD = 64
        SEG = 64
        THETA = 10000.0
        NEG_INF = -1e+30

        def _rotate_half(t):
            t2 = t.reshape(*t.shape[:-1], t.shape[-1] // 2, 2)
            return jnp.stack((-t2[..., 1], t2[..., 0]), axis=-1).reshape(t.shape)
        key = jax.random.key(seed)
        ks = jax.random.split(key, 4)
        b, n, d = (2, 512, 128)
        dim_inner = HEADS * DIM_HEAD
        seq = jax.random.normal(ks[0], (b, n, d), dtype=jnp.float32)
        g_norm = jnp.ones((d,), dtype=jnp.float32)
        W_qkv = jax.random.normal(ks[1], (d, 3 * dim_inner), dtype=jnp.float32) * d ** (-0.5)
        W_out = jax.random.normal(ks[2], (dim_inner, d), dtype=jnp.float32) * dim_inner ** (-0.5)
        pm = jax.random.normal(ks[3], (2, HEADS, 16, DIM_HEAD), dtype=jnp.float32) * 0.02
        return {'seq': seq, 'g_norm': g_norm, 'W_qkv': W_qkv, 'W_out': W_out, 'pm': pm}
    _L0_attn_in = _L0_attn_setup()

    def _L0_ffn_setup():
        import jax, jax.numpy as jnp
        import numpy as np
        H = 128
        I = 88
        E = 64
        TOP_K = 8
        NG = 8
        TOPK_GROUP = 4
        N_SHARED = 2
        ROUTED_SCALE = 2.5
        S_I = I * N_SHARED

        def _route(x, gate_w, gate_bias):
            T = x.shape[0]
            logits = x @ gate_w.T
            scores = jax.nn.sigmoid(logits)
            scores_for_choice = scores + gate_bias[None, :]
            grp = scores_for_choice.reshape(T, NG, E // NG)
            group_scores = jnp.sum(jax.lax.top_k(grp, 2)[0], axis=-1)
            _, gidx = jax.lax.top_k(group_scores, TOPK_GROUP)
            gmask = jnp.zeros((T, NG), dtype=scores.dtype).at[jnp.arange(T)[:, None], gidx].set(1.0)
            emask = jnp.repeat(gmask, E // NG, axis=1)
            masked = jnp.where(emask > 0, scores_for_choice, 0.0)
            _, topk_idx = jax.lax.top_k(masked, TOP_K)
            topk_w = jnp.take_along_axis(scores, topk_idx, axis=1)
            topk_w = topk_w / (jnp.sum(topk_w, axis=-1, keepdims=True) + 1e-20)
            topk_w = topk_w * ROUTED_SCALE
            rw = jnp.zeros((T, E), dtype=scores.dtype).at[jnp.arange(T)[:, None], topk_idx].add(topk_w)
            return rw

        def _mlp(x, gw, uw, dw):
            return jax.nn.silu(x @ gw.T) * (x @ uw.T) @ dw.T
        key = jax.random.key(seed)
        ks = jax.random.split(key, 10)
        sc = 0.02
        return {'hidden_states': jax.random.normal(ks[0], (1, 128, H), dtype=jnp.float32), 'gate_w': sc * jax.random.normal(ks[1], (E, H), dtype=jnp.float32), 'gate_bias': sc * jax.random.normal(ks[2], (E,), dtype=jnp.float32), 'Wg': sc * jax.random.normal(ks[3], (E, I, H), dtype=jnp.float32), 'Wu': sc * jax.random.normal(ks[4], (E, I, H), dtype=jnp.float32), 'Wd': sc * jax.random.normal(ks[5], (E, H, I), dtype=jnp.float32), 'Sg': sc * jax.random.normal(ks[6], (S_I, H), dtype=jnp.float32), 'Su': sc * jax.random.normal(ks[7], (S_I, H), dtype=jnp.float32), 'Sd': sc * jax.random.normal(ks[8], (H, S_I), dtype=jnp.float32)}
    _L0_ffn_in = _L0_ffn_setup()
    _L0_c = _w((lambda *s: np.random.randn(*s).astype(np.float32) * 0.05)(2, 128))
    _L0_wmod = _w((lambda *s: np.random.randn(*s).astype(np.float32) * 0.05)(128, 6 * 128) * 128 ** (-0.5))

    def _L1_attn_setup():
        import jax, jax.numpy as jnp
        import numpy as np
        B, L = (2, 256)
        D_MODEL = 128
        D_STATE = 128
        D_CONV = 4
        EXPAND = 2
        HEADDIM = 64
        D_HALF = D_MODEL // 2
        D_INNER = EXPAND * D_HALF
        NHEADS = D_INNER // HEADDIM
        CONV_DIM = D_INNER + 2 * D_STATE
        D_IN_PROJ = 2 * D_INNER + 2 * D_STATE + NHEADS
        EPS = 1e-05

        def _rmsnorm(x, w):
            return x * jax.lax.rsqrt(jnp.mean(x * x, axis=-1, keepdims=True) + EPS) * w

        def _mamba2(u, in_w, conv_w, conv_b, dt_bias, A_log, D, gnorm_w, outp_w):
            b, l, _ = u.shape
            zxbcdt = u @ in_w.T
            z = zxbcdt[..., :D_INNER]
            xBC = zxbcdt[..., D_INNER:D_INNER + CONV_DIM]
            dt = zxbcdt[..., D_INNER + CONV_DIM:]
            xp = jnp.pad(xBC, ((0, 0), (D_CONV - 1, 0), (0, 0)))
            conv = conv_b + sum((xp[:, k:k + l, :] * conv_w[:, k] for k in range(D_CONV)))
            xBC = jax.nn.silu(conv)
            x = xBC[..., :D_INNER]
            Bm = xBC[..., D_INNER:D_INNER + D_STATE]
            Cm = xBC[..., D_INNER + D_STATE:]
            dt = jax.nn.softplus(dt + dt_bias)
            A = -jnp.exp(A_log)
            xh = x.reshape(b, l, NHEADS, HEADDIM)
            dA = jnp.exp(dt * A)
            dtx = dt[..., None] * xh

            def step(h, inp):
                dA_t, dtx_t, B_t, C_t = inp
                h = dA_t[:, :, None, None] * h + jnp.einsum('bhp,bn->bhpn', dtx_t, B_t)
                return (h, jnp.einsum('bhpn,bn->bhp', h, C_t))
            h0 = jnp.zeros((b, NHEADS, HEADDIM, D_STATE), u.dtype)
            xs = (jnp.moveaxis(dA, 1, 0), jnp.moveaxis(dtx, 1, 0), jnp.moveaxis(Bm, 1, 0), jnp.moveaxis(Cm, 1, 0))
            _, ys = jax.lax.scan(step, h0, xs)
            y = jnp.moveaxis(ys, 0, 1) + xh * D[None, None, :, None]
            y = y.reshape(b, l, D_INNER) * jax.nn.silu(z)
            y = _rmsnorm(y, gnorm_w)
            return y @ outp_w.T

        def _forward(x, norm_w, op_w, op_b, f_in_w, f_conv_w, f_conv_b, f_dt_bias, f_A_log, f_D, f_gnorm_w, f_outp_w, b_in_w, b_conv_w, b_conv_b, b_dt_bias, b_A_log, b_D, b_gnorm_w, b_outp_w):
            xn = _rmsnorm(x, norm_w)
            x_f, x_b = (xn[..., :D_HALF], xn[..., D_HALF:])
            out_f = _mamba2(x_f, f_in_w, f_conv_w, f_conv_b, f_dt_bias, f_A_log, f_D, f_gnorm_w, f_outp_w)
            out_b = jnp.flip(_mamba2(jnp.flip(x_b, 1), b_in_w, b_conv_w, b_conv_b, b_dt_bias, b_A_log, b_D, b_gnorm_w, b_outp_w), 1)
            out = jnp.concatenate([out_f, out_b], axis=-1) @ op_w.T + op_b
            return x + out

        def _mamba_params(key, prefix):
            k = jax.random.split(key, 5)
            return {prefix + 'in_w': jax.random.normal(k[0], (D_IN_PROJ, D_HALF), jnp.float32) * 0.02, prefix + 'conv_w': jax.random.normal(k[1], (CONV_DIM, D_CONV), jnp.float32) * 0.2, prefix + 'conv_b': jnp.zeros((CONV_DIM,), jnp.float32), prefix + 'dt_bias': jax.random.normal(k[2], (NHEADS,), jnp.float32) * 0.1, prefix + 'A_log': jnp.log(jax.random.uniform(k[3], (NHEADS,), jnp.float32, 1.0, 16.0)), prefix + 'D': jnp.ones((NHEADS,), jnp.float32), prefix + 'gnorm_w': jnp.ones((D_INNER,), jnp.float32), prefix + 'outp_w': jax.random.normal(k[4], (D_HALF, D_INNER), jnp.float32) * 0.02}
        key = jax.random.key(seed)
        k = jax.random.split(key, 4)
        inp = {'x': jax.random.normal(k[0], (B, L, D_MODEL), jnp.float32), 'norm_w': jnp.ones((D_MODEL,), jnp.float32), 'op_w': jax.random.normal(k[1], (D_MODEL, D_MODEL), jnp.float32) * 0.02, 'op_b': jnp.zeros((D_MODEL,), jnp.float32)}
        inp.update(_mamba_params(k[2], 'f_'))
        inp.update(_mamba_params(k[3], 'b_'))
        return inp
    _L1_attn_in = _L1_attn_setup()

    def _L1_ffn_setup():
        import jax, jax.numpy as jnp
        import numpy as np
        N_BLOCKS = 16
        BLOCK = 32
        TOP_K = N_BLOCKS // 4
        key = jax.random.key(seed)
        ks = jax.random.split(key, 7)
        D, H = (128, 512)
        s = lambda k, shape, scale: jax.random.normal(k, shape, dtype=jnp.float32) * scale
        return {'x': s(ks[0], (4, 512, D), 1.0), 'w_router': s(ks[1], (D, N_BLOCKS), 0.03), 'b_router': s(ks[2], (N_BLOCKS,), 0.01), 'w1': s(ks[3], (H, D), 0.03), 'b1': s(ks[4], (H,), 0.01), 'w2': s(ks[5], (D, H), 0.03), 'b2': s(ks[6], (D,), 0.01)}
    _L1_ffn_in = _L1_ffn_setup()
    _L1_c = _w((lambda *s: np.random.randn(*s).astype(np.float32) * 0.05)(2, 128))
    _L1_wmod = _w((lambda *s: np.random.randn(*s).astype(np.float32) * 0.05)(128, 6 * 128) * 128 ** (-0.5))
    _d = {'L0_attn_seq': _L0_attn_in['seq'], 'L0_attn_g_norm': _L0_attn_in['g_norm'], 'L0_attn_W_qkv': _L0_attn_in['W_qkv'], 'L0_attn_W_out': _L0_attn_in['W_out'], 'L0_attn_pm': _L0_attn_in['pm'], 'L0_ffn_gate_w': _L0_ffn_in['gate_w'], 'L0_ffn_gate_bias': _L0_ffn_in['gate_bias'], 'L0_ffn_Wg': _L0_ffn_in['Wg'], 'L0_ffn_Wu': _L0_ffn_in['Wu'], 'L0_ffn_Wd': _L0_ffn_in['Wd'], 'L0_ffn_Sg': _L0_ffn_in['Sg'], 'L0_ffn_Su': _L0_ffn_in['Su'], 'L0_ffn_Sd': _L0_ffn_in['Sd'], 'L0_c': _L0_c, 'L0_wmod': _L0_wmod, 'L1_attn_norm_w': _L1_attn_in['norm_w'], 'L1_attn_op_w': _L1_attn_in['op_w'], 'L1_attn_op_b': _L1_attn_in['op_b'], 'L1_attn_f_in_w': _L1_attn_in['f_in_w'], 'L1_attn_f_conv_w': _L1_attn_in['f_conv_w'], 'L1_attn_f_conv_b': _L1_attn_in['f_conv_b'], 'L1_attn_f_dt_bias': _L1_attn_in['f_dt_bias'], 'L1_attn_f_A_log': _L1_attn_in['f_A_log'], 'L1_attn_f_D': _L1_attn_in['f_D'], 'L1_attn_f_gnorm_w': _L1_attn_in['f_gnorm_w'], 'L1_attn_f_outp_w': _L1_attn_in['f_outp_w'], 'L1_attn_b_in_w': _L1_attn_in['b_in_w'], 'L1_attn_b_conv_w': _L1_attn_in['b_conv_w'], 'L1_attn_b_conv_b': _L1_attn_in['b_conv_b'], 'L1_attn_b_dt_bias': _L1_attn_in['b_dt_bias'], 'L1_attn_b_A_log': _L1_attn_in['b_A_log'], 'L1_attn_b_D': _L1_attn_in['b_D'], 'L1_attn_b_gnorm_w': _L1_attn_in['b_gnorm_w'], 'L1_attn_b_outp_w': _L1_attn_in['b_outp_w'], 'L1_ffn_w_router': _L1_ffn_in['w_router'], 'L1_ffn_b_router': _L1_ffn_in['b_router'], 'L1_ffn_w1': _L1_ffn_in['w1'], 'L1_ffn_b1': _L1_ffn_in['b1'], 'L1_ffn_w2': _L1_ffn_in['w2'], 'L1_ffn_b2': _L1_ffn_in['b2'], 'L1_c': _L1_c, 'L1_wmod': _L1_wmod}
    _x0 = _d['L0_attn_seq']
    _d['L0_attn_seq'] = jax.random.normal(jax.random.fold_in(jax.random.key(seed), 1), (2, 1024, 128), dtype=_x0.dtype)
    del _x0
    return _d

def reference(L0_attn_seq, L0_attn_g_norm, L0_attn_W_qkv, L0_attn_W_out, L0_attn_pm, L0_ffn_gate_w, L0_ffn_gate_bias, L0_ffn_Wg, L0_ffn_Wu, L0_ffn_Wd, L0_ffn_Sg, L0_ffn_Su, L0_ffn_Sd, L0_c, L0_wmod, L1_attn_norm_w, L1_attn_op_w, L1_attn_op_b, L1_attn_f_in_w, L1_attn_f_conv_w, L1_attn_f_conv_b, L1_attn_f_dt_bias, L1_attn_f_A_log, L1_attn_f_D, L1_attn_f_gnorm_w, L1_attn_f_outp_w, L1_attn_b_in_w, L1_attn_b_conv_w, L1_attn_b_conv_b, L1_attn_b_dt_bias, L1_attn_b_A_log, L1_attn_b_D, L1_attn_b_gnorm_w, L1_attn_b_outp_w, L1_ffn_w_router, L1_ffn_b_router, L1_ffn_w1, L1_ffn_b1, L1_ffn_w2, L1_ffn_b2, L1_c, L1_wmod):

    def _L0_attn_ref(seq, g_norm, W_qkv, W_out, pm):
        import jax, jax.numpy as jnp
        import numpy as np
        HEADS = 16
        DIM_HEAD = 64
        SEG = 64
        THETA = 10000.0
        NEG_INF = -1e+30

        def _rotate_half(t):
            t2 = t.reshape(*t.shape[:-1], t.shape[-1] // 2, 2)
            return jnp.stack((-t2[..., 1], t2[..., 0]), axis=-1).reshape(t.shape)
        b, n_tot, dim = seq.shape
        p = pm.shape[2]
        dh = DIM_HEAD
        eps = jnp.asarray(jnp.finfo(seq.dtype).eps, seq.dtype)
        x = seq * jax.lax.rsqrt(jnp.mean(seq * seq, axis=-1, keepdims=True) + eps) * g_norm
        qkv = x @ W_qkv
        q, k, v = jnp.split(qkv, 3, axis=-1)

        def split_heads(t):
            return t.reshape(b, n_tot, HEADS, dh).transpose(0, 2, 1, 3)
        q, k, v = map(split_heads, (q, k, v))
        pos = jnp.arange(n_tot, dtype=seq.dtype)
        inv_freq = 1.0 / THETA ** (jnp.arange(0, dh, 2, dtype=seq.dtype) / dh)
        ang = jnp.repeat(pos[:, None] * inv_freq, 2, axis=-1)
        cos, sin = (jnp.cos(ang), jnp.sin(ang))
        q = q * cos + _rotate_half(q) * sin
        k = k * cos + _rotate_half(k) * sin
        w = n_tot // SEG

        def seg_fold(t):
            return t.reshape(b, HEADS, w, SEG, dh).transpose(0, 2, 1, 3, 4).reshape(b * w, HEADS, SEG, dh)
        q, k, v = map(seg_fold, (q, k, v))
        pmk = jnp.broadcast_to(pm[0], (b * w, HEADS, p, dh))
        pmv = jnp.broadcast_to(pm[1], (b * w, HEADS, p, dh))
        k = jnp.concatenate((pmk, k), axis=-2)
        v = jnp.concatenate((pmv, v), axis=-2)
        scores = jnp.einsum('bhid,bhjd->bhij', q, k) * dh ** (-0.5)
        i = jnp.arange(SEG)[:, None]
        j = jnp.arange(SEG + p)[None, :]
        mask = (j < p) | (j - p <= i)
        scores = jnp.where(mask, scores, NEG_INF)
        attn = jax.nn.softmax(scores, axis=-1)
        out = jnp.einsum('bhij,bhjd->bhid', attn, v)
        out = out.transpose(0, 2, 1, 3).reshape(b * w, SEG, HEADS * dh)
        out = out @ W_out
        return out.reshape(b, n_tot, dim)

    def _L0_ffn_ref(hidden_states, gate_w, gate_bias, Wg, Wu, Wd, Sg, Su, Sd):
        import jax, jax.numpy as jnp
        import numpy as np
        H = 128
        I = 88
        E = 64
        TOP_K = 8
        NG = 8
        TOPK_GROUP = 4
        N_SHARED = 2
        ROUTED_SCALE = 2.5
        S_I = I * N_SHARED

        def _route(x, gate_w, gate_bias):
            T = x.shape[0]
            logits = x @ gate_w.T
            scores = jax.nn.sigmoid(logits)
            scores_for_choice = scores + gate_bias[None, :]
            grp = scores_for_choice.reshape(T, NG, E // NG)
            group_scores = jnp.sum(jax.lax.top_k(grp, 2)[0], axis=-1)
            _, gidx = jax.lax.top_k(group_scores, TOPK_GROUP)
            gmask = jnp.zeros((T, NG), dtype=scores.dtype).at[jnp.arange(T)[:, None], gidx].set(1.0)
            emask = jnp.repeat(gmask, E // NG, axis=1)
            masked = jnp.where(emask > 0, scores_for_choice, 0.0)
            _, topk_idx = jax.lax.top_k(masked, TOP_K)
            topk_w = jnp.take_along_axis(scores, topk_idx, axis=1)
            topk_w = topk_w / (jnp.sum(topk_w, axis=-1, keepdims=True) + 1e-20)
            topk_w = topk_w * ROUTED_SCALE
            rw = jnp.zeros((T, E), dtype=scores.dtype).at[jnp.arange(T)[:, None], topk_idx].add(topk_w)
            return rw

        def _mlp(x, gw, uw, dw):
            return jax.nn.silu(x @ gw.T) * (x @ uw.T) @ dw.T
        B, S, _ = hidden_states.shape
        x = hidden_states.reshape(B * S, H)
        rw = _route(x, gate_w, gate_bias)
        expert_out = jax.vmap(lambda gw_, uw_, dw_: _mlp(x, gw_, uw_, dw_))(Wg, Wu, Wd)
        routed = jnp.einsum('eth,te->th', expert_out, rw)
        shared = _mlp(x, Sg, Su, Sd)
        out = (routed + shared).reshape(B, S, H)
        return out

    def _L1_attn_ref(x, norm_w, op_w, op_b, f_in_w, f_conv_w, f_conv_b, f_dt_bias, f_A_log, f_D, f_gnorm_w, f_outp_w, b_in_w, b_conv_w, b_conv_b, b_dt_bias, b_A_log, b_D, b_gnorm_w, b_outp_w):
        import jax, jax.numpy as jnp
        import numpy as np
        B, L = (2, 256)
        D_MODEL = 128
        D_STATE = 128
        D_CONV = 4
        EXPAND = 2
        HEADDIM = 64
        D_HALF = D_MODEL // 2
        D_INNER = EXPAND * D_HALF
        NHEADS = D_INNER // HEADDIM
        CONV_DIM = D_INNER + 2 * D_STATE
        D_IN_PROJ = 2 * D_INNER + 2 * D_STATE + NHEADS
        EPS = 1e-05

        def _rmsnorm(x, w):
            return x * jax.lax.rsqrt(jnp.mean(x * x, axis=-1, keepdims=True) + EPS) * w

        def _mamba2(u, in_w, conv_w, conv_b, dt_bias, A_log, D, gnorm_w, outp_w):
            b, l, _ = u.shape
            zxbcdt = u @ in_w.T
            z = zxbcdt[..., :D_INNER]
            xBC = zxbcdt[..., D_INNER:D_INNER + CONV_DIM]
            dt = zxbcdt[..., D_INNER + CONV_DIM:]
            xp = jnp.pad(xBC, ((0, 0), (D_CONV - 1, 0), (0, 0)))
            conv = conv_b + sum((xp[:, k:k + l, :] * conv_w[:, k] for k in range(D_CONV)))
            xBC = jax.nn.silu(conv)
            x = xBC[..., :D_INNER]
            Bm = xBC[..., D_INNER:D_INNER + D_STATE]
            Cm = xBC[..., D_INNER + D_STATE:]
            dt = jax.nn.softplus(dt + dt_bias)
            A = -jnp.exp(A_log)
            xh = x.reshape(b, l, NHEADS, HEADDIM)
            dA = jnp.exp(dt * A)
            dtx = dt[..., None] * xh

            def step(h, inp):
                dA_t, dtx_t, B_t, C_t = inp
                h = dA_t[:, :, None, None] * h + jnp.einsum('bhp,bn->bhpn', dtx_t, B_t)
                return (h, jnp.einsum('bhpn,bn->bhp', h, C_t))
            h0 = jnp.zeros((b, NHEADS, HEADDIM, D_STATE), u.dtype)
            xs = (jnp.moveaxis(dA, 1, 0), jnp.moveaxis(dtx, 1, 0), jnp.moveaxis(Bm, 1, 0), jnp.moveaxis(Cm, 1, 0))
            _, ys = jax.lax.scan(step, h0, xs)
            y = jnp.moveaxis(ys, 0, 1) + xh * D[None, None, :, None]
            y = y.reshape(b, l, D_INNER) * jax.nn.silu(z)
            y = _rmsnorm(y, gnorm_w)
            return y @ outp_w.T

        def _forward(x, norm_w, op_w, op_b, f_in_w, f_conv_w, f_conv_b, f_dt_bias, f_A_log, f_D, f_gnorm_w, f_outp_w, b_in_w, b_conv_w, b_conv_b, b_dt_bias, b_A_log, b_D, b_gnorm_w, b_outp_w):
            xn = _rmsnorm(x, norm_w)
            x_f, x_b = (xn[..., :D_HALF], xn[..., D_HALF:])
            out_f = _mamba2(x_f, f_in_w, f_conv_w, f_conv_b, f_dt_bias, f_A_log, f_D, f_gnorm_w, f_outp_w)
            out_b = jnp.flip(_mamba2(jnp.flip(x_b, 1), b_in_w, b_conv_w, b_conv_b, b_dt_bias, b_A_log, b_D, b_gnorm_w, b_outp_w), 1)
            out = jnp.concatenate([out_f, out_b], axis=-1) @ op_w.T + op_b
            return x + out

        def _mamba_params(key, prefix):
            k = jax.random.split(key, 5)
            return {prefix + 'in_w': jax.random.normal(k[0], (D_IN_PROJ, D_HALF), jnp.float32) * 0.02, prefix + 'conv_w': jax.random.normal(k[1], (CONV_DIM, D_CONV), jnp.float32) * 0.2, prefix + 'conv_b': jnp.zeros((CONV_DIM,), jnp.float32), prefix + 'dt_bias': jax.random.normal(k[2], (NHEADS,), jnp.float32) * 0.1, prefix + 'A_log': jnp.log(jax.random.uniform(k[3], (NHEADS,), jnp.float32, 1.0, 16.0)), prefix + 'D': jnp.ones((NHEADS,), jnp.float32), prefix + 'gnorm_w': jnp.ones((D_INNER,), jnp.float32), prefix + 'outp_w': jax.random.normal(k[4], (D_HALF, D_INNER), jnp.float32) * 0.02}
        return _forward(x, norm_w, op_w, op_b, f_in_w, f_conv_w, f_conv_b, f_dt_bias, f_A_log, f_D, f_gnorm_w, f_outp_w, b_in_w, b_conv_w, b_conv_b, b_dt_bias, b_A_log, b_D, b_gnorm_w, b_outp_w)

    def _L1_ffn_ref(x, w_router, b_router, w1, b1, w2, b2):
        import jax, jax.numpy as jnp
        import numpy as np
        N_BLOCKS = 16
        BLOCK = 32
        TOP_K = N_BLOCKS // 4
        orig_shape = x.shape
        D = orig_shape[-1]
        xf = x.reshape(-1, D)
        prob = jax.nn.softmax(xf @ w_router + b_router, axis=-1)
        _, idx = jax.lax.top_k(prob, TOP_K)
        mask = (idx[:, :, None] == jnp.arange(N_BLOCKS)[None, None, :]).any(axis=1)
        mask = mask.astype(x.dtype)
        w1b = w1.reshape(N_BLOCKS, BLOCK, D)
        b1b = b1.reshape(N_BLOCKS, BLOCK)
        w2b = jnp.transpose(w2.reshape(D, N_BLOCKS, BLOCK), (1, 2, 0))
        h = jax.nn.relu(jnp.einsum('nd,ebd->neb', xf, w1b) + b1b[None])
        y = jnp.einsum('neb,ebd,ne->nd', h, w2b, mask)
        y = y + b2[None, :]
        return y.reshape(orig_shape)
    x = L0_attn_seq
    mod = (_silu(L0_c) @ L0_wmod).reshape(L0_c.shape[0], 6, 1, -1)
    sa, ca, ga, sb, cb, gb = (mod[:, 0], mod[:, 1], mod[:, 2], mod[:, 3], mod[:, 4], mod[:, 5])
    ga = (2 * (ga >= 0) - 1) * jnp.maximum(jnp.abs(ga), 0.25)
    gb = (2 * (gb >= 0) - 1) * jnp.maximum(jnp.abs(gb), 0.25)
    h = _layernorm(x, axis=-1) * (1 + ca) + sa
    x = x + ga * _L0_attn_ref(h, L0_attn_g_norm, L0_attn_W_qkv, L0_attn_W_out, L0_attn_pm)
    h = _layernorm(x, axis=-1) * (1 + cb) + sb
    x = x + gb * _L0_ffn_ref(h, L0_ffn_gate_w, L0_ffn_gate_bias, L0_ffn_Wg, L0_ffn_Wu, L0_ffn_Wd, L0_ffn_Sg, L0_ffn_Su, L0_ffn_Sd)
    mod = (_silu(L1_c) @ L1_wmod).reshape(L1_c.shape[0], 6, 1, -1)
    sa, ca, ga, sb, cb, gb = (mod[:, 0], mod[:, 1], mod[:, 2], mod[:, 3], mod[:, 4], mod[:, 5])
    ga = (2 * (ga >= 0) - 1) * jnp.maximum(jnp.abs(ga), 0.25)
    gb = (2 * (gb >= 0) - 1) * jnp.maximum(jnp.abs(gb), 0.25)
    h = _layernorm(x, axis=-1) * (1 + ca) + sa
    x = x + ga * _L1_attn_ref(h, L1_attn_norm_w, L1_attn_op_w, L1_attn_op_b, L1_attn_f_in_w, L1_attn_f_conv_w, L1_attn_f_conv_b, L1_attn_f_dt_bias, L1_attn_f_A_log, L1_attn_f_D, L1_attn_f_gnorm_w, L1_attn_f_outp_w, L1_attn_b_in_w, L1_attn_b_conv_w, L1_attn_b_conv_b, L1_attn_b_dt_bias, L1_attn_b_A_log, L1_attn_b_D, L1_attn_b_gnorm_w, L1_attn_b_outp_w)
    h = _layernorm(x, axis=-1) * (1 + cb) + sb
    x = x + gb * _L1_ffn_ref(h, L1_ffn_w_router, L1_ffn_b_router, L1_ffn_w1, L1_ffn_b1, L1_ffn_w2, L1_ffn_b2)
    return x

_drawn_inputs = setup_inputs


def setup_inputs(seed=0):
    import zlib

    import numpy as np

    out = dict(_drawn_inputs(seed))
    spreads = {'L0_attn_g_norm': (1.0, 0.6),
     'L1_attn_norm_w': (1.0, 0.6),
     'L1_attn_op_b': (0.0, 0.369),
     'L1_attn_f_conv_b': (0.0, 0.8),
     'L1_attn_f_D': (1.0, 0.6),
     'L1_attn_f_gnorm_w': (1.0, 0.6),
     'L1_attn_b_conv_b': (0.0, 0.8),
     'L1_attn_b_D': (1.0, 0.6),
     'L1_attn_b_gnorm_w': (1.0, 0.6)}
    factors = {'L0_attn_pm': 8.0,
     'L0_ffn_gate_w': 8.0,
     'L0_ffn_gate_bias': 8.0,
     'L0_ffn_Wg': 8.0,
     'L0_ffn_Wu': 8.0,
     'L0_ffn_Wd': 8.0,
     'L0_ffn_Sg': 8.0,
     'L0_ffn_Su': 8.0,
     'L0_ffn_Sd': 8.0,
     'L1_attn_op_w': 5.163,
     'L1_attn_f_in_w': 7.432,
     'L1_attn_f_conv_w': 8.0,
     'L1_attn_f_dt_bias': 8.0,
     'L1_attn_f_A_log': 8.0,
     'L1_attn_f_outp_w': 7.374,
     'L1_attn_b_in_w': 7.111,
     'L1_attn_b_conv_w': 8.0,
     'L1_attn_b_dt_bias': 8.0,
     'L1_attn_b_A_log': 8.0,
     'L1_attn_b_outp_w': 7.019,
     'L1_ffn_w_router': 3.395,
     'L1_ffn_b_router': 8.0,
     'L1_ffn_w1': 3.516,
     'L1_ffn_b1': 61.947,
     'L1_ffn_w2': 2.915,
     'L1_ffn_b2': 39.095}
    for name, (base, spread) in spreads.items():
        noise = np.random.default_rng([zlib.crc32(name.encode()), seed]).standard_normal(out[name].shape)
        drawn = base * np.exp(spread * noise) if base else spread * noise
        out[name] = jnp.asarray(drawn.astype(out[name].dtype))
    for name, factor in factors.items():
        out[name] = (out[name] * factor).astype(out[name].dtype)
    return out
```

```python
from contextlib import ExitStack

import numpy as np

import concourse.bass as bass
from concourse import mybir

F32 = mybir.dt.float32
BF16 = mybir.dt.bfloat16
ALU = mybir.AluOpType
ACT = mybir.ActivationFunctionType
AX = mybir.AxisListType

P = 128
BATCH, SEQ = 2, 1024
TOK = BATCH * SEQ
TILES = TOK // P
BLK = 512
BLKS = TOK // BLK
HEADS, DH, SEG, PM = 16, 64, 64, 16
PAIRS = HEADS // 2
KEYS = SEG + PM
ITER = 256
ITERS = TOK // ITER
SEGS = ITER // SEG
QG = 4
UNITS = (ITER // P) * HEADS // QG
EXPERTS, FF, TOPK, GROUPS, TOPG = 64, 88, 8, 8, 4
GSIZE = EXPERTS // GROUPS
CHUNKS = EXPERTS * FF // P + 2
NST, HD = 128, 64
CONVPAD = 6
BLOCKS16, FBLK, FTOP = 16, 32, 4
HID1 = BLOCKS16 * FBLK
BIG = 1e30


class Shared:
    pass


def alloc(nc, ctx):
    def sb(name, shape, dt=F32):
        return ctx.enter_context(nc.sbuf_tensor(name, shape, dt))

    def ps(name, shape, dt=F32):
        return ctx.enter_context(nc.psum_tensor(name, shape, dt))

    def sem(name):
        return ctx.enter_context(nc.semaphore(name))
    return sb, ps, sem


def stage_modulation(nc, d, g):
    with ExitStack() as ctx:
        sb, ps, sem = alloc(nc, ctx)
        ct = sb("ct", [P, 2, BATCH])
        st = sb("st", [P, 2, BATCH])
        wmod = sb("wmod", [P, 2, 6 * P])
        mag = sb("mag", [P, 2, 2, BATCH])
        sgn = sb("sgn", [P, 2, 2, BATCH])
        mp = ps("mp", [P, 2, 6, BATCH])
        s_c, s_x, s_silu, s_mod, s_dve = sem("m_c"), sem("m_x"), sem("m_silu"), sem("m_mod"), sem("m_dve")
        block = ctx.enter_context(nc.Block())

        @block.sync
        def _(sp):
            sp.dma_start(ct[:, :, :], d["ct"]).then_inc(s_c, 16)
            sp.dma_start(wmod[:, :, :], d["wmod"]).then_inc(s_c, 16)
            sp.dma_start(g.X[:, :], d["xT"]).then_inc(s_x, 16)
            sp.dma_start(g.ident[:, :], d["ident"]).then_inc(s_x, 16)
            sp.dma_start(g.center[:, :], d["center"]).then_inc(s_x, 16)
            sp.dma_start(g.vecs[:, :], d["vecs"]).then_inc(s_x, 16)
            sp.wait_ge(s_x, 64)

        @block.scalar
        def _(act):
            act.wait_ge(s_c, 32)
            nc.scalar.activation(st[:, :, :], ct[:, :, :], ACT.Silu).then_inc(s_silu, 1)

        @block.tensor
        def _(pe):
            pe.wait_ge(s_silu, 1)
            for layer in range(2):
                for v in range(6):
                    mm = nc.tensor.matmul(mp[:, layer, v, :], wmod[:, layer, v * P:(v + 1) * P],
                                          st[:, layer, :], start=True, stop=True)
            mm.then_inc(s_mod, 1)

        @block.vector
        def _(dve):
            nc.vector.memset(g.mean_col[:, :], 1.0 / P).then_inc(s_dve, 1)
            nc.vector.memset(g.ones[:, :], 1.0).then_inc(s_dve, 1)
            dve.wait_ge(s_mod, 1)
            nc.vector.tensor_copy(g.mod[:, :, :, :], mp[:, :, :, :]).then_inc(s_dve, 1)
            dve.wait_ge(s_dve, 3)
            for n, v in enumerate((1, 4)):
                nc.vector.tensor_scalar(g.mod[:, :, v, :], g.mod[:, :, v, :], 1.0, None, ALU.add).then_inc(s_dve, 1)
            gates = g.mod[:, :, 2:6:3, :]
            nc.vector.tensor_scalar(mag[:, :, :, :], gates, -1.0, None, ALU.mult).then_inc(s_dve, 1)
            nc.vector.tensor_scalar(sgn[:, :, :, :], gates, 0.0, 2.0, ALU.is_ge, ALU.mult).then_inc(s_dve, 1)
            dve.wait_ge(s_dve, 7)
            nc.vector.tensor_tensor(mag[:, :, :, :], mag[:, :, :, :], gates, ALU.max).then_inc(s_dve, 1)
            nc.vector.tensor_scalar(sgn[:, :, :, :], sgn[:, :, :, :], -1.0, None, ALU.add).then_inc(s_dve, 1)
            dve.wait_ge(s_dve, 9)
            nc.vector.tensor_scalar(mag[:, :, :, :], mag[:, :, :, :], 0.25, None, ALU.max).then_inc(s_dve, 1)
            dve.wait_ge(s_dve, 10)
            nc.vector.tensor_tensor(gates, mag[:, :, :, :], sgn[:, :, :, :], ALU.mult).then_inc(s_dve, 1)


def stage_norm(nc, g, tag, layer, half, rms=None):
    norms = 2 if rms else 1
    scale, shift = (1, 0) if half == 0 else (4, 3)
    with ExitStack() as ctx:
        sb, ps, sem = alloc(nc, ctx)
        D = sb(tag + "D", [P, TOK])
        SQ = sb(tag + "SQ", [P, norms, TOK])
        ST = sb(tag + "ST", [P, norms, TILES])
        R = sb(tag + "R", [P, norms, TILES])
        DG = sb(tag + "DG", [P, norms, TOK])
        XN = sb(tag + "XN", [P, TOK])
        eps = sb(tag + "eps", [P, norms])
        d_ps = ps(tag + "d_ps", [P, 2, BLK])
        ms_ps = ps(tag + "ms_ps", [P, 2, BLK])
        r_ps = ps(tag + "r_ps", [P, 2, BLK])
        s_eps, s_cent, s_dcopy = sem(tag + "eps"), sem(tag + "cent"), sem(tag + "dcopy")
        s_sq, s_ms, s_root, s_inv, s_diag = (sem(tag + n) for n in ("sq", "ms", "root", "inv", "diag"))
        s_r, s_xn, s_h, s_u = (sem(tag + n) for n in ("r", "xn", "h", "u"))
        block = ctx.enter_context(nc.Block())
        TB = BLK // P

        def cols(b):
            return slice(b * BLK, (b + 1) * BLK)

        @block.tensor
        def _(pe):
            def mean_square(n, b):
                pe.wait_ge(s_sq, n * BLKS + b + 1)
                if n * BLKS + b >= 2:
                    pe.wait_ge(s_root, n * BLKS + b - 1)
                for t in range(TB * b, TB * b + TB):
                    mm = nc.tensor.matmul(ms_ps[:, b % 2, t:t + 1], SQ[:, n, t * P:(t + 1) * P], g.mean_col[:, :],
                                          start=True, stop=True)
                mm.then_inc(s_ms, 1)

            def broadcast(n, b):
                pe.wait_ge(s_diag, n * BLKS + b + 1)
                i = n * BLKS + b
                if n == 0 and b >= 2:
                    pe.wait_ge(s_xn, b - 1)
                if n == 1:
                    pe.wait_ge(s_xn, b + 3 if b < 2 else BLKS)
                    if b >= 2:
                        pe.wait_ge(s_u, b - 1)
                nc.tensor.matmul(r_ps[:, i % 2, :], g.ones[:, :], DG[:, n, cols(b)], start=True, stop=True).then_inc(s_r, 1)

            for b in range(BLKS):
                if b >= 2:
                    pe.wait_ge(s_dcopy, b - 1)
                nc.tensor.matmul(d_ps[:, b % 2, :], g.center[:, :], g.X[:, cols(b)], start=True, stop=True).then_inc(s_cent, 1)
                if b >= 1:
                    mean_square(0, b - 1)
            mean_square(0, BLKS - 1)
            for n in range(norms):
                for b in range(BLKS):
                    broadcast(n, b)
                    if n == 0 and norms == 2:
                        mean_square(1, b)

        @block.scalar
        def _(act):
            act.wait_ge(s_eps, norms)
            nc.scalar.preload_act_table(ACT.Sqrt)

            def root(n, b):
                act.wait_ge(s_ms, n * BLKS + b + 1)
                tiles = slice(TB * b, TB * b + TB)
                nc.scalar.activation(ST[:, n, tiles], ms_ps[:, b % 2, tiles], ACT.Sqrt, bias=eps[:, n:n + 1]).then_inc(s_root, 1)

            for b in range(BLKS):
                act.wait_ge(s_dcopy, b + 1)
                nc.scalar.activation(SQ[:, 0, cols(b)], D[:, cols(b)], ACT.Square).then_inc(s_sq, 1)
                if b >= 1:
                    root(0, b - 1)
            root(0, BLKS - 1)
            for b in range(BLKS):
                batch = b * BLK // SEQ
                act.wait_ge(s_xn, b + 1)
                nc.scalar.activation(g.H[:, cols(b)], XN[:, cols(b)], ACT.Identity,
                                     scale=g.mod[:, layer, scale, batch:batch + 1],
                                     bias=g.mod[:, layer, shift, batch:batch + 1]).then_inc(s_h, 1)
                if norms == 2:
                    act.wait_ge(s_h, b + 1)
                    nc.scalar.activation(SQ[:, 1, cols(b)], g.H[:, cols(b)], ACT.Square).then_inc(s_sq, 1)
                    if b >= 1:
                        root(1, b - 1)
            if norms == 2:
                root(1, BLKS - 1)

        @block.vector
        def _(dve):
            nc.vector.memset(eps[:, 0:1], 1e-5).then_inc(s_eps, 1)
            if rms:
                nc.vector.memset(eps[:, 1:2], rms[1]).then_inc(s_eps, 1)

            def inverse(n, b):
                i = n * BLKS + b
                tiles = slice(TB * b, TB * b + TB)
                dve.wait_ge(s_root, i + 1)
                nc.vector.reciprocal(R[:, n, tiles], ST[:, n, tiles]).then_inc(s_inv, 1)
                dve.wait_ge(s_inv, i + 1)
                nc.vector.tensor_tensor(DG[:, n, cols(b)].rearrange("p (t k) -> p t k", t=TB),
                                        g.ident[:, :].unsqueeze(1).broadcast_to([P, TB, P]),
                                        R[:, n, tiles].unsqueeze(2).broadcast_to([P, TB, P]), ALU.mult).then_inc(s_diag, 1)

            for b in range(BLKS):
                dve.wait_ge(s_cent, b + 1)
                nc.vector.tensor_copy(D[:, cols(b)], d_ps[:, b % 2, :]).then_inc(s_dcopy, 1)
                if b >= 1:
                    inverse(0, b - 1)
            inverse(0, BLKS - 1)
            for b in range(BLKS):
                dve.wait_ge(s_r, b + 1)
                dve.wait_ge(s_dcopy, b + 1)
                nc.vector.tensor_tensor(XN[:, cols(b)], D[:, cols(b)], r_ps[:, b % 2, :], ALU.mult).then_inc(s_xn, 1)
                if norms == 2 and b >= 1:
                    inverse(1, b - 1)
            if norms == 2:
                inverse(1, BLKS - 1)
                for b in range(BLKS):
                    dve.wait_ge(s_r, BLKS + b + 1)
                    dve.wait_ge(s_h, b + 1)
                    nc.vector.scalar_tensor_tensor(out=g.U[:, cols(b)], in0=g.H[:, cols(b)], scalar=rms[0],
                                                   in1=r_ps[:, b % 2, :], op0=ALU.mult, op1=ALU.mult).then_inc(s_u, 1)


def stage_attention(nc, d, g):
    with ExitStack() as ctx:
        sb, ps, sem = alloc(nc, ctx)
        wqk = sb("wqk", [P, 2 * PAIRS, 2, P])
        wv = sb("wv", [P, HEADS * DH])
        wo = sb("wo", [P, PAIRS, P])
        cs = sb("cs", [P, ITERS * 2 * ITER])
        pmk = sb("pmk", [P, PAIRS, PM])
        maskb = sb("maskb", [P, QG * KEYS], BF16)
        identb = sb("identb", [P, P], BF16)
        Gb = sb("Gb", [P, 2, ITER])
        T = sb("T", [P, 4, 2 * ITER])
        Q = sb("Q", [P, 2, PAIRS, ITER])
        K = sb("K", [P, 2, PAIRS, SEGS, KEYS])
        V = sb("V", [KEYS, 2, SEGS, HEADS * DH])
        MX = sb("MX", [P, 2, QG])
        SM = sb("SM", [P, 2, QG])
        RC = sb("RC", [P, 2, QG])
        PR = sb("PR", [P, 4, QG, KEYS])
        PT = sb("PT", [KEYS, 2, QG, P])
        OT = sb("OT", [P, 2, PAIRS, ITER])
        s_bank = ps("s_bank", [P, 2, 512])
        pt_bank = ps("pt_bank", [P, 2, QG, P])
        o_bank = ps("o_bank", [P, QG, P])
        qk_bank = ps("qk_bank", [P, 2, 2 * ITER])
        v_bank = ps("v_bank", [P, 512])
        s_w, s_pm, s_g = sem("a_w"), sem("a_pm"), sem("a_g")
        s_qk, s_mul, s_add = sem("a_qk"), sem("a_mul"), sem("a_add")
        s_v, s_vev = sem("a_v"), sem("a_vev")
        s_sc, s_mx, s_sub, s_exp, s_sum, s_rc, s_pr = (sem("a_" + n) for n in ("sc", "mx", "sub", "exp", "sum", "rc", "pr"))
        s_tr, s_ptev, s_av, s_oev, s_y, s_yev = (sem("a_" + n) for n in ("tr", "ptev", "av", "oev", "y", "yev"))
        G16 = 2 * PAIRS
        VH = 2 * SEGS

        def loops(eng, body, first, tail):
            first()
            body(0, 0, "first")
            with eng.Fori(0, (ITERS - 2) // 2) as i:
                body(i * 2 + 1, 1, "mid")
                body(i * 2 + 2, 0, "mid")
            body(ITERS - 1, 1, "last")
            tail()

        def noop():
            pass

        block = ctx.enter_context(nc.Block())

        @block.sync
        def _(sp):
            for dst, src in ((wqk[:, :, :, :], d["wqk"]), (wv[:, :], d["wv"]), (wo[:, :, :], d["wo"]), (cs[:, :], d["cs"]),
                             (pmk[:, :, :], d["pmk"]), (maskb[:, :], d["maskb"]), (identb[:, :], d["identb"])):
                sp.dma_start(dst, src).then_inc(s_w, 16)
            for par in range(2):
                for seg in range(SEGS):
                    sp.dma_start(V[SEG:KEYS, par, seg, :], d["pmv"]).then_inc(s_w, 16)

        LOADS = 16 * (7 + 2 * SEGS)

        @block.tensor
        def _(pe):
            def scores(it, par, u):
                sp_, hh, odd = u // 4, (u // 2) % 2, u % 2
                U = it * UNITS + u
                if not (isinstance(it, int) and U < 2):
                    pe.wait_ge(s_sub, U - 1)
                bank = s_bank[:, u % 2, 0:QG * KEYS]
                nc.tensor.matmul(bank, identb[:, :], maskb[:, :], start=True, stop=False, skip_group_check=True)
                for j in range(QG):
                    for s in range(2):
                        mm = nc.tensor.matmul(
                            s_bank[SEG * s:SEG * (s + 1), u % 2, j * KEYS:(j + 1) * KEYS],
                            Q[DH * odd:DH * (odd + 1), par, QG * hh + j, P * sp_ + SEG * s:P * sp_ + SEG * (s + 1)],
                            K[DH * odd:DH * (odd + 1), par, QG * hh + j, 2 * sp_ + s, :],
                            start=False, stop=True, skip_group_check=True)
                mm.then_inc(s_sc, 1)

            def transposes(U, u):
                pe.wait_ge(s_pr, U + 1)
                if not (isinstance(U, int) and U < 2):
                    pe.wait_ge(s_ptev, U - 1)
                for j in range(QG):
                    mm = nc.tensor.transpose(pt_bank[0:KEYS, u % 2, j, :], PR[:, u % 4, j, :], g.ident[:, :])
                mm.then_inc(s_tr, 1)

            def values(U, u, it, par):
                sp_, hh, odd = u // 4, (u // 2) % 2, u % 2
                pe.wait_ge(s_ptev, U + 1)
                if u % 4 == 0:
                    pe.wait_ge(s_vev, it * VH + 4 * (sp_ + 1))
                if odd == 0 and not (isinstance(U, int) and U == 0):
                    pe.wait_ge(s_oev, it * (UNITS // 2) + u // 2)
                for j in range(QG):
                    head = 2 * (QG * hh + j) + odd
                    for s in range(2):
                        mm = nc.tensor.matmul(o_bank[DH * odd:DH * (odd + 1), j, SEG * s:SEG * (s + 1)],
                                              V[:, par, 2 * sp_ + s, head * DH:(head + 1) * DH],
                                              PT[:, u % 2, j, SEG * s:SEG * (s + 1)], start=True, stop=True)
                mm.then_inc(s_av, 1)

            def project_qk(n, par, i):
                first = isinstance(n, int) and n == 0 and i < 2
                if not first:
                    pe.wait_ge(s_mul, n * G16 + i - 1)
                for swapped in range(2):
                    mm = nc.tensor.matmul(qk_bank[:, i % 2, swapped * ITER:(swapped + 1) * ITER], wqk[:, i, swapped, :], Gb[:, par, :],
                                          start=True, stop=True)
                mm.then_inc(s_qk, 1)

            def project_v(n, par, v):
                if not (isinstance(n, int) and n == 0 and v == 0):
                    pe.wait_ge(s_vev, n * VH + v)
                seg, half = v // 2, v % 2
                nc.tensor.matmul(v_bank[0:SEG, :], Gb[:, par, SEG * seg:SEG * (seg + 1)], wv[:, 512 * half:512 * (half + 1)],
                                 start=True, stop=True).then_inc(s_v, 1)

            def project_out(it, par, vdone):
                pe.wait_ge(s_oev, (it + 1) * (UNITS // 2))
                pe.wait_ge(s_vev, vdone)
                for hp in range(PAIRS):
                    mm = nc.tensor.matmul(v_bank[:, 0:ITER], wo[:, hp, :], OT[:, par, hp, :],
                                          start=(hp == 0), stop=(hp == PAIRS - 1))
                mm.then_inc(s_y, 1)

            def first():
                pe.sem_inc(s_y, 2)
                pe.wait_ge(s_w, LOADS)
                pe.wait_ge(s_g, 1)
                for v in range(VH):
                    for i in (2 * v, 2 * v + 1):
                        project_qk(0, 0, i)
                    project_v(0, 0, v)

            def body(it, par, which):
                if which == "first":
                    pe.wait_ge(s_pm, 2 * SEGS)
                for u in range(UNITS):
                    if u == 0:
                        pe.wait_ge(s_add, (it + 1) * G16)
                    scores(it, par, u)
                    old = not (which == "first" and u < 2)
                    pu, pit, ppar = (u - 2, it, par) if u >= 2 else (u + UNITS - 2, it - 1, 1 - par)
                    if old:
                        transposes(pit * UNITS + pu, pu)
                    if u == 2 and which != "first":
                        project_out(it - 1, 1 - par, (it + 1) * VH + (2 if which != "last" else 0))
                    if which != "last":
                        if u == 0:
                            pe.wait_ge(s_g, it + 2)
                        for i in (2 * u, 2 * u + 1):
                            project_qk(it + 1, 1 - par, i)
                        if u == 2 and which != "first":
                            pe.wait_ge(s_yev, it)
                        project_v(it + 1, 1 - par, u)
                    if old:
                        values(pit * UNITS + pu, pu, pit, ppar)

            def tail():
                it = ITERS - 1
                for u in (UNITS - 2, UNITS - 1):
                    transposes(it * UNITS + u, u)
                for u in (UNITS - 2, UNITS - 1):
                    values(it * UNITS + u, u, it, 1)
                pe.wait_ge(s_yev, it)
                project_out(it, 1, ITERS * VH)

            loops(pe, body, first, tail)

        @block.vector
        def _(dve):
            def load_block(n, par):
                if not (isinstance(n, int) and n < 2):
                    dve.wait_ge(s_v, (n - 1) * VH)
                nc.vector.tensor_copy(Gb[:, par, :], g.U[:, bass.ds(n * ITER, ITER)]).then_inc(s_g, 1)

            def rope(n, i):
                dve.wait_ge(s_qk, n * G16 + i + 1)
                if not (isinstance(n, int) and n == 0 and i < 4):
                    dve.wait_ge(s_add, n * G16 + i - 3)
                nc.vector.tensor_tensor(T[:, i % 4, :], qk_bank[:, i % 2, :],
                                        cs[:, bass.ds(n * (2 * ITER), 2 * ITER)], ALU.mult).then_inc(s_mul, 1)

            def softmax_a(it, u):
                U = it * UNITS + u
                S = s_bank[:, u % 2, 0:QG * KEYS].rearrange("p (j k) -> p j k", j=QG)
                dve.wait_ge(s_sc, U + 1)
                nc.vector.tensor_reduce(MX[:, u % 2, :], S, AX.X, ALU.max).then_inc(s_mx, 1)
                dve.wait_ge(s_mx, U + 1)
                if not (isinstance(it, int) and U < 4):
                    dve.wait_ge(s_tr, U - 3)
                nc.vector.tensor_tensor(PR[:, u % 4, :, :], S, MX[:, u % 2, :].unsqueeze(2).broadcast_to([P, QG, KEYS]),
                                        ALU.subtract).then_inc(s_sub, 1)

            def softmax_b(it, u):
                U = it * UNITS + u
                dve.wait_ge(s_exp, U + 1)
                nc.vector.tensor_reduce(SM[:, u % 2, :], PR[:, u % 4, :, :], AX.X, ALU.add).then_inc(s_sum, 1)
                dve.wait_ge(s_sum, U + 1)
                if not (isinstance(it, int) and U < 2):
                    dve.wait_ge(s_pr, U - 1)
                nc.vector.reciprocal(RC[:, u % 2, :], SM[:, u % 2, :]).then_inc(s_rc, 1)

            def first():
                load_block(0, 0)
                dve.wait_ge(s_w, LOADS)
                for par in range(2):
                    for seg in range(SEGS):
                        nc.vector.tensor_copy(K[:, par, :, seg, SEG:KEYS], pmk[:, :, :]).then_inc(s_pm, 1)
                for i in range(G16):
                    rope(0, i)

            def body(it, par, which):
                if which != "last":
                    load_block(it + 1, 1 - par)
                for u in range(UNITS):
                    softmax_a(it, u)
                    if which != "last":
                        rope(it + 1, 2 * u)
                    softmax_b(it, u)
                    if which != "last":
                        rope(it + 1, 2 * u + 1)
            loops(dve, body, first, noop)

        @block.gpsimd
        def _(pool):
            def add(n, par, i):
                pool.wait_ge(s_mul, n * G16 + i + 1)
                hp = i % PAIRS
                if i == 0 and not (isinstance(n, int) and n < 2):
                    pool.wait_ge(s_sc, (n - 1) * UNITS)
                a, b = T[:, i % 4, 0:ITER], T[:, i % 4, ITER:2 * ITER]
                if i < PAIRS:
                    nc.gpsimd.tensor_tensor(Q[:, par, hp, :], a, b, ALU.add).then_inc(s_add, 1)
                else:
                    nc.gpsimd.tensor_tensor(K[:, par, hp, :, 0:SEG], a.rearrange("p (s k) -> p s k", s=SEGS),
                                            b.rearrange("p (s k) -> p s k", s=SEGS), ALU.add).then_inc(s_add, 1)

            def normalise(it, u):
                pool.wait_ge(s_rc, it * UNITS + u + 1)
                nc.gpsimd.tensor_tensor(PR[:, u % 4, :, :], PR[:, u % 4, :, :],
                                        RC[:, u % 2, :].unsqueeze(2).broadcast_to([P, QG, KEYS]), ALU.mult).then_inc(s_pr, 1)

            def first():
                for i in range(G16):
                    add(0, 0, i)

            def body(it, par, which):
                for u in range(UNITS):
                    if which != "last":
                        add(it + 1, 1 - par, 2 * u)
                    normalise(it, u)
                    if which != "last":
                        add(it + 1, 1 - par, 2 * u + 1)

            loops(pool, body, first, noop)

        @block.scalar
        def _(act):
            nc.scalar.preload_act_table(ACT.Exp)

            def exponent(it, u):
                act.wait_ge(s_sub, it * UNITS + u + 1)
                nc.scalar.activation(PR[:, u % 4, :, :], PR[:, u % 4, :, :], ACT.Exp, scale=DH ** -0.5).then_inc(s_exp, 1)

            def take_pt(U, u):
                act.wait_ge(s_tr, U + 1)
                if not (isinstance(U, int) and U < 2):
                    act.wait_ge(s_av, U - 1)
                nc.scalar.activation(PT[:, u % 2, :, :], pt_bank[0:KEYS, u % 2, :, :], ACT.Copy).then_inc(s_ptev, 1)

            def take_v(n, par, v):
                act.wait_ge(s_v, n * VH + v + 1)
                if not (isinstance(n, int) and n < 2):
                    act.wait_ge(s_av, (n - 2) * UNITS + (UNITS // 2 if v < VH // 2 else UNITS))
                nc.scalar.activation(V[0:SEG, par, v // 2, 512 * (v % 2):512 * (v % 2 + 1)], v_bank[0:SEG, :],
                                     ACT.Copy).then_inc(s_vev, 1)

            def take_o(U, u, it, par):
                act.wait_ge(s_av, U + 1)
                act.wait_ge(s_y, it + 1)
                sp_, hh = u // 4, (u // 2) % 2
                nc.scalar.activation(OT[:, par, QG * hh:QG * (hh + 1), P * sp_:P * (sp_ + 1)], o_bank[:, :, :],
                                     ACT.Copy).then_inc(s_oev, 1)

            def take_y(it):
                act.wait_ge(s_y, it + 3)
                nc.scalar.activation(g.Y[:, bass.ds(it * ITER, ITER)], v_bank[:, 0:ITER], ACT.Copy).then_inc(s_yev, 1)

            def first():
                for v in range(VH):
                    take_v(0, 0, v)

            def body(it, par, which):
                for u in range(UNITS):
                    old = not (which == "first" and u < 2)
                    pu, pit, ppar = (u - 2, it, par) if u >= 2 else (u + UNITS - 2, it - 1, 1 - par)
                    if old:
                        take_pt(pit * UNITS + pu, pu)
                    exponent(it, u)
                    if u == 2 and which != "first":
                        take_y(it - 1)
                    if which != "last":
                        take_v(it + 1, 1 - par, u)
                    if old and pu % 2:
                        take_o(pit * UNITS + pu, pu, pit, ppar)

            def tail():
                it = ITERS - 1
                for u in (UNITS - 2, UNITS - 1):
                    take_pt(it * UNITS + u, u)
                take_o(it * UNITS + UNITS - 1, UNITS - 1, it, 1)
                take_y(it)

            loops(act, body, first, tail)


def stage_route(nc, d, g):
    with ExitStack() as ctx:
        sb, ps, sem = alloc(nc, ctx)
        gate = sb("gate", [P, EXPERTS])
        gbias = sb("gbias", [P, EXPERTS])
        identb = sb("ridentb", [P, P], BF16)
        shape = [P, TILES, EXPERTS]
        SC, SF, EQ, LOW = sb("SC", shape), sb("SF", shape), sb("EQ", shape), sb("LOW", shape)
        M1, CNT, M2 = (sb(n, [P, TILES, GROUPS]) for n in ("M1", "CNT", "M2"))
        GA, GR = sb("GA", [P, TILES, GROUPS + 8 - TOPG]), sb("GR", [P, TILES, GROUPS + 8 - TOPG])
        T8 = sb("T8", [P, TILES, 8])
        GM = sb("GM", [P, TILES, GROUPS])
        WS, WR = sb("WS", [P, TILES]), sb("WR", [P, TILES])
        SP = sb("SP", [P, TILES, 2, P], BF16)
        lg = ps("lg", [P, 2, TILES // 2, EXPERTS])
        rt = ps("rt", [P, 2, 2, 4, P], BF16)
        s_w, s_lg, s_sig, s_v, s_tr, s_ev = (sem("r_" + n) for n in ("w", "lg", "sig", "v", "tr", "ev"))
        block = ctx.enter_context(nc.Block())

        @block.sync
        def _(sp):
            sp.dma_start(gate[:, :], d["gateT"]).then_inc(s_w, 16)
            sp.dma_start(gbias[:, :], d["gbias"]).then_inc(s_w, 16)
            sp.dma_start(identb[:, :], d["identb"]).then_inc(s_w, 16)

        @block.tensor
        def _(pe):
            pe.wait_ge(s_w, 48)
            for t in range(TILES):
                mm = nc.tensor.matmul(lg[:, t // 8, t % 8, :], g.H[:, t * P:(t + 1) * P], gate[:, :], start=True, stop=True)
                if t % 8 == 7:
                    mm.then_inc(s_lg, 1)
            pe.wait_ge(s_v, ROUTE_STEPS)
            for q in range(TILES // 4):
                if q >= 2:
                    pe.wait_ge(s_ev, 2 * (q - 1))
                for part in range(2):
                    for t in range(4):
                        mm = nc.tensor.transpose(rt[:, q % 2, part, t, :], SP[:, 4 * q + t, part, :], identb[:, :])
                mm.then_inc(s_tr, 1)

        @block.scalar
        def _(act):
            nc.scalar.preload_act_table(ACT.Sigmoid)
            for h in range(2):
                act.wait_ge(s_lg, h + 1)
                nc.scalar.activation(SC[:, 8 * h:8 * h + 8, :], lg[:, h, :, :], ACT.Sigmoid).then_inc(s_sig, 1)
            for q in range(TILES // 4):
                act.wait_ge(s_tr, q + 1)
                for part in range(2):
                    nc.scalar.activation(g.RT[:, part, q * BLK:(q + 1) * BLK].rearrange("p (t k) -> p t k", t=4),
                                         rt[:, q % 2, part, :, :], ACT.Copy).then_inc(s_ev, 1)

        @block.vector
        def _(dve):
            n = 0

            def step(ins, wait=True):
                nonlocal n
                ins.then_inc(s_v, 1)
                n += 1
                if wait:
                    dve.wait_ge(s_v, n)

            def grouped(t):
                return t[:, :, :].rearrange("p t (a b) -> p (t a) b", b=GSIZE)

            def per_group(t):
                return t[:, :, :].rearrange("p t a -> p (t a)")

            def over_group(t):
                return per_group(t).unsqueeze(2).broadcast_to([P, TILES * GROUPS, GSIZE])

            for k in range(8 - TOPG):
                step(nc.vector.memset(GA[:, :, GROUPS + k:GROUPS + k + 1], BIG * (k + 1)), wait=False)
            step(nc.vector.memset(SP[:, :, 1, EXPERTS:P], 0.0))
            step(nc.vector.memset(SP[:, :, 1, EXPERTS:EXPERTS + 1], 1.0))
            dve.wait_ge(s_w, 48)
            dve.wait_ge(s_sig, 2)
            step(nc.vector.tensor_tensor(SF[:, :, :], SC[:, :, :], gbias[:, :].unsqueeze(1).broadcast_to(shape), ALU.add))
            step(nc.vector.tensor_reduce(per_group(M1), grouped(SF), AX.X, ALU.max))
            step(nc.vector.tensor_tensor(grouped(EQ), grouped(SF), over_group(M1), ALU.is_equal))
            step(nc.vector.tensor_reduce(per_group(CNT), grouped(EQ), AX.X, ALU.add))
            step(nc.vector.scalar_tensor_tensor(out=LOW[:, :, :], in0=EQ[:, :, :], scalar=-BIG, in1=SF[:, :, :],
                                                op0=ALU.mult, op1=ALU.add))
            step(nc.vector.tensor_reduce(per_group(M2), grouped(LOW), AX.X, ALU.max))
            step(nc.vector.tensor_scalar(CNT[:, :, :], CNT[:, :, :], 2.0, -BIG, ALU.is_lt, ALU.mult))
            step(nc.vector.tensor_tensor(CNT[:, :, :], CNT[:, :, :], M1[:, :, :], ALU.add))
            step(nc.vector.tensor_tensor(M2[:, :, :], M2[:, :, :], CNT[:, :, :], ALU.max))
            step(nc.vector.tensor_tensor(GA[:, :, 0:GROUPS], M1[:, :, :], M2[:, :, :], ALU.add))
            for t in range(TILES):
                step(nc.vector.max(T8[:, t, :], GA[:, t, :]), wait=(t == TILES - 1))
            for t in range(TILES):
                step(nc.vector.match_replace(GR[:, t, :], T8[:, t, :], GA[:, t, :], -4 * BIG), wait=(t == TILES - 1))
            step(nc.vector.tensor_scalar(GM[:, :, :], GR[:, :, 0:GROUPS], -4 * BIG, None, ALU.is_equal))
            step(nc.vector.tensor_tensor(grouped(LOW), grouped(SF), over_group(GM), ALU.mult))
            step(nc.vector.tensor_scalar(LOW[:, :, :], LOW[:, :, :], 0.0, None, ALU.add))
            for t in range(TILES):
                step(nc.vector.max(T8[:, t, :], LOW[:, t, :]), wait=(t == TILES - 1))
            for t in range(TILES):
                step(nc.vector.match_replace(EQ[:, t, :], T8[:, t, :], LOW[:, t, :], -4 * BIG), wait=(t == TILES - 1))
            step(nc.vector.scalar_tensor_tensor(out=SF[:, :, :], in0=EQ[:, :, :], scalar=-4 * BIG, in1=SC[:, :, :],
                                                op0=ALU.is_equal, op1=ALU.mult))
            step(nc.vector.tensor_reduce(WS[:, :], SF[:, :, :], AX.X, ALU.add))
            step(nc.vector.tensor_scalar(WS[:, :], WS[:, :], 1e-20, None, ALU.add))
            step(nc.vector.reciprocal(WR[:, :], WS[:, :]))
            step(nc.vector.tensor_scalar(WR[:, :], WR[:, :], 2.5, None, ALU.mult))
            step(nc.vector.tensor_tensor(SF[:, :, :], SF[:, :, :], WR[:, :].unsqueeze(2).broadcast_to(shape), ALU.mult))
            step(nc.vector.tensor_copy(SP[:, :, 0, 0:EXPERTS], SF[:, :, :]))
            step(nc.vector.tensor_tensor(SF[:, :, :], SF[:, :, :], SP[:, :, 0, 0:EXPERTS], ALU.subtract))
            step(nc.vector.tensor_copy(SP[:, :, 0, EXPERTS:P], SF[:, :, :]))
            step(nc.vector.tensor_tensor(SF[:, :, :], SF[:, :, :], SP[:, :, 0, EXPERTS:P], ALU.subtract))
            step(nc.vector.tensor_copy(SP[:, :, 1, 0:EXPERTS], SF[:, :, :]))
            assert n == ROUTE_STEPS, n


ROUTE_STEPS = 94


def stage_experts(nc, d, g):
    RING, TBS = 4, 2
    LOOPS, REST = CHUNKS // RING, CHUNKS % RING
    with ExitStack() as ctx:
        sb, ps, sem = alloc(nc, ctx)
        W = sb("W", [P, RING, 3, P])
        SEL = sb("SEL", [P, RING, 2, P], BF16)
        zero = sb("zero", [P, P], BF16)
        SG, TT, HH = (sb(n, [P, 2, BLK]) for n in ("SG", "TT", "HH"))
        g_ps, u_ps, rb_ps, acc = (ps(n, [P, 2, BLK]) for n in ("g_ps", "u_ps", "rb_ps", "acc"))
        s_ld = [sem(f"e_ld{k}") for k in range(RING)]
        s_z, s_g, s_u, s_rb, s_silu, s_t, s_hh, s_down, s_out = (
            sem("e_" + n) for n in ("z", "g", "u", "rb", "silu", "t", "hh", "down", "out"))

        def runs(eng, body, end):
            for half in range(2):
                n0 = half * CHUNKS

                def one(i, k):
                    body(half, i * RING + (n0 + k), (n0 + k) % RING, i + (n0 + k) // RING, isinstance(i, int) and i + k == 0)
                for k in range(RING):
                    one(0, k)
                with eng.Fori(1, LOOPS) as i:
                    for k in range(RING):
                        one(i, k)
                for k in range(REST):
                    one(LOOPS, k)
                end(half)

        def cols(half, tb):
            return slice((half * TBS + tb) * BLK, (half * TBS + tb + 1) * BLK)

        def early(U):
            return isinstance(U, int) and U < 2

        block = ctx.enter_context(nc.Block())

        @block.sync
        def _(sp):
            def body(half, n, slot, uses, first):
                if not (isinstance(n, int) and n < RING):
                    sp.wait_ge(s_down, (n - (RING - 1)) * TBS)
                chunk = n - half * CHUNKS
                sp.dma_start(W[:, slot, :, :].rearrange("p a b -> p (a b)"),
                             d["w3"][bass.ds(chunk, 1), :, :].rearrange("o p n -> (o p) n")).then_inc(s_ld[slot], 16)
                sp.dma_start(SEL[:, slot, :, :].rearrange("p a b -> p (a b)"),
                             d["sel"][bass.ds(chunk, 1), :, :].rearrange("o p n -> (o p) n")).then_inc(s_ld[slot], 16)
            runs(sp, body, lambda half: None)

        @block.tensor
        def _(pe):
            def down(U, slot, tb):
                pe.wait_ge(s_hh, U + 1)
                nc.tensor.matmul(acc[:, tb, :], W[:, slot, 2, :], HH[:, tb, :], start=False, stop=False,
                                 skip_group_check=True).then_inc(s_down, 1)

            def open_sums(half):
                if half == 0:
                    pe.wait_ge(s_z, 1)
                else:
                    pe.wait_ge(s_out, TBS)
                for tb in range(TBS):
                    nc.tensor.matmul(acc[:, tb, :], zero[:, :], g.RT[:, 0, 0:BLK], start=True, stop=False,
                                     skip_group_check=True)

            def body(half, n, slot, uses, first):
                for tb in range(TBS):
                    U = n * TBS + tb
                    if tb == 0:
                        pe.wait_ge(s_ld[slot], (uses + 1) * 32)
                    if not early(U):
                        pe.wait_ge(s_silu, U - 1)
                    nc.tensor.matmul(g_ps[:, tb, :], W[:, slot, 0, :], g.H[:, cols(half, tb)], start=True, stop=True).then_inc(s_g, 1)
                    if not early(U):
                        pe.wait_ge(s_t, U - 1)
                    nc.tensor.matmul(u_ps[:, tb, :], W[:, slot, 1, :], g.H[:, cols(half, tb)], start=True, stop=True).then_inc(s_u, 1)
                    if not early(U):
                        pe.wait_ge(s_hh, U - 1)
                    for part in range(2):
                        mm = nc.tensor.matmul(rb_ps[:, tb, :], SEL[:, slot, part, :], g.RT[:, part, cols(half, tb)],
                                              start=(part == 0), stop=(part == 1))
                    mm.then_inc(s_rb, 1)
                    if first and tb == 0:
                        open_sums(half)
                    else:
                        down(U - 1, slot if tb else (slot - 1) % RING, 1 - tb)

            def end(half):
                down((half + 1) * CHUNKS * TBS - 1, ((half + 1) * CHUNKS - 1) % RING, 1)

            runs(pe, body, end)

        @block.scalar
        def _(act):
            nc.scalar.preload_act_table(ACT.Silu)

            def body(half, n, slot, uses, first):
                for tb in range(TBS):
                    U = n * TBS + tb
                    act.wait_ge(s_g, U + 1)
                    if not early(U):
                        act.wait_ge(s_t, U - 1)
                    nc.scalar.activation(SG[:, tb, :], g_ps[:, tb, :], ACT.Silu).then_inc(s_silu, 1)

            def end(half):
                act.wait_ge(s_down, (half + 1) * CHUNKS * TBS)
                for tb in range(TBS):
                    nc.scalar.activation(g.Y[:, cols(half, tb)], acc[:, tb, :], ACT.Copy).then_inc(s_out, 1)

            runs(act, body, end)

        @block.vector
        def _(dve):
            nc.vector.memset(zero[:, :], 0.0).then_inc(s_z, 1)

            def body(half, n, slot, uses, first):
                for tb in range(TBS):
                    U = n * TBS + tb
                    dve.wait_ge(s_silu, U + 1)
                    dve.wait_ge(s_u, U + 1)
                    nc.vector.tensor_tensor(TT[:, tb, :], SG[:, tb, :], u_ps[:, tb, :], ALU.mult).then_inc(s_t, 1)
                    dve.wait_ge(s_t, U + 1)
                    dve.wait_ge(s_rb, U + 1)
                    if not early(U):
                        dve.wait_ge(s_down, U - 1)
                    nc.vector.tensor_tensor(HH[:, tb, :], TT[:, tb, :], rb_ps[:, tb, :], ALU.mult).then_inc(s_hh, 1)

            runs(dve, body, lambda half: None)


def stage_moe(nc, d, g):
    with ExitStack() as ctx:
        sb, _, _ = alloc(nc, ctx)
        g.RT = sb("RT", [P, 2, TOK], BF16)
        stage_route(nc, d, g)
        stage_experts(nc, d, g)


W2 = SEQ + CONVPAD
DIRS = 2


def stage_mamba_project(nc, d, g, m):
    with ExitStack() as ctx:
        sb, ps, sem = alloc(nc, ctx)
        U2 = sb("U2", [P, DIRS, BATCH, W2])
        wx = sb("wx", [P, DIRS, 3 * P])
        cw = sb("cw", [P, DIRS, 2, 3 * P])
        wc = sb("wc", [P, DIRS, 2, 3 * P])
        wz = sb("wz", [P, DIRS, P])
        wdt = sb("wdt", [P, 4])
        cb = sb("cb", [P, DIRS, 3])
        dtb, al = sb("dtb", [P, 4]), sb("al", [P, 4])
        A = sb("A", [P, 4])
        shape = [P, TILES, 4]
        VV, NV, E, W1, DD, IZ, LN = (sb(n, shape) for n in ("VV", "NV", "E", "W1", "DD", "IZ", "LN"))
        job_ps = ps("job_ps", [P, 4, BLK])
        dt_ps = ps("dt_ps", shape)
        sum_ps = ps("sum_ps", [P, 3, 4, TILES])
        s_w, s_u2, s_pad, s_wc, s_dt, s_v, s_act, s_job, s_ev, s_sum = (
            sem("p_" + n) for n in ("w", "u2", "pad", "wc", "dt", "v", "act", "job", "ev", "sum"))
        JOBS = 4 * DIRS
        SHIFT = (3, 0)
        FAR = (-2, 2)
        block = ctx.enter_context(nc.Block())

        def blocks(eng, body):
            with eng.Fori(0, BATCH) as b:
                with eng.Fori(0, SEQ // BLK) as h:
                    for j in range(JOBS):
                        body(b, h, j, (b * (SEQ // BLK) + h) * JOBS + j)

        @block.sync
        def _(sp):
            for dst, src in ((wx[:, :, :], d["wxbc"]), (cw[:, :, :, :], d["cw"]), (wz[:, :, :], d["wz"]), (wdt[:, :], d["wdt"]),
                             (cb[:, :, :], d["cb"]), (dtb[:, :], d["dtb"]), (al[:, :], d["alog"]), (m.tri[:, :, :], d["tri"])):
                sp.dma_start(dst, src).then_inc(s_w, 16)
            for b in range(BATCH):
                t0 = b * SEQ
                for dst, src in ((U2[0:HD, 0, b, 3:3 + SEQ], g.U[0:HD, t0:t0 + SEQ]),
                                 (U2[HD:P, 0, b, 4:3 + SEQ], g.U[0:HD, t0:t0 + SEQ - 1]),
                                 (U2[0:HD, 1, b, 0:SEQ], g.U[HD:P, t0:t0 + SEQ]),
                                 (U2[HD:P, 1, b, 0:SEQ - 1], g.U[HD:P, t0 + 1:t0 + SEQ])):
                    sp.dma_start(dst, src).then_inc(s_u2, 16)

        @block.gpsimd
        def _(pool):
            nc.gpsimd.memset(U2[0:HD, 0, :, 0:3], 0.0).then_inc(s_pad, 1)
            nc.gpsimd.memset(U2[HD:P, 0, :, 0:4], 0.0).then_inc(s_pad, 1)
            nc.gpsimd.memset(U2[0:HD, 1, :, SEQ:W2], 0.0).then_inc(s_pad, 1)
            nc.gpsimd.memset(U2[HD:P, 1, :, SEQ - 1:W2], 0.0).then_inc(s_pad, 1)

        @block.tensor
        def _(pe):
            pe.wait_ge(s_w, 128)
            for t in range(TILES):
                mm = nc.tensor.matmul(dt_ps[:, t, :], g.U[:, t * P:(t + 1) * P], wdt[:, :], start=True, stop=True)
            mm.then_inc(s_dt, 1)
            pe.wait_ge(s_pad, 4)
            pe.wait_ge(s_u2, 128)
            pe.wait_ge(s_wc, 1)

            def job(b, h, j, J):
                dr, c = j // 4, j % 4
                pe.wait_ge(s_ev, J + 1)
                base = dr * BATCH * W2 + SHIFT[dr]
                flat = U2[:, :, :, :].rearrange("p a b c -> p (a b c)")
                if c < 3:
                    for q in range(2):
                        mm = nc.tensor.matmul(job_ps[:, j % 4, :], wc[:, dr, q, c * P:(c + 1) * P],
                                              flat[:, bass.ds(b * W2 + h * BLK + (base + q * FAR[dr]), BLK)],
                                              start=(q == 0), stop=(q == 1))
                else:
                    mm = nc.tensor.matmul(job_ps[:, j % 4, :], wz[:, dr, :],
                                          flat[:, bass.ds(b * W2 + h * BLK + base, BLK)], start=True, stop=True)
                mm.then_inc(s_job, 1)

            blocks(pe, job)
            pe.wait_ge(s_v, PROJECT_STEPS)
            for k in range(2):
                for dr in range(DIRS):
                    nc.tensor.matmul(sum_ps[:, k, 2 * dr:2 * dr + 2, :], m.tri[:, 2 * dr + k, :],
                                     m.AA[:, :, 2 * dr:2 * dr + 2].rearrange("p t h -> p h t"), start=True, stop=True)
            nc.tensor.matmul(sum_ps[:, 2, :, :], g.ones[:, :], m.AA[:, :, :].rearrange("p t h -> p h t"),
                             start=True, stop=True).then_inc(s_sum, 1)

        @block.scalar
        def _(act):
            act.sem_inc(s_ev, 4)
            act.wait_ge(s_w, 128)
            nc.scalar.activation(A[:, :], al[:, :], ACT.Exp).then_inc(s_act, 1)
            act.wait_ge(s_v, 3)
            nc.scalar.activation(E[:, :, :], NV[:, :, :], ACT.Exp).then_inc(s_act, 1)
            act.wait_ge(s_v, 4)
            nc.scalar.activation(LN[:, :, :], W1[:, :, :], ACT.Ln).then_inc(s_act, 1)
            nc.scalar.preload_act_table(ACT.Silu)

            def job(b, h, j, J):
                dr, c = j // 4, j % 4
                act.wait_ge(s_job, J + 1)
                at = bass.ds(b * SEQ + h * BLK, BLK)
                if c < 3:
                    nc.scalar.activation(m.XBC[:, dr, c, at], job_ps[:, j % 4, :], ACT.Silu, bias=cb[:, dr, c:c + 1]).then_inc(s_ev, 1)
                else:
                    nc.scalar.activation(m.SZ[:, dr, at], job_ps[:, j % 4, :], ACT.Silu).then_inc(s_ev, 1)

            blocks(act, job)
            act.wait_ge(s_sum, 1)
            nc.scalar.activation(m.EX[:, :, :, :], sum_ps[:, :, :, :], ACT.Exp).then_inc(s_act, 1)

        @block.vector
        def _(dve):
            n = 0

            def step(ins):
                nonlocal n
                ins.then_inc(s_v, 1)
                n += 1
                dve.wait_ge(s_v, n)

            dve.wait_ge(s_w, 128)
            for dr in range(DIRS):
                mm = nc.vector.tensor_tensor(wc[:, dr, :, :], cw[:, dr, :, :],
                                             wx[:, dr, :].unsqueeze(1).broadcast_to([P, 2, 3 * P]), ALU.mult)
            mm.then_inc(s_wc, 1)
            dve.wait_ge(s_dt, 1)
            step(nc.vector.tensor_tensor(VV[:, :, :], dt_ps[:, :, :], dtb[:, :].unsqueeze(1).broadcast_to(shape), ALU.add))
            step(nc.vector.tensor_scalar(NV[:, :, :], VV[:, :, :], -1.0, None, ALU.mult))
            step(nc.vector.tensor_tensor(NV[:, :, :], NV[:, :, :], VV[:, :, :], ALU.min))
            dve.wait_ge(s_act, 2)
            step(nc.vector.tensor_scalar(W1[:, :, :], E[:, :, :], 1.0, None, ALU.add))
            step(nc.vector.tensor_scalar(DD[:, :, :], W1[:, :, :], -1.0, None, ALU.add))
            step(nc.vector.tensor_scalar(IZ[:, :, :], DD[:, :, :], 0.0, None, ALU.is_equal))
            step(nc.vector.tensor_tensor(DD[:, :, :], DD[:, :, :], IZ[:, :, :], ALU.add))
            step(nc.vector.reciprocal(DD[:, :, :], DD[:, :, :]))
            dve.wait_ge(s_act, 3)
            step(nc.vector.tensor_tensor(LN[:, :, :], LN[:, :, :], IZ[:, :, :], ALU.add))
            step(nc.vector.tensor_tensor(LN[:, :, :], LN[:, :, :], E[:, :, :], ALU.mult))
            step(nc.vector.tensor_tensor(LN[:, :, :], LN[:, :, :], DD[:, :, :], ALU.mult))
            step(nc.vector.scalar_tensor_tensor(out=m.DT[:, :, :], in0=VV[:, :, :], scalar=0.0, in1=LN[:, :, :],
                                                op0=ALU.max, op1=ALU.add))
            step(nc.vector.scalar_tensor_tensor(out=m.AA[:, :, :], in0=m.DT[:, :, :], scalar=-1.0,
                                                in1=A[:, :].unsqueeze(1).broadcast_to(shape), op0=ALU.mult, op1=ALU.mult))
            assert n == PROJECT_STEPS


PROJECT_STEPS = 13


def stage_mamba_scan(nc, g, m):
    SEQS, STEPS = DIRS * BATCH, SEQ // P
    with ExitStack() as ctx:
        sb, ps, sem = alloc(nc, ctx)
        CP = sb("CP", [P, 2, 3, P])
        AR = sb("AR", [P, 2, 2, P])
        ED = sb("ED", [P, 2, 2, P])
        BT = sb("BT", [P, 2, P])
        GM = sb("GMt", [P, 2, P])
        MT = sb("MT", [P, 2, 2, P])
        DX, DS = sb("DX", [P, 2, 2, HD]), sb("DS", [P, 2, 2, HD])
        YT = sb("YT", [P, 2, 2, HD])
        HST, HD1 = sb("HST", [P, SEQS, 2, HD]), sb("HD1", [P, 2, 2, HD])
        t_ps = ps("t_ps", [P, 2, 4, P])
        d_ps = ps("dd_ps", [P, 2, 4, P])
        y_ps = ps("y_ps", [P, 2, 4, P])
        yt_ps = ps("yt_ps", [P, 2, 4, P])
        (s_z, s_cp, s_ar, s_t, s_d, s_ed, s_bt, s_gm, s_dx, s_ds, s_mt, s_y, s_y1, s_y2, s_h1, s_h2, s_yt, s_yev) = (
            sem("s_" + n) for n in ("z", "cp", "ar", "t", "d", "ed", "bt", "gm", "dx", "ds", "mt", "y", "y1", "y2", "h1",
                                    "h2", "yt", "yev"))
        block = ctx.enter_context(nc.Block())

        def early(U, n=2):
            return isinstance(U, int) and U < n

        def tile(i, q):
            dr, b = q // BATCH, q % BATCH
            return i + b * STEPS if dr == 0 else i * -1 + (b * STEPS + STEPS - 1)

        def at(i, q, n=P):
            return bass.ds(tile(i, q) * n, n)

        def units(eng, body, tail):
            def step(i):
                for q in range(SEQS):
                    body(i, q, i * SEQS + q)
            step(0)
            with eng.Fori(1, STEPS) as i:
                step(i)
            tail()

        def back(i, q, n):
            return (i, q - n) if q >= n else (i - 1, q - n + SEQS)

        def heads(i, q, kind):
            dr = q // BATCH
            return m.EX[:, kind, 2 * dr:2 * dr + 2, bass.ds(tile(i, q), 1)].broadcast_to([P, 2, HD])

        LAST = (STEPS - 1, SEQS - 1)

        @block.scalar
        def _(act):
            nc.scalar.preload_act_table(ACT.Exp)

            def body(i, q, U):
                dr = q // BATCH
                if not early(U):
                    act.wait_ge(s_y, U - 1)
                nc.scalar.activation(CP[:, q % 2, :, :], m.XBC[:, dr, :, at(i, q)], ACT.Copy).then_inc(s_cp, 1)
                act.wait_ge(s_d, U + 1)
                if not early(U):
                    act.wait_ge(s_mt, U - 1)
                nc.scalar.activation(ED[:, q % 2, :, :], d_ps[:, q % 2, 0:2, :], ACT.Exp).then_inc(s_ed, 1)
                nc.scalar.activation(BT[:, q % 2, :], d_ps[:, q % 2, 2, :], ACT.Copy).then_inc(s_bt, 1)
                if not early(U):
                    take_y(*back(i, q, 2), U - 2)

            def take_y(i, q, U):
                act.wait_ge(s_yt, U + 1)
                nc.scalar.activation(m.YB[:, q // BATCH, at(i, q)], yt_ps[:, q % 2, 0, :], ACT.Copy).then_inc(s_yev, 1)

            def tail():
                for n in (1, 0):
                    i, q = back(*LAST, n)
                    take_y(i, q, i * SEQS + q)

            units(act, body, tail)

        @block.gpsimd
        def _(pool):
            def body(i, q, U):
                dr = q // BATCH
                if not early(U):
                    pool.wait_ge(s_d, U - 1)
                shape = [P, 2, P]
                nc.gpsimd.tensor_tensor(AR[:, q % 2, :, :], m.tri[:, 2 * dr, :].unsqueeze(1).broadcast_to(shape),
                                        m.AA[:, bass.ds(tile(i, q), 1), 2 * dr:2 * dr + 2].rearrange("p o h -> p h o")
                                        .broadcast_to(shape), ALU.mult).then_inc(s_ar, 1)
            units(pool, body, lambda: None)

        @block.tensor
        def _(pe):
            def phase1(i, q, U):
                dr, k = q // BATCH, q % 2
                pe.wait_ge(s_cp, U + 1)
                if not early(U):
                    pe.wait_ge(s_dx, U - 1)
                nc.tensor.transpose(t_ps[:, k, 0, :], CP[:, k, 0, :], g.ident[:, :])
                nc.tensor.matmul(t_ps[:, k, 1, :], CP[:, k, 1, :], CP[:, k, 2, :], start=True, stop=True).then_inc(s_t, 1)
                pe.wait_ge(s_ar, U + 1)
                if not early(U):
                    pe.wait_ge(s_bt, U - 1)
                nc.tensor.matmul(d_ps[:, k, 0:2, :], m.tri[:, 2 * dr + 1, :], AR[:, k, :, :], start=True, stop=True)
                nc.tensor.transpose(d_ps[:, k, 2, :], CP[:, k, 1, :], g.ident[:, :]).then_inc(s_d, 1)

            def phase2(i, q, U):
                k = q % 2
                pe.wait_ge(s_mt, U + 1)
                pe.wait_ge(s_ds, U + 1)
                pe.wait_ge(s_bt, U + 1)
                if early(U, SEQS):
                    pe.wait_ge(s_z, 1)
                if not early(U):
                    pe.wait_ge(s_h2, U - 1)
                for h in range(2):
                    nc.tensor.matmul(y_ps[:, k, 0, h * HD:(h + 1) * HD], MT[:, k, h, :], DX[:, k, h, :], start=True, stop=True)
                nc.tensor.matmul(y_ps[:, k, 1, :], CP[:, k, 2, :], HST[:, q, :, :], start=True, stop=True)
                nc.tensor.matmul(y_ps[:, k, 2, :], BT[:, k, :], DS[:, k, :, :], start=True, stop=True).then_inc(s_y, 1)

            def turn(i, q, U):
                k = q % 2
                pe.wait_ge(s_y2, U + 1)
                if not early(U):
                    pe.wait_ge(s_yev, U - 1)
                nc.tensor.transpose(yt_ps[:, k, 0, :], YT[:, k, :, :], g.ident[:, :]).then_inc(s_yt, 1)

            def body(i, q, U):
                phase1(i, q, U)
                if not early(U, 1):
                    phase2(*back(i, q, 1), U - 1)
                if not early(U):
                    turn(*back(i, q, 2), U - 2)

            def tail():
                i, q = LAST
                U = i * SEQS + q
                phase2(i, q, U)
                turn(*back(i, q, 1), U - 1)
                turn(i, q, U)

            units(pe, body, tail)

        @block.vector
        def _(dve):
            nc.vector.memset(HST[:, :, :, :], 0.0).then_inc(s_z, 1)

            def body(i, q, U):
                dr, k = q // BATCH, q % 2
                dve.wait_ge(s_t, U + 1)
                nc.vector.tensor_tensor(GM[:, k, :], t_ps[:, k, 1, :], m.tri[:, 2 * dr, :], ALU.mult).then_inc(s_gm, 1)
                if not early(U):
                    dve.wait_ge(s_y, U - 1)
                nc.vector.tensor_tensor(DX[:, k, :, :], t_ps[:, k, 0, :].rearrange("p (h c) -> p h c", h=2),
                                        m.DT[:, bass.ds(tile(i, q), 1), 2 * dr:2 * dr + 2].rearrange("p o h -> p h o")
                                        .broadcast_to([P, 2, HD]), ALU.mult).then_inc(s_dx, 1)
                dve.wait_ge(s_dx, U + 1)
                nc.vector.tensor_tensor(DS[:, k, :, :], DX[:, k, :, :], heads(i, q, 1), ALU.mult).then_inc(s_ds, 1)
                dve.wait_ge(s_ed, U + 1)
                dve.wait_ge(s_gm, U + 1)
                nc.vector.tensor_tensor(MT[:, k, :, :], ED[:, k, :, :], GM[:, k, :].unsqueeze(1).broadcast_to([P, 2, P]),
                                        ALU.mult).then_inc(s_mt, 1)
                if not early(U, 1):
                    result(*back(i, q, 1), U - 1)

            def result(i, q, U):
                k = q % 2
                dve.wait_ge(s_y, U + 1)
                if not early(U):
                    dve.wait_ge(s_yt, U - 1)
                two = lambda n: y_ps[:, k, n, :].rearrange("p (h c) -> p h c", h=2)
                nc.vector.tensor_tensor(YT[:, k, :, :], two(1), heads(i, q, 0), ALU.mult).then_inc(s_y1, 1)
                nc.vector.tensor_tensor(HD1[:, k, :, :], HST[:, q, :, :], heads(i, q, 2), ALU.mult).then_inc(s_h1, 1)
                dve.wait_ge(s_y1, U + 1)
                nc.vector.tensor_tensor(YT[:, k, :, :], two(0), YT[:, k, :, :], ALU.add).then_inc(s_y2, 1)
                dve.wait_ge(s_h1, U + 1)
                nc.vector.tensor_tensor(HST[:, q, :, :], two(2), HD1[:, k, :, :], ALU.add).then_inc(s_h2, 1)

            def tail():
                result(*LAST, STEPS * SEQS - 1)

            units(dve, body, tail)


def stage_mamba_output(nc, d, g, m):
    with ExitStack() as ctx:
        sb, ps, sem = alloc(nc, ctx)
        wp = sb("wp", [P, DIRS, HD])
        op = sb("op", [P, P])
        YG = sb("YG", [P, DIRS, TOK])
        SQ = sb("oSQ", [P, 2, BLK])
        ST, R = sb("oST", [P, 2, 4]), sb("oR", [P, 2, 4])
        DG = sb("oDG", [P, 2, 4, P])
        CAT = sb("CAT", [P, 2, BLK])
        eps = sb("oeps", [P, 1])
        ms_ps, r_ps = ps("oms", [P, 2, BLK]), ps("or", [P, 2, BLK])
        cat_ps, o_ps = ps("cat_ps", [P, 2, BLK]), ps("oo_ps", [P, 2, BLK])
        s_w, s_e, s_g1, s_g2, s_sq, s_ms, s_st, s_r, s_dg, s_b, s_yn, s_cat, s_cc, s_o, s_out = (
            sem("o_" + n) for n in ("w", "e", "g1", "g2", "sq", "ms", "st", "r", "dg", "b", "yn", "cat", "cc", "o", "out"))
        ITEMS = DIRS * BLKS
        GN, DS = (g.vec["gn_f"], g.vec["gn_b"]), (g.vec["D_f"], g.vec["D_b"])

        def cols(n):
            return slice((n // 2) * BLK, (n // 2 + 1) * BLK)
        block = ctx.enter_context(nc.Block())

        @block.sync
        def _(sp):
            sp.dma_start(wp[:, :, :], d["wp"]).then_inc(s_w, 16)
            sp.dma_start(op[:, :], d["opT"]).then_inc(s_w, 16)

        @block.tensor
        def _(pe):
            pe.wait_ge(s_w, 32)
            for n in range(ITEMS + 2):
                if n < ITEMS:
                    pe.wait_ge(s_sq, n + 1)
                    if n >= 2:
                        pe.wait_ge(s_st, n - 1)
                    for t in range(4):
                        mm = nc.tensor.matmul(ms_ps[:, n % 2, t:t + 1], SQ[:, n % 2, t * P:(t + 1) * P], g.mean_col[:, :],
                                              start=True, stop=True)
                    mm.then_inc(s_ms, 1)
                if 1 <= n <= ITEMS:
                    k = n - 1
                    pe.wait_ge(s_dg, k + 1)
                    if k >= 2:
                        pe.wait_ge(s_yn, k - 1)
                    nc.tensor.matmul(r_ps[:, k % 2, :], g.ones[:, :], DG[:, k % 2, :, :], start=True, stop=True).then_inc(s_b, 1)
                if n >= 2:
                    k = n - 2
                    blk, dr = k // 2, k % 2
                    pe.wait_ge(s_yn, k + 1)
                    if blk >= 2:
                        pe.wait_ge(s_cc, blk - 1)
                    nc.tensor.matmul(cat_ps[dr * HD:(dr + 1) * HD, blk % 2, :], wp[:, dr, :], YG[:, dr, cols(k)],
                                     start=True, stop=True).then_inc(s_cat, 1)
                    if dr == 1:
                        pe.wait_ge(s_cc, blk + 1)
                        if blk >= 2:
                            pe.wait_ge(s_out, blk - 1)
                        nc.tensor.matmul(o_ps[:, blk % 2, :], op[:, :], CAT[:, blk % 2, :], start=True, stop=True).then_inc(s_o, 1)

        @block.scalar
        def _(act):
            nc.scalar.preload_act_table(ACT.Sqrt)
            act.wait_ge(s_e, 1)
            for n in range(ITEMS + 2):
                if n < ITEMS:
                    act.wait_ge(s_g2, n + 1)
                    if n >= 2:
                        act.wait_ge(s_ms, n - 1)
                    nc.scalar.activation(SQ[:, n % 2, :], YG[:, n % 2, cols(n)], ACT.Square).then_inc(s_sq, 1)
                    act.wait_ge(s_ms, n + 1)
                    if n >= 2:
                        act.wait_ge(s_r, n - 1)
                    nc.scalar.activation(ST[:, n % 2, :], ms_ps[:, n % 2, 0:4], ACT.Sqrt, bias=eps[:, :]).then_inc(s_st, 1)
                if n >= 2 and n % 2:
                    blk = (n - 2) // 2
                    act.wait_ge(s_cat, 2 * blk + 2)
                    if blk >= 2:
                        act.wait_ge(s_o, blk - 1)
                    nc.scalar.activation(CAT[:, blk % 2, :], cat_ps[:, blk % 2, :], ACT.Copy).then_inc(s_cc, 1)

        @block.vector
        def _(dve):
            nc.vector.memset(eps[:, :], 1e-5).then_inc(s_e, 1)
            for n in range(ITEMS + 3):
                if n < ITEMS:
                    dr = n % 2
                    nc.vector.scalar_tensor_tensor(out=YG[:, dr, cols(n)], in0=m.XBC[:, dr, 0, cols(n)], scalar=DS[dr],
                                                   in1=m.YB[:, dr, cols(n)], op0=ALU.mult, op1=ALU.add).then_inc(s_g1, 1)
                    dve.wait_ge(s_g1, n + 1)
                    nc.vector.tensor_tensor(YG[:, dr, cols(n)], YG[:, dr, cols(n)], m.SZ[:, dr, cols(n)], ALU.mult).then_inc(s_g2, 1)
                if 1 <= n <= ITEMS:
                    k = n - 1
                    dve.wait_ge(s_st, k + 1)
                    nc.vector.reciprocal(R[:, k % 2, :], ST[:, k % 2, :]).then_inc(s_r, 1)
                    dve.wait_ge(s_r, k + 1)
                    if k >= 2:
                        dve.wait_ge(s_b, k - 1)
                    nc.vector.tensor_tensor(DG[:, k % 2, :, :], g.ident[:, :].unsqueeze(1).broadcast_to([P, 4, P]),
                                            R[:, k % 2, :].unsqueeze(2).broadcast_to([P, 4, P]), ALU.mult).then_inc(s_dg, 1)
                    dve.wait_ge(s_b, k + 1)
                    dve.wait_ge(s_g2, k + 1)
                    y = YG[:, k % 2, cols(k)]
                    nc.vector.scalar_tensor_tensor(out=y, in0=y, scalar=GN[k % 2], in1=r_ps[:, k % 2, :],
                                                   op0=ALU.mult, op1=ALU.mult).then_inc(s_yn, 1)
                if n >= 4 and n % 2 == 0:
                    blk = (n - 4) // 2
                    dve.wait_ge(s_o, blk + 1)
                    at = slice(blk * BLK, (blk + 1) * BLK)
                    nc.vector.scalar_tensor_tensor(out=g.Y[:, at], in0=o_ps[:, blk % 2, :], scalar=g.vec["op_b"],
                                                   in1=g.H[:, at], op0=ALU.add, op1=ALU.add).then_inc(s_out, 1)


def stage_mamba(nc, d, g):
    with ExitStack() as ctx:
        sb, _, _ = alloc(nc, ctx)
        m = Shared()
        m.XBC, m.SZ = sb("XBC", [P, DIRS, 3, TOK]), sb("SZ", [P, DIRS, TOK])
        m.DT, m.AA, m.EX = sb("DT", [P, TILES, 4]), sb("AA", [P, TILES, 4]), sb("EX", [P, 3, 4, TILES])
        m.tri = sb("tri", [P, 4, P])
        stage_mamba_project(nc, d, g, m)
        with ExitStack() as inner:
            m.YB = inner.enter_context(nc.sbuf_tensor("YB", [P, DIRS, TOK], F32))
            stage_mamba_scan(nc, g, m)
            stage_mamba_output(nc, d, g, m)


def stage_ffn(nc, d, g, out):
    CH = HID1 // P
    with ExitStack() as ctx:
        sb, ps, sem = alloc(nc, ctx)
        wr, br = sb("wr", [P, BLOCKS16]), sb("br", [P, BLOCKS16])
        w1, b1, w2 = sb("w1", [P, HID1]), sb("b1", [P, CH]), sb("w2", [P, CH, P])
        sel, identb = sb("fsel", [BLOCKS16, HID1], BF16), sb("fidentb", [P, P], BF16)
        shape = [P, TILES, BLOCKS16]
        V, MX, SM, RC = sb("fV", shape), sb("fMX", [P, TILES]), sb("fSM", [P, TILES]), sb("fRC", [P, TILES])
        PA, PR = sb("PA", [P, TILES, BLOCKS16 + FTOP]), sb("fPR", [P, TILES, BLOCKS16 + FTOP])
        T8, MK = sb("fT8", [P, TILES, 8]), sb("MK", shape, BF16)
        MKT = sb("MKT", [BLOCKS16, TOK], BF16)
        HR = sb("HR", [P, CH, TOK])
        lg = ps("flg", [P, 512])
        mt_ps = ps("mt_ps", [BLOCKS16, 8, P], BF16)
        h_ps, mb_ps, y_ps = ps("fh", [P, 2, BLK]), ps("fmb", [P, 2, BLK]), ps("fy", [P, 2, BLK])
        s_w, s_lg, s_v, s_exp, s_mt, s_mev, s_h, s_hr, s_mb, s_hm, s_y, s_yb, s_x, s_out = (
            sem("f_" + n) for n in ("w", "lg", "v", "exp", "mt", "mev", "h", "hr", "mb", "hm", "y", "yb", "x", "out"))
        JOBS = BLKS * CH

        def cols(b):
            return slice(b * BLK, (b + 1) * BLK)
        block = ctx.enter_context(nc.Block())

        @block.sync
        def _(sp):
            for dst, src in ((wr[:, :], d["wr"]), (br[:, :], d["br"]), (w1[:, :], d["w1T"]), (b1[:, :], d["b1"]), (w2[:, :, :], d["w2T"]),
                             (sel[:, :], d["self"]), (identb[:, :], d["identb"])):
                sp.dma_start(dst, src).then_inc(s_w, 16)
            for b in range(BLKS):
                sp.wait_ge(s_x, b + 1)
                sp.dma_start(out[:, cols(b)], g.X[:, cols(b)]).then_inc(s_out, 16)
            sp.wait_ge(s_out, 16 * BLKS)

        @block.tensor
        def _(pe):
            pe.wait_ge(s_w, 112)
            for t in range(TILES):
                mm = nc.tensor.matmul(lg[:, t * BLOCKS16:(t + 1) * BLOCKS16], g.H[:, t * P:(t + 1) * P], wr[:, :],
                                      start=True, stop=True)
            mm.then_inc(s_lg, 1)
            for J in range(JOBS):
                if J >= 2:
                    pe.wait_ge(s_hr, J - 1)
                nc.tensor.matmul(h_ps[:, J % 2, :], w1[:, (J % CH) * P:(J % CH + 1) * P], g.H[:, cols(J // CH)],
                                 start=True, stop=True).then_inc(s_h, 1)
            pe.wait_ge(s_v, FFN_STEPS)
            for half in range(2):
                if half:
                    pe.wait_ge(s_mev, 1)
                for t in range(8):
                    mm = nc.tensor.transpose(mt_ps[:, t, :], MK[:, 8 * half + t, :], identb[:, :])
                mm.then_inc(s_mt, 1)
            for J in range(JOBS + 1):
                if J < JOBS:
                    pe.wait_ge(s_mev, J // (JOBS // 2) + 1)
                    if J >= 2:
                        pe.wait_ge(s_hm, J - 1)
                    nc.tensor.matmul(mb_ps[:, J % 2, :], sel[:, (J % CH) * P:(J % CH + 1) * P], MKT[:, cols(J // CH)],
                                     start=True, stop=True).then_inc(s_mb, 1)
                if J >= 1:
                    K = J - 1
                    b, c = K // CH, K % CH
                    pe.wait_ge(s_hm, K + 1)
                    if b >= 2 and c == 0:
                        pe.wait_ge(s_yb, b - 1)
                    mm = nc.tensor.matmul(y_ps[:, b % 2, :], w2[:, c, :], HR[:, c, cols(b)], start=(c == 0), stop=(c == CH - 1))
                    if c == CH - 1:
                        mm.then_inc(s_y, 1)

        @block.scalar
        def _(act):
            nc.scalar.preload_act_table(ACT.Exp)
            act.wait_ge(s_w, 112)
            for J in range(JOBS):
                if J == 4:
                    act.wait_ge(s_v, 4)
                    nc.scalar.activation(V[:, :, :], V[:, :, :], ACT.Exp).then_inc(s_exp, 1)
                act.wait_ge(s_h, J + 1)
                nc.scalar.activation(HR[:, J % CH, cols(J // CH)], h_ps[:, J % 2, :], ACT.Relu,
                                     bias=b1[:, J % CH:J % CH + 1]).then_inc(s_hr, 1)
            for half in range(2):
                act.wait_ge(s_mt, half + 1)
                nc.scalar.activation(MKT[:, half * SEQ:(half + 1) * SEQ].rearrange("e (t k) -> e t k", t=8),
                                     mt_ps[:, :, :], ACT.Copy).then_inc(s_mev, 1)
            for b in range(BLKS):
                act.wait_ge(s_y, b + 1)
                nc.scalar.activation(g.Y[:, cols(b)], y_ps[:, b % 2, :], ACT.Identity, bias=g.vec["b2"]).then_inc(s_yb, 1)

        @block.vector
        def _(dve):
            n = 0

            def step(ins, wait=True):
                nonlocal n
                ins.then_inc(s_v, 1)
                n += 1
                if wait:
                    dve.wait_ge(s_v, n)

            over = lambda t: t[:, :].unsqueeze(2).broadcast_to(shape)
            dve.wait_ge(s_lg, 1)
            step(nc.vector.tensor_tensor(V[:, :, :], lg[:, 0:TILES * BLOCKS16].rearrange("p (t e) -> p t e", t=TILES),
                                         br[:, :].unsqueeze(1).broadcast_to(shape), ALU.add))
            step(nc.vector.tensor_reduce(MX[:, :], V[:, :, :], AX.X, ALU.max))
            step(nc.vector.tensor_tensor(V[:, :, :], V[:, :, :], over(MX), ALU.subtract))
            step(nc.vector.memset(PA[:, :, BLOCKS16:BLOCKS16 + 1], 2.0))
            for k in range(1, FTOP):
                step(nc.vector.memset(PA[:, :, BLOCKS16 + k:BLOCKS16 + k + 1], 2.0 + k))
            dve.wait_ge(s_exp, 1)
            step(nc.vector.tensor_reduce(SM[:, :], V[:, :, :], AX.X, ALU.add))
            step(nc.vector.reciprocal(RC[:, :], SM[:, :]))
            step(nc.vector.tensor_tensor(PA[:, :, 0:BLOCKS16], V[:, :, :], over(RC), ALU.mult))
            for t in range(TILES):
                step(nc.vector.max(T8[:, t, :], PA[:, t, :]), wait=(t == TILES - 1))
            for t in range(TILES):
                step(nc.vector.match_replace(PR[:, t, :], T8[:, t, :], PA[:, t, :], -1.0), wait=(t == TILES - 1))
            step(nc.vector.tensor_scalar(MK[:, :, :], PR[:, :, 0:BLOCKS16], -1.0, None, ALU.is_equal))
            assert n == FFN_STEPS, n
            for J in range(JOBS):
                at = HR[:, J % CH, cols(J // CH)]
                dve.wait_ge(s_mb, J + 1)
                dve.wait_ge(s_hr, J + 1)
                nc.vector.tensor_tensor(at, at, mb_ps[:, J % 2, :], ALU.mult).then_inc(s_hm, 1)
            for b in range(BLKS):
                batch = b * BLK // SEQ
                dve.wait_ge(s_yb, b + 1)
                nc.vector.scalar_tensor_tensor(out=g.X[:, cols(b)], in0=g.Y[:, cols(b)],
                                               scalar=g.mod[:, 1, 5, batch:batch + 1], in1=g.X[:, cols(b)],
                                               op0=ALU.mult, op1=ALU.add).then_inc(s_x, 1)


FFN_STEPS = 43


def stage_residual(nc, g, layer, which):
    with ExitStack() as ctx:
        block = ctx.enter_context(nc.Block())

        @block.vector
        def _(dve):
            for b in range(BATCH):
                cols = slice(b * SEQ, (b + 1) * SEQ)
                nc.vector.scalar_tensor_tensor(out=g.X[:, cols], in0=g.Y[:, cols], scalar=g.mod[:, layer, which, b:b + 1],
                                               in1=g.X[:, cols], op0=ALU.mult, op1=ALU.add)


VECS = ("g_norm", "norm_w", "op_b", "b2", "gn_f", "gn_b", "D_f", "D_b")


def program(nc, d, out):
    with ExitStack() as ctx:
        sb, _, _ = alloc(nc, ctx)
        g = Shared()
        g.X, g.H, g.U, g.Y = (sb(n, [P, TOK]) for n in ("X", "H", "U", "Y"))
        g.mod, g.vecs = sb("mod", [P, 2, 6, BATCH]), sb("vecs", [P, len(VECS)])
        g.ident, g.center, g.ones = (sb(n, [P, P]) for n in ("ident", "center", "ones"))
        g.mean_col = sb("mean_col", [P, 1])
        g.vec = {n: g.vecs[:, i:i + 1] for i, n in enumerate(VECS)}
        stage_modulation(nc, d, g)
        stage_norm(nc, g, "n0", 0, 0, rms=(g.vec["g_norm"], float(np.finfo(np.float32).eps)))
        stage_attention(nc, d, g)
        stage_residual(nc, g, 0, 2)
        stage_norm(nc, g, "n1", 0, 1)
        stage_moe(nc, d, g)
        stage_residual(nc, g, 0, 5)
        stage_norm(nc, g, "n2", 1, 0, rms=(g.vec["norm_w"], 1e-5))
        stage_mamba(nc, d, g)
        stage_residual(nc, g, 1, 2)
        stage_norm(nc, g, "n3", 1, 1)
        stage_ffn(nc, d, g, out)


def constants():
    def bits(a):
        return np.ascontiguousarray((np.ascontiguousarray(a, np.float32).view(np.uint32) >> 16).astype(np.uint16))
    inv = (1.0 / np.float32(10000.0) ** (np.arange(0, DH, 2, dtype=np.float32) / np.float32(DH))).astype(np.float32)
    ang = np.repeat(np.arange(SEQ, dtype=np.float32)[:, None] * inv, 2, axis=-1)
    sign = np.where(np.arange(DH) % 2 == 0, np.float32(-1), np.float32(1))
    cs = np.stack([np.cos(ang), np.sin(ang) * sign])
    cs = np.tile(cs.transpose(2, 1, 0), (2, BATCH, 1))
    cs = cs.reshape(P, ITERS, ITER, 2).transpose(0, 1, 3, 2).reshape(P, -1)
    i, j = np.arange(P)[:, None] % SEG, np.arange(KEYS)[None, :]
    mask = np.where((j >= SEG) | (j <= i), 0.0, -BIG)
    r, c = np.arange(P)[:, None], np.arange(P)[None, :]
    tri = np.stack([r <= c, r > c, r >= c, r < c], axis=1)
    sel = np.zeros((CHUNKS, P, 2, P), np.float32)
    for ch in range(CHUNKS):
        for p in range(P):
            if ch < CHUNKS - 2:
                e = (ch * P + p) // FF
                sel[ch, e, 0, p] = sel[ch, EXPERTS + e, 0, p] = sel[ch, e, 1, p] = 1
            elif p < FF:
                sel[ch, EXPERTS, 1, p] = 1
    self_ = np.repeat(np.eye(BLOCKS16, dtype=np.float32), FBLK, axis=1)
    eye = np.eye(P, dtype=np.float32)
    f = lambda a: np.ascontiguousarray(a, np.float32)
    return {"cs": f(cs), "maskb": bits(np.tile(mask, (1, QG))), "identb": bits(eye), "ident": eye,
            "center": f(eye - np.float32(1 / P)), "tri": f(tri), "sel": bits(sel.reshape(CHUNKS, P, 2 * P)),
            "self": bits(self_)}


def layouts(x):
    a = {k: np.asarray(v) for k, v in x.items()}
    L = {}
    L["xT"] = a["L0_attn_seq"].reshape(TOK, P).T
    L["ct"] = np.stack([a["L0_c"].T, a["L1_c"].T], 1)
    L["wmod"] = np.stack([a["L0_wmod"], a["L1_wmod"]], 1)
    L["vecs"] = np.stack([a["L0_attn_g_norm"], a["L1_attn_norm_w"], a["L1_attn_op_b"], a["L1_ffn_b2"],
                          a["L1_attn_f_gnorm_w"], a["L1_attn_b_gnorm_w"],
                          np.repeat(a["L1_attn_f_D"], HD), np.repeat(a["L1_attn_b_D"], HD)], 1)
    w = a["L0_attn_W_qkv"]
    qk = w[:, 0:2 * HEADS * DH].reshape(P, 2 * PAIRS, P)
    L["wqk"] = np.stack([qk, qk.reshape(P, 2 * PAIRS, P // 2, 2)[..., ::-1].reshape(P, 2 * PAIRS, P)], 2)
    L["wv"] = w[:, 2 * HEADS * DH:]
    L["wo"] = a["L0_attn_W_out"].reshape(PAIRS, P, P).transpose(1, 0, 2)
    pm = a["L0_attn_pm"]
    L["pmk"] = pm[0].reshape(PAIRS, 2, PM, DH).transpose(1, 3, 0, 2).reshape(P, PAIRS, PM)
    L["pmv"] = pm[1].transpose(1, 0, 2).reshape(PM, HEADS * DH)
    L["gateT"] = a["L0_ffn_gate_w"].T
    L["gbias"] = np.broadcast_to(a["L0_ffn_gate_bias"], (P, EXPERTS))

    def hidden(e, s):
        s = np.concatenate([s.reshape(2, FF, P), np.zeros((2, P - FF, P), s.dtype)], 1)
        return np.concatenate([e.reshape(-1, P), s.reshape(-1, P)]).reshape(CHUNKS, P, P)
    wg = hidden(a["L0_ffn_Wg"], a["L0_ffn_Sg"]).transpose(0, 2, 1)
    wu = hidden(a["L0_ffn_Wu"], a["L0_ffn_Su"]).transpose(0, 2, 1)
    wd = hidden(a["L0_ffn_Wd"].transpose(0, 2, 1), a["L0_ffn_Sd"].T)
    L["w3"] = np.stack([wg, wu, wd], 2).reshape(CHUNKS, P, 3 * P)
    dirs = ("f", "b")
    inw = [a[f"L1_attn_{k}_in_w"].T for k in dirs]
    L["wxbc"] = np.stack([np.concatenate([m[:, P:4 * P]] * 2, 0) for m in inw], 1)
    L["wz"] = np.stack([np.concatenate([m[:, 0:P], np.zeros((HD, P), m.dtype)]) for m in inw], 1)
    wdt = np.zeros((P, 4), np.float32)
    wdt[0:HD, 0:2], wdt[HD:P, 2:4] = inw[0][:, 4 * P:], inw[1][:, 4 * P:]
    L["wdt"] = wdt
    cw = [a[f"L1_attn_{k}_conv_w"].T for k in dirs]
    L["cw"] = np.stack([np.stack([np.repeat(m[[3 - 2 * q, 2 - 2 * q]], HD, axis=0) for q in range(2)], 1) for m in cw], 1)
    L["cb"] = np.stack([a[f"L1_attn_{k}_conv_b"].reshape(3, P).T for k in dirs], 1)
    L["dtb"] = np.broadcast_to(np.concatenate([a[f"L1_attn_{k}_dt_bias"] for k in dirs]), (P, 4))
    L["alog"] = np.broadcast_to(np.concatenate([a[f"L1_attn_{k}_A_log"] for k in dirs]), (P, 4))
    L["wp"] = np.stack([a[f"L1_attn_{k}_outp_w"].T for k in dirs], 1)
    L["opT"] = a["L1_attn_op_w"].T
    L["wr"] = a["L1_ffn_w_router"]
    L["br"] = np.broadcast_to(a["L1_ffn_b_router"], (P, BLOCKS16))
    L["w1T"] = a["L1_ffn_w1"].T
    L["b1"] = a["L1_ffn_b1"].reshape(HID1 // P, P).T
    L["w2T"] = a["L1_ffn_w2"].T.reshape(HID1 // P, P, P).transpose(1, 0, 2)
    return {k: np.ascontiguousarray(v) for k, v in L.items()}


def kernel(**inputs):
    import concourse.bacc as bacc
    from concourse.bass_utils import run_bass_kernel_spmd

    arrays = {**layouts(inputs), **constants()}
    nc = bacc.Bacc("TRN2", target_bir_lowering=False, num_devices=1)
    aps = {n: nc.dram_tensor(f"in_{n}", a.shape, mybir.dt.from_np(a.dtype), kind="ExternalInput").ap()
           for n, a in arrays.items()}
    d = {n: ap.bitcast(BF16) if arrays[n].dtype == np.uint16 else ap for n, ap in aps.items()}
    out = nc.dram_tensor("out_xT", (P, TOK), F32, kind="ExternalOutput").ap()
    program(nc, d, out)
    r = run_bass_kernel_spmd(nc, [{f"in_{n}": a for n, a in arrays.items()}], core_ids=[0])
    return np.ascontiguousarray(r.results[0]["out_xT"].T).reshape(BATCH, SEQ, P)
```

```python
from contextlib import ExitStack

import numpy as np

import concourse.bass as bass
from concourse import mybir

F32 = mybir.dt.float32
F32R = mybir.dt.float32r
BF16 = mybir.dt.bfloat16
ALU = mybir.AluOpType
ACT = mybir.ActivationFunctionType
AX = mybir.AxisListType

P = 128
BATCH, SEQ = 2, 1024
TOK = BATCH * SEQ
TILES = TOK // P
BLK = 512
BLKS = TOK // BLK
HEADS, DH, SEG, PM = 16, 64, 64, 16
PAIRS = HEADS // 2
KEYS = SEG + PM
ITER = 256
ITERS = TOK // ITER
SEGS = ITER // SEG
QG = 4
UNITS = (ITER // P) * HEADS // QG
EXPERTS, FF, TOPK, GROUPS, TOPG = 64, 88, 8, 8, 4
GSIZE = EXPERTS // GROUPS
CHUNKS = EXPERTS * FF // P + 2
NST, HD = 128, 64
CONVPAD = 6
BLOCKS16, FBLK, FTOP = 16, 32, 4
HID1 = BLOCKS16 * FBLK
BIG = 1e30


class Shared:
    pass


def alloc(nc, ctx):
    def sb(name, shape, dt=F32):
        return ctx.enter_context(nc.sbuf_tensor(name, shape, dt))

    def ps(name, shape, dt=F32):
        return ctx.enter_context(nc.psum_tensor(name, shape, dt))

    def sem(name):
        return ctx.enter_context(nc.semaphore(name))
    return sb, ps, sem


def stage_modulation(nc, d, g):
    with ExitStack() as ctx:
        sb, ps, sem = alloc(nc, ctx)
        ct = sb("ct", [P, 2, BATCH])
        st = sb("st", [P, 2, BATCH])
        wmod = sb("wmod", [P, 2, 6 * P])
        mag = sb("mag", [P, 2, 2, BATCH])
        sgn = sb("sgn", [P, 2, 2, BATCH])
        mp = ps("mp", [P, 2, 6, BATCH])
        s_c, s_x, s_silu, s_mod, s_dve = sem("m_c"), sem("m_x"), sem("m_silu"), sem("m_mod"), sem("m_dve")
        block = ctx.enter_context(nc.Block())

        @block.sync
        def _(sp):
            sp.dma_start(ct[:, :, :], d["ct"]).then_inc(s_c, 16)
            sp.dma_start(wmod[:, :, :], d["wmod"]).then_inc(s_c, 16)
            sp.dma_start(g.X[:, :], d["xT"]).then_inc(s_x, 16)
            sp.dma_start(g.ident[:, :], d["ident"]).then_inc(s_x, 16)
            sp.dma_start(g.center[:, :], d["center"]).then_inc(s_x, 16)
            sp.dma_start(g.vecs[:, :], d["vecs"]).then_inc(s_x, 16)
            sp.wait_ge(s_x, 64)

        @block.scalar
        def _(act):
            act.wait_ge(s_c, 32)
            nc.scalar.activation(st[:, :, :], ct[:, :, :], ACT.Silu).then_inc(s_silu, 1)

        @block.tensor
        def _(pe):
            pe.wait_ge(s_silu, 1)
            for layer in range(2):
                for v in range(6):
                    mm = nc.tensor.matmul(mp[:, layer, v, :], wmod[:, layer, v * P:(v + 1) * P],
                                          st[:, layer, :], start=True, stop=True)
            mm.then_inc(s_mod, 1)

        @block.vector
        def _(dve):
            nc.vector.memset(g.mean_col[:, :], 1.0 / P).then_inc(s_dve, 1)
            nc.vector.memset(g.ones[:, :], 1.0).then_inc(s_dve, 1)
            nc.vector.memset(g.eps[:, 0:1], 1e-5).then_inc(s_dve, 1)
            nc.vector.memset(g.eps[:, 1:2], float(np.finfo(np.float32).eps)).then_inc(s_dve, 1)
            dve.wait_ge(s_mod, 1)
            nc.vector.tensor_copy(g.mod[:, :, :, :], mp[:, :, :, :]).then_inc(s_dve, 1)
            dve.wait_ge(s_dve, 5)
            for n, v in enumerate((1, 4)):
                nc.vector.tensor_scalar(g.mod[:, :, v, :], g.mod[:, :, v, :], 1.0, None, ALU.add).then_inc(s_dve, 1)
            gates = g.mod[:, :, 2:6:3, :]
            nc.vector.tensor_scalar(mag[:, :, :, :], gates, -1.0, None, ALU.mult).then_inc(s_dve, 1)
            nc.vector.tensor_scalar(sgn[:, :, :, :], gates, 0.0, 2.0, ALU.is_ge, ALU.mult).then_inc(s_dve, 1)
            dve.wait_ge(s_dve, 9)
            nc.vector.tensor_tensor(mag[:, :, :, :], mag[:, :, :, :], gates, ALU.max).then_inc(s_dve, 1)
            nc.vector.tensor_scalar(sgn[:, :, :, :], sgn[:, :, :, :], -1.0, None, ALU.add).then_inc(s_dve, 1)
            dve.wait_ge(s_dve, 11)
            nc.vector.tensor_scalar(mag[:, :, :, :], mag[:, :, :, :], 0.25, None, ALU.max).then_inc(s_dve, 1)
            dve.wait_ge(s_dve, 12)
            nc.vector.tensor_tensor(gates, mag[:, :, :, :], sgn[:, :, :, :], ALU.mult).then_inc(s_dve, 1)


def stage_norm(nc, g, tag, layer, half, rms=None, loads=()):
    norms = 2 if rms else 1
    scale, shift = (1, 0) if half == 0 else (4, 3)
    with ExitStack() as ctx:
        sb, ps, sem = alloc(nc, ctx)
        D = sb(tag + "D", [P, TOK])
        SQ = sb(tag + "SQ", [P, norms, TOK])
        ST = sb(tag + "ST", [P, norms, TILES])
        R = sb(tag + "R", [P, norms, TILES])
        DG = sb(tag + "DG", [P, norms, TOK])
        XN = sb(tag + "XN", [P, TOK])
        d_ps = ps(tag + "d_ps", [P, 2, BLK])
        ms_ps = ps(tag + "ms_ps", [P, 2, BLK])
        r_ps = ps(tag + "r_ps", [P, 2, BLK])
        s_cent, s_dcopy = sem(tag + "cent"), sem(tag + "dcopy")
        s_sq, s_ms, s_root, s_inv, s_diag = (sem(tag + n) for n in ("sq", "ms", "root", "inv", "diag"))
        s_r, s_xn, s_h = (sem(tag + n) for n in ("r", "xn", "h"))
        s_u = sem(tag + "u") if rms else None
        s_load = sem(tag + "load") if loads else None
        block = ctx.enter_context(nc.Block())
        TB = BLK // P

        @block.sync
        def _(sp):
            for dst, src in loads:
                sp.dma_start(dst, src).then_inc(s_load, 16)
            if loads:
                sp.wait_ge(s_load, 16 * len(loads))

        def cols(b):
            return slice(b * BLK, (b + 1) * BLK)

        @block.tensor
        def _(pe):
            def mean_square(n, b):
                pe.wait_ge(s_sq, n * BLKS + b + 1)
                if n * BLKS + b >= 2:
                    pe.wait_ge(s_root, n * BLKS + b - 1)
                for t in range(TB * b, TB * b + TB):
                    mm = nc.tensor.matmul(ms_ps[:, b % 2, t:t + 1], SQ[:, n, t * P:(t + 1) * P], g.mean_col[:, :],
                                          start=True, stop=True)
                mm.then_inc(s_ms, 1)

            def broadcast(n, b):
                pe.wait_ge(s_diag, n * BLKS + b + 1)
                i = n * BLKS + b
                if n == 0 and b >= 2:
                    pe.wait_ge(s_xn, b - 1)
                if n == 1:
                    pe.wait_ge(s_xn, b + 3 if b < 2 else BLKS)
                    if b >= 2:
                        pe.wait_ge(s_u, b - 1)
                nc.tensor.matmul(r_ps[:, i % 2, :], g.ones[:, :], DG[:, n, cols(b)], start=True, stop=True).then_inc(s_r, 1)

            for b in range(BLKS):
                if b >= 2:
                    pe.wait_ge(s_dcopy, b - 1)
                nc.tensor.matmul(d_ps[:, b % 2, :], g.center[:, :], g.X[:, cols(b)], start=True, stop=True).then_inc(s_cent, 1)
                if b >= 1:
                    mean_square(0, b - 1)
            mean_square(0, BLKS - 1)
            for n in range(norms):
                for b in range(BLKS):
                    broadcast(n, b)
                    if n == 0 and norms == 2:
                        mean_square(1, b)

        @block.scalar
        def _(act):
            nc.scalar.preload_act_table(ACT.Sqrt)

            def root(n, b):
                act.wait_ge(s_ms, n * BLKS + b + 1)
                tiles = slice(TB * b, TB * b + TB)
                nc.scalar.activation(ST[:, n, tiles], ms_ps[:, b % 2, tiles], ACT.Sqrt, bias=(rms[1] if n else g.eps5)).then_inc(s_root, 1)

            for b in range(BLKS):
                act.wait_ge(s_dcopy, b + 1)
                nc.scalar.activation(SQ[:, 0, cols(b)], D[:, cols(b)], ACT.Square).then_inc(s_sq, 1)
                if b >= 1:
                    root(0, b - 1)
            root(0, BLKS - 1)
            for b in range(BLKS):
                batch = b * BLK // SEQ
                act.wait_ge(s_xn, b + 1)
                nc.scalar.activation(g.H[:, cols(b)], XN[:, cols(b)], ACT.Identity,
                                     scale=g.mod[:, layer, scale, batch:batch + 1],
                                     bias=g.mod[:, layer, shift, batch:batch + 1]).then_inc(s_h, 1)
                if norms == 2:
                    act.wait_ge(s_h, b + 1)
                    nc.scalar.activation(SQ[:, 1, cols(b)], g.H[:, cols(b)], ACT.Square).then_inc(s_sq, 1)
                    if b >= 1:
                        root(1, b - 1)
            if norms == 2:
                root(1, BLKS - 1)

        @block.vector
        def _(dve):
            def inverse(n, b):
                i = n * BLKS + b
                tiles = slice(TB * b, TB * b + TB)
                dve.wait_ge(s_root, i + 1)
                nc.vector.reciprocal(R[:, n, tiles], ST[:, n, tiles]).then_inc(s_inv, 1)
                dve.wait_ge(s_inv, i + 1)
                nc.vector.tensor_tensor(DG[:, n, cols(b)].rearrange("p (t k) -> p t k", t=TB),
                                        g.ident[:, :].unsqueeze(1).broadcast_to([P, TB, P]),
                                        R[:, n, tiles].unsqueeze(2).broadcast_to([P, TB, P]), ALU.mult).then_inc(s_diag, 1)

            for b in range(BLKS):
                dve.wait_ge(s_cent, b + 1)
                nc.vector.tensor_copy(D[:, cols(b)], d_ps[:, b % 2, :]).then_inc(s_dcopy, 1)
                if b >= 1:
                    inverse(0, b - 1)
            inverse(0, BLKS - 1)
            for b in range(BLKS):
                dve.wait_ge(s_r, b + 1)
                dve.wait_ge(s_dcopy, b + 1)
                nc.vector.tensor_tensor(XN[:, cols(b)], D[:, cols(b)], r_ps[:, b % 2, :], ALU.mult).then_inc(s_xn, 1)
                if norms == 2 and b >= 1:
                    inverse(1, b - 1)
            if norms == 2:
                inverse(1, BLKS - 1)
                for b in range(BLKS):
                    dve.wait_ge(s_r, BLKS + b + 1)
                    dve.wait_ge(s_h, b + 1)
                    nc.vector.scalar_tensor_tensor(out=g.U[:, cols(b)], in0=g.H[:, cols(b)], scalar=rms[0],
                                                   in1=r_ps[:, b % 2, :], op0=ALU.mult, op1=ALU.mult).then_inc(s_u, 1)


NEIGHBOUR = [i ^ 1 for i in range(32)]


def attention_loads(d, g, sb):
    a = Shared()
    a.wv = sb("wv", [P, HEADS * DH])
    a.wo = sb("wo", [P, PAIRS, P])
    a.pmk = sb("pmk", [P, PAIRS, PM])
    a.maskb, a.identb = sb("maskb", [P, QG * KEYS], BF16), sb("identb", [P, P], BF16)
    a.V = sb("V", [KEYS, 2, SEGS, HEADS * DH])
    loads = [(g.Y[:, :], d["wqk"]), (a.wv[:, :], d["wv"]), (a.wo[:, :, :], d["wo"]),
             (a.pmk[:, :, :], d["pmk"]), (a.maskb[:, :], d["maskb"]), (a.identb[:, :], d["identb"])]
    for par in range(2):
        for seg in range(SEGS):
            loads.append((a.V[SEG:KEYS, par, seg, :], d["pmv"]))
    return a, loads


def stage_attention(nc, d, g, a):
    with ExitStack() as ctx:
        sb, ps, sem = alloc(nc, ctx)
        wqkh, wqkl = (sb(n, [P, 2 * PAIRS, P], F32R) for n in ("wqkh", "wqkl"))
        wvh, wvl = (sb(n, [P, HEADS * DH], F32R) for n in ("wvh", "wvl"))
        Gh, Gl = (sb(n, [P, 2, ITER], F32R) for n in ("Gh", "Gl"))
        cs = sb("cs", [P, 2, 2, ITER])
        T = sb("T", [P, 2, 2, ITER])
        S = sb("S", [P, 2, 2, ITER])
        Q = sb("Q", [P, 2, PAIRS, ITER])
        K = sb("K", [P, 2, PAIRS, SEGS, KEYS])
        MX, NM = sb("MX", [P, 2, QG]), sb("NM", [P, 2, QG])
        SM = sb("SM", [P, 2, QG])
        RC = sb("RC", [P, 2, QG])
        PR = sb("PR", [P, 4, QG, KEYS])
        PT = sb("PT", [KEYS, 4, QG, P])
        OT = sb("OT", [P, 2, PAIRS, ITER])
        s_bank = ps("s_bank", [P, 2, 512])
        pt_bank = ps("pt_bank", [P, 2, QG, P])
        o_bank = ps("o_bank", [P, QG, P])
        qk_bank = ps("qk_bank", [P, 2, 2, ITER])
        v_bank = ps("v_bank", [P, 512])
        s_wh, s_wl, s_pm, s_gh, s_gl, s_cs = (sem("a_" + n) for n in ("wh", "wl", "pm", "gh", "gl", "cs"))
        s_qk, s_rot, s_sin, s_add = (sem("a_" + n) for n in ("qk", "rot", "sin", "add"))
        s_v, s_vev = sem("a_v"), sem("a_vev")
        s_sc, s_mx, s_nm, s_exp, s_sum, s_rc, s_pr = (sem("a_" + n) for n in ("sc", "mx", "nm", "exp", "sum", "rc", "pr"))
        s_tr, s_ptev, s_av, s_oev, s_y, s_yev = (sem("a_" + n) for n in ("tr", "ptev", "av", "oev", "y", "yev"))
        ROPES = PAIRS
        VH = 2 * SEGS

        def loops(eng, body, first, tail):
            first()
            body(0, 0, "first")
            with eng.Fori(0, (ITERS - 2) // 2) as i:
                body(i * 2 + 1, 1, "mid")
                body(i * 2 + 2, 0, "mid")
            body(ITERS - 1, 1, "last")
            tail()

        def noop():
            pass

        wo, pmk, maskb, identb, V = a.wo, a.pmk, a.maskb, a.identb, a.V
        half = PAIRS * P
        splits = ((g.Y[:, 0:half].rearrange("p (a b) -> p a b", a=PAIRS), wqkh[:, 0:PAIRS, :], wqkl[:, 0:PAIRS, :]),
                  (a.wv[:, :], wvh[:, :], wvl[:, :]),
                  (g.Y[:, half:2 * half].rearrange("p (a b) -> p a b", a=PAIRS), wqkh[:, PAIRS:, :], wqkl[:, PAIRS:, :]))

        block = ctx.enter_context(nc.Block())

        @block.sync
        def _(sp):
            def load(n, par):
                src = d["cs"][bass.ds(n, 1), :, :].rearrange("o p n -> (o p) n")
                if not (isinstance(n, int) and n < 1):
                    sp.wait_ge(s_add, (n - 1) * ROPES + 1)
                sp.dma_start(cs[:, par, :, :].rearrange("p a b -> p (a b)"), src).then_inc(s_cs, 16)

            def first():
                load(0, 0)

            def body(it, par, which):
                if which != "last":
                    load(it + 1, 1 - par)

            loops(sp, body, first, noop)

        @block.tensor
        def _(pe):
            def scores(it, par, u):
                sp_, hh, odd = u // 4, (u // 2) % 2, u % 2
                U = it * UNITS + u
                if not (isinstance(it, int) and U < 2):
                    pe.wait_ge(s_exp, U - 1)
                bank = s_bank[:, u % 2, 0:QG * KEYS]
                nc.tensor.matmul(bank, identb[:, :], maskb[:, :], start=True, stop=False, skip_group_check=True)
                for j in range(QG):
                    for s in range(2):
                        mm = nc.tensor.matmul(
                            s_bank[SEG * s:SEG * (s + 1), u % 2, j * KEYS:(j + 1) * KEYS],
                            Q[DH * odd:DH * (odd + 1), par, QG * hh + j, P * sp_ + SEG * s:P * sp_ + SEG * (s + 1)],
                            K[DH * odd:DH * (odd + 1), par, QG * hh + j, 2 * sp_ + s, :],
                            start=False, stop=True, skip_group_check=True)
                mm.then_inc(s_sc, 1)

            def transposes(U, u):
                pe.wait_ge(s_pr, U + 1)
                if not (isinstance(U, int) and U < 2):
                    pe.wait_ge(s_ptev, U - 1)
                for j in range(QG):
                    mm = nc.tensor.transpose(pt_bank[0:KEYS, u % 2, j, :], PR[:, u % 4, j, :], g.ident[:, :])
                mm.then_inc(s_tr, 1)

            def values(U, u, it, par):
                sp_, hh = u // 4, (u // 2) % 2
                pe.wait_ge(s_ptev, U + 1)
                if u % 4 == 1:
                    pe.wait_ge(s_vev, it * VH + 4 * (sp_ + 1))
                if not (isinstance(U, int) and U == 1):
                    pe.wait_ge(s_oev, it * (UNITS // 2) + u // 2)
                for j in range(QG):
                    for s in range(2):
                        for odd in range(2):
                            head = 2 * (QG * hh + j) + odd
                            mm = nc.tensor.matmul(o_bank[DH * odd:DH * (odd + 1), j, SEG * s:SEG * (s + 1)],
                                                  V[:, par, 2 * sp_ + s, head * DH:(head + 1) * DH],
                                                  PT[:, (u - 1 + odd) % 4, j, SEG * s:SEG * (s + 1)], start=True, stop=True)
                mm.then_inc(s_av, 1)

            def project_qk(n, par, i):
                if not (isinstance(n, int) and n == 0 and i < 2):
                    pe.wait_ge(s_rot, 2 * (n * ROPES + i - 1))
                for h in range(2):
                    out, c = qk_bank[:, i % 2, h, :], 2 * i + h
                    nc.tensor.matmul(out, wqkh[:, c, :], Gh[:, par, :], start=True, stop=False)
                    nc.tensor.matmul(out, wqkh[:, c, :], Gl[:, par, :], start=False, stop=False)
                    mm = nc.tensor.matmul(out, wqkl[:, c, :], Gh[:, par, :], start=False, stop=True)
                mm.then_inc(s_qk, 1)

            def project_v(n, par, v):
                if not (isinstance(n, int) and n == 0 and v == 0):
                    pe.wait_ge(s_vev, n * VH + 2 * v)
                cols, toks = slice(512 * (v % 2), 512 * (v % 2 + 1)), slice(P * (v // 2), P * (v // 2 + 1))
                nc.tensor.matmul(v_bank[:, :], Gh[:, par, toks], wvh[:, cols], start=True, stop=False)
                nc.tensor.matmul(v_bank[:, :], Gl[:, par, toks], wvh[:, cols], start=False, stop=False)
                nc.tensor.matmul(v_bank[:, :], Gh[:, par, toks], wvl[:, cols], start=False, stop=True).then_inc(s_v, 1)

            def project_out(it, par, vdone):
                pe.wait_ge(s_oev, (it + 1) * (UNITS // 2))
                pe.wait_ge(s_vev, vdone)
                for hp in range(PAIRS):
                    mm = nc.tensor.matmul(v_bank[:, 0:ITER], wo[:, hp, :], OT[:, par, hp, :],
                                          start=(hp == 0), stop=(hp == PAIRS - 1))
                mm.then_inc(s_y, 1)

            def first():
                pe.sem_inc(s_y, 2)
                pe.wait_ge(s_wl, 3)
                pe.wait_ge(s_gl, 1)
                for i in range(ROPES):
                    project_qk(0, 0, i)
                    if i % 2 == 0:
                        project_v(0, 0, i // 2)

            def body(it, par, which):
                if which == "first":
                    pe.wait_ge(s_pm, 2 * SEGS)
                for u in range(UNITS):
                    if u == 0:
                        pe.wait_ge(s_add, it * ROPES + ROPES // 2)
                    if u == 2:
                        pe.wait_ge(s_add, (it + 1) * ROPES)
                    scores(it, par, u)
                    old = not (which == "first" and u < 2)
                    pu, pit, ppar = (u - 2, it, par) if u >= 2 else (u + UNITS - 2, it - 1, 1 - par)
                    if old:
                        transposes(pit * UNITS + pu, pu)
                    if u == 3 and which != "first":
                        project_out(it - 1, 1 - par, (it + 1) * VH + (4 if which != "last" else 0))
                    if which != "last":
                        if u == 0:
                            pe.wait_ge(s_gl, it + 2)
                        project_qk(it + 1, 1 - par, u)
                        if u == 4 and which != "first":
                            pe.wait_ge(s_yev, it)
                        if u % 2 == 0:
                            project_v(it + 1, 1 - par, u // 2)
                    if old and pu % 2:
                        values(pit * UNITS + pu, pu, pit, ppar)

            def tail():
                it = ITERS - 1
                for u in (UNITS - 2, UNITS - 1):
                    transposes(it * UNITS + u, u)
                values(it * UNITS + UNITS - 1, UNITS - 1, it, 1)
                pe.wait_ge(s_yev, it)
                project_out(it, 1, ITERS * VH)

            loops(pe, body, first, tail)

        @block.vector
        def _(dve):
            def low_block(n, par):
                dve.wait_ge(s_gh, n + 1)
                if not (isinstance(n, int) and n < 2):
                    dve.wait_ge(s_v, (n - 1) * (VH // 2))
                nc.vector.tensor_tensor(Gl[:, par, :], g.U[:, bass.ds(n * ITER, ITER)], Gh[:, par, :], ALU.subtract).then_inc(s_gl, 1)

            def rope(n, par, i):
                dve.wait_ge(s_qk, n * ROPES + i + 1)
                if not (isinstance(n, int) and n == 0 and i < 2):
                    dve.wait_ge(s_add, n * ROPES + i - 1)
                if i == 0:
                    dve.wait_ge(s_cs, (n + 1) * 16)
                nc.vector.tensor_tensor(T[:, i % 2, :, :], qk_bank[:, i % 2, :, :],
                                        cs[:, par, 0, :].unsqueeze(1).broadcast_to([P, 2, ITER]),
                                        ALU.mult).then_inc(s_rot, 1)
                nc.vector.stream_shuffle(S[:, i % 2, :, :], qk_bank[:, i % 2, :, :], NEIGHBOUR).then_inc(s_rot, 1)

            def softmax_a(it, u):
                U = it * UNITS + u
                S = s_bank[:, u % 2, 0:QG * KEYS].rearrange("p (j k) -> p j k", j=QG)
                dve.wait_ge(s_sc, U + 1)
                nc.vector.tensor_reduce(MX[:, u % 2, :], S, AX.X, ALU.max).then_inc(s_mx, 1)
                dve.wait_ge(s_mx, U + 1)
                if not (isinstance(it, int) and U < 2):
                    dve.wait_ge(s_exp, U - 1)
                nc.vector.tensor_scalar(NM[:, u % 2, :], MX[:, u % 2, :], -(DH ** -0.5), None, ALU.mult).then_inc(s_nm, 1)

            def softmax_b(it, u):
                U = it * UNITS + u
                dve.wait_ge(s_exp, U + 1)
                nc.vector.tensor_reduce(SM[:, u % 2, :], PR[:, u % 4, :, :], AX.X, ALU.add).then_inc(s_sum, 1)
                dve.wait_ge(s_sum, U + 1)
                if not (isinstance(it, int) and U < 2):
                    dve.wait_ge(s_pr, U - 1)
                nc.vector.reciprocal(RC[:, u % 2, :], SM[:, u % 2, :]).then_inc(s_rc, 1)

            def normalise(it, u):
                dve.wait_ge(s_rc, it * UNITS + u + 1)
                nc.vector.tensor_tensor(PR[:, u % 4, :, :], PR[:, u % 4, :, :],
                                        RC[:, u % 2, :].unsqueeze(2).broadcast_to([P, QG, KEYS]), ALU.mult).then_inc(s_pr, 1)

            def first():
                for n, (raw, high, low) in enumerate(splits):
                    dve.wait_ge(s_wh, n + 1)
                    nc.vector.tensor_tensor(low, raw, high, ALU.subtract).then_inc(s_wl, 1)
                low_block(0, 0)
                for par in range(2):
                    for seg in range(SEGS):
                        nc.vector.tensor_copy(K[:, par, :, seg, SEG:KEYS], pmk[:, :, :]).then_inc(s_pm, 1)
                for i in range(ROPES):
                    rope(0, 0, i)

            def body(it, par, which):
                if which != "last":
                    low_block(it + 1, 1 - par)
                for u in range(UNITS):
                    softmax_a(it, u)
                    if which != "last":
                        rope(it + 1, 1 - par, u)
                    softmax_b(it, u)
                    normalise(it, u)
            loops(dve, body, first, noop)

        @block.gpsimd
        def _(pool):
            def turn(n, par, i):
                if i == 0:
                    pool.wait_ge(s_cs, (n + 1) * 16)
                pool.wait_ge(s_rot, 2 * (n * ROPES + i + 1))
                nc.gpsimd.tensor_tensor(S[:, i % 2, :, :], S[:, i % 2, :, :],
                                        cs[:, par, 1, :].unsqueeze(1).broadcast_to([P, 2, ITER]),
                                        ALU.mult).then_inc(s_sin, 1)

            def add(n, par, i):
                pool.wait_ge(s_sin, n * ROPES + i + 1)
                two = slice(4 * (i // 4) + 2 * (i % 2), 4 * (i // 4) + 2 * (i % 2) + 2)
                if i == 0 and not (isinstance(n, int) and n < 2):
                    pool.wait_ge(s_sc, (n - 1) * UNITS)
                if i % 4 < 2:
                    nc.gpsimd.tensor_tensor(Q[:, par, two, :], T[:, i % 2, :, :], S[:, i % 2, :, :], ALU.add).then_inc(s_add, 1)
                else:
                    nc.gpsimd.tensor_tensor(K[:, par, two, :, 0:SEG], T[:, i % 2, :, :].rearrange("p h (s k) -> p h s k", s=SEGS),
                                            S[:, i % 2, :, :].rearrange("p h (s k) -> p h s k", s=SEGS), ALU.add).then_inc(s_add, 1)

            def first():
                for i in range(ROPES):
                    turn(0, 0, i)
                    add(0, 0, i)

            def body(it, par, which):
                if which != "last":
                    for u in range(UNITS):
                        turn(it + 1, 1 - par, u)
                        add(it + 1, 1 - par, u)

            loops(pool, body, first, noop)

        @block.scalar
        def _(act):
            nc.scalar.preload_act_table(ACT.Exp)

            def exponent(it, u):
                U = it * UNITS + u
                act.wait_ge(s_nm, U + 1)
                if not (isinstance(it, int) and U < 4):
                    act.wait_ge(s_tr, U - 3)
                for j in range(QG):
                    ins = nc.scalar.activation(PR[:, u % 4, j, :], s_bank[:, u % 2, j * KEYS:(j + 1) * KEYS], ACT.Exp,
                                               scale=DH ** -0.5, bias=NM[:, u % 2, j:j + 1])
                ins.then_inc(s_exp, 1)

            def take_pt(U, u, it):
                act.wait_ge(s_tr, U + 1)
                if not (isinstance(U, int) and U < 4):
                    act.wait_ge(s_av, it * (UNITS // 2) + u // 2 - 1)
                nc.scalar.activation(PT[:, u % 4, :, :], pt_bank[0:KEYS, u % 2, :, :], ACT.Copy).then_inc(s_ptev, 1)

            def take_v(n, par, v):
                act.wait_ge(s_v, n * (VH // 2) + v + 1)
                if not (isinstance(n, int) and n < 2):
                    act.wait_ge(s_av, (n - 2) * (UNITS // 2) + (UNITS // 4) * (v // 2 + 1))
                for s in range(2):
                    nc.scalar.activation(V[0:SEG, par, 2 * (v // 2) + s, 512 * (v % 2):512 * (v % 2 + 1)],
                                         v_bank[SEG * s:SEG * (s + 1), :], ACT.Copy).then_inc(s_vev, 1)

            def take_o(U, u, it, par):
                act.wait_ge(s_av, it * (UNITS // 2) + u // 2 + 1)
                act.wait_ge(s_y, it + 1)
                sp_, hh = u // 4, (u // 2) % 2
                nc.scalar.activation(OT[:, par, QG * hh:QG * (hh + 1), P * sp_:P * (sp_ + 1)], o_bank[:, :, :],
                                     ACT.Copy).then_inc(s_oev, 1)

            def take_y(it):
                act.wait_ge(s_y, it + 3)
                nc.scalar.activation(g.Y[:, bass.ds(it * ITER, ITER)], v_bank[:, 0:ITER], ACT.Copy).then_inc(s_yev, 1)

            def high_block(n, par):
                if not (isinstance(n, int) and n < 2):
                    act.wait_ge(s_v, (n - 1) * (VH // 2))
                nc.scalar.activation(Gh[:, par, :], g.U[:, bass.ds(n * ITER, ITER)], ACT.Copy).then_inc(s_gh, 1)

            def first():
                for raw, high, _ in splits:
                    nc.scalar.activation(high, raw, ACT.Copy).then_inc(s_wh, 1)
                high_block(0, 0)
                for v in range(VH // 2):
                    take_v(0, 0, v)

            def body(it, par, which):
                if which == "first":
                    act.wait_ge(s_wl, 3)
                for u in range(UNITS):
                    old = not (which == "first" and u < 2)
                    pu, pit, ppar = (u - 2, it, par) if u >= 2 else (u + UNITS - 2, it - 1, 1 - par)
                    if old:
                        take_pt(pit * UNITS + pu, pu, pit)
                    if u == 0 and which != "last":
                        high_block(it + 1, 1 - par)
                    exponent(it, u)
                    if u == 3 and which != "first":
                        take_y(it - 1)
                    if which != "last" and u % 2 == 0:
                        take_v(it + 1, 1 - par, u // 2)
                    if old and pu % 2:
                        take_o(pit * UNITS + pu, pu, pit, ppar)

            def tail():
                it = ITERS - 1
                for u in (UNITS - 2, UNITS - 1):
                    take_pt(it * UNITS + u, u, it)
                take_o(it * UNITS + UNITS - 1, UNITS - 1, it, 1)
                take_y(it)

            loops(act, body, first, tail)


def stage_route(nc, d, g):
    with ExitStack() as ctx:
        sb, ps, sem = alloc(nc, ctx)
        gate = sb("gate", [P, EXPERTS])
        gbias = sb("gbias", [P, EXPERTS])
        shape = [P, TILES, EXPERTS]
        SC, SF, EQ, LOW = sb("SC", shape), sb("SF", shape), sb("EQ", shape), sb("LOW", shape)
        M1, CNT, M2 = (sb(n, [P, TILES, GROUPS]) for n in ("M1", "CNT", "M2"))
        GA, GR = sb("GA", [P, TILES, GROUPS + 8 - TOPG]), sb("GR", [P, TILES, GROUPS + 8 - TOPG])
        T8 = sb("T8", [P, TILES, 8])
        GM = sb("GM", [P, TILES, GROUPS])
        WS, WR = sb("WS", [P, TILES]), sb("WR", [P, TILES])
        RH = sb("RH", [P, TILES, EXPERTS], F32R)
        SP = sb("SP", [P, TILES, 2, EXPERTS])
        lg = ps("lg", [P, 2, TILES // 2, EXPERTS])
        rt = ps("rt", [P, 2, 4, P])
        s_w, s_lg, s_sig, s_v, s_tr, s_ev, s_hh = (sem("r_" + n) for n in ("w", "lg", "sig", "v", "tr", "ev", "hh"))
        block = ctx.enter_context(nc.Block())

        @block.sync
        def _(sp):
            sp.dma_start(gate[:, :], d["gateT"]).then_inc(s_w, 16)
            sp.dma_start(gbias[:, :], d["gbias"]).then_inc(s_w, 16)

        @block.tensor
        def _(pe):
            pe.wait_ge(s_w, 32)
            for t in range(TILES):
                mm = nc.tensor.matmul(lg[:, t // 8, t % 8, :], g.H[:, t * P:(t + 1) * P], gate[:, :], start=True, stop=True)
                if t % 8 == 7:
                    mm.then_inc(s_lg, 1)
            pe.wait_ge(s_v, ROUTE_STEPS)
            for q in range(TILES // 4):
                if q >= 2:
                    pe.wait_ge(s_ev, q - 1)
                for t in range(4):
                    mm = nc.tensor.transpose(rt[:, q % 2, t, :], SP[:, 4 * q + t, :, :], g.ident[:, :])
                mm.then_inc(s_tr, 1)

        @block.gpsimd
        def _(pool):
            for b in range(BLKS):
                cols = slice(b * BLK, (b + 1) * BLK)
                pool.wait_ge(s_hh, b + 1)
                nc.gpsimd.tensor_tensor(g.Hl[:, cols], g.H[:, cols], g.Hh[:, cols], ALU.subtract)

        @block.scalar
        def _(act):
            nc.scalar.preload_act_table(ACT.Sigmoid)
            for h in range(2):
                act.wait_ge(s_lg, h + 1)
                nc.scalar.activation(SC[:, 8 * h:8 * h + 8, :], lg[:, h, :, :], ACT.Sigmoid).then_inc(s_sig, 1)
            for b in range(BLKS):
                cols = slice(b * BLK, (b + 1) * BLK)
                nc.scalar.activation(g.Hh[:, cols], g.H[:, cols], ACT.Copy).then_inc(s_hh, 1)
            for q in range(TILES // 4):
                act.wait_ge(s_tr, q + 1)
                nc.scalar.activation(g.RT[:, q * BLK:(q + 1) * BLK].rearrange("p (t k) -> p t k", t=4),
                                     rt[:, q % 2, :, :], ACT.Copy).then_inc(s_ev, 1)

        @block.vector
        def _(dve):
            n = 0

            def step(ins, wait=True):
                nonlocal n
                ins.then_inc(s_v, 1)
                n += 1
                if wait:
                    dve.wait_ge(s_v, n)

            def grouped(t):
                return t[:, :, :].rearrange("p t (a b) -> p (t a) b", b=GSIZE)

            def per_group(t):
                return t[:, :, :].rearrange("p t a -> p (t a)")

            def over_group(t):
                return per_group(t).unsqueeze(2).broadcast_to([P, TILES * GROUPS, GSIZE])

            for k in range(8 - TOPG):
                step(nc.vector.memset(GA[:, :, GROUPS + k:GROUPS + k + 1], BIG * (k + 1)), wait=False)
            dve.wait_ge(s_w, 32)
            dve.wait_ge(s_sig, 2)
            step(nc.vector.tensor_tensor(SF[:, :, :], SC[:, :, :], gbias[:, :].unsqueeze(1).broadcast_to(shape), ALU.add))
            step(nc.vector.tensor_reduce(per_group(M1), grouped(SF), AX.X, ALU.max))
            step(nc.vector.tensor_tensor(grouped(EQ), grouped(SF), over_group(M1), ALU.is_equal))
            step(nc.vector.tensor_reduce(per_group(CNT), grouped(EQ), AX.X, ALU.add))
            step(nc.vector.scalar_tensor_tensor(out=LOW[:, :, :], in0=EQ[:, :, :], scalar=-BIG, in1=SF[:, :, :],
                                                op0=ALU.mult, op1=ALU.add))
            step(nc.vector.tensor_reduce(per_group(M2), grouped(LOW), AX.X, ALU.max))
            step(nc.vector.tensor_scalar(CNT[:, :, :], CNT[:, :, :], 2.0, -BIG, ALU.is_lt, ALU.mult))
            step(nc.vector.tensor_tensor(CNT[:, :, :], CNT[:, :, :], M1[:, :, :], ALU.add))
            step(nc.vector.tensor_tensor(M2[:, :, :], M2[:, :, :], CNT[:, :, :], ALU.max))
            step(nc.vector.tensor_tensor(GA[:, :, 0:GROUPS], M1[:, :, :], M2[:, :, :], ALU.add))
            for t in range(TILES):
                step(nc.vector.max(T8[:, t, :], GA[:, t, :]), wait=(t == TILES - 1))
            for t in range(TILES):
                step(nc.vector.match_replace(GR[:, t, :], T8[:, t, :], GA[:, t, :], -4 * BIG), wait=(t == TILES - 1))
            step(nc.vector.tensor_scalar(GM[:, :, :], GR[:, :, 0:GROUPS], -4 * BIG, None, ALU.is_equal))
            step(nc.vector.tensor_tensor(grouped(LOW), grouped(SF), over_group(GM), ALU.mult))
            step(nc.vector.tensor_scalar(LOW[:, :, :], LOW[:, :, :], 0.0, None, ALU.add))
            for t in range(TILES):
                step(nc.vector.max(T8[:, t, :], LOW[:, t, :]), wait=(t == TILES - 1))
            for t in range(TILES):
                step(nc.vector.match_replace(EQ[:, t, :], T8[:, t, :], LOW[:, t, :], -4 * BIG), wait=(t == TILES - 1))
            step(nc.vector.scalar_tensor_tensor(out=SF[:, :, :], in0=EQ[:, :, :], scalar=-4 * BIG, in1=SC[:, :, :],
                                                op0=ALU.is_equal, op1=ALU.mult))
            step(nc.vector.tensor_reduce(WS[:, :], SF[:, :, :], AX.X, ALU.add))
            step(nc.vector.tensor_scalar(WS[:, :], WS[:, :], 1e-20, None, ALU.add))
            step(nc.vector.reciprocal(WR[:, :], WS[:, :]))
            step(nc.vector.tensor_scalar(WR[:, :], WR[:, :], 2.5, None, ALU.mult))
            step(nc.vector.tensor_tensor(SF[:, :, :], SF[:, :, :], WR[:, :].unsqueeze(2).broadcast_to(shape), ALU.mult))
            step(nc.vector.tensor_copy(RH[:, :, :], SF[:, :, :]))
            step(nc.vector.tensor_copy(SP[:, :, 0, :], RH[:, :, :]), wait=False)
            step(nc.vector.tensor_tensor(SP[:, :, 1, :], SF[:, :, :], RH[:, :, :], ALU.subtract))
            assert n == ROUTE_STEPS, n


ROUTE_STEPS = 90


def stage_experts(nc, d, g):
    RING, TBS, LAG, AHEAD = 4, 2, 2, 2
    LOOPS, REST = CHUNKS // RING, CHUNKS % RING
    ALL = 2 * CHUNKS
    SHARED_UNITS = 2 * TBS
    with ExitStack() as ctx:
        sb, ps, sem = alloc(nc, ctx)
        W = sb("W", [P, RING, 4, P])
        WH = sb("WH", [P, RING, 4, P], F32R)
        WL = sb("WL", [P, RING, 3, P], F32R)
        zero = sb("zero", [P, BLK], BF16)
        SG, TT = (sb(n, [P, 2, BLK]) for n in ("SG", "TT"))
        HH = sb("HH", [P, 4, BLK])
        HHh, HHl = (sb(n, [P, 4, BLK], F32R) for n in ("HHh", "HHl"))
        g_ps, u_ps, rb_ps, acc = (ps(n, [P, 2, BLK]) for n in ("g_ps", "u_ps", "rb_ps", "acc"))
        s_ld = [sem(f"e_ld{k}") for k in range(RING)]
        s_z, s_wh, s_wl, s_g, s_u, s_rb, s_silu, s_t, s_hh, s_hi, s_lo, s_down, s_out = (
            sem("e_" + n) for n in ("z", "wh", "wl", "g", "u", "rb", "silu", "t", "hh", "hi", "lo", "down", "out"))

        def runs(eng, body):
            for half in range(2):
                n0 = half * CHUNKS

                def one(i, k):
                    body(half, i * RING + (n0 + k), (n0 + k) % RING, i + (n0 + k) // RING,
                         i * RING + k if isinstance(i, int) else None)
                for k in range(RING):
                    one(0, k)
                with eng.Fori(1, LOOPS) as i:
                    for k in range(RING):
                        one(i, k)
                for k in range(REST):
                    one(LOOPS, k)

        def cols(half, tb):
            return slice((half * TBS + tb) * BLK, (half * TBS + tb + 1) * BLK)

        def early(U, n):
            return isinstance(U, int) and U < n

        def shared(c):
            return c is not None and c >= CHUNKS - 2

        block = ctx.enter_context(nc.Block())

        @block.sync
        def _(sp):
            def body(half, n, k, uses, c):
                if not early(n, RING):
                    sp.wait_ge(s_wl, n - (RING - 1))
                sp.dma_start(W[:, k, :, :].rearrange("p a b -> p (a b)"),
                             d["w4"][bass.ds(n - half * CHUNKS, 1), :, :].rearrange("o p n -> (o p) n")).then_inc(s_ld[k], 16)
            runs(sp, body)

        @block.gpsimd
        def _(pool):
            def body(half, n, k, uses, c):
                pool.wait_ge(s_wh, n + 1)
                nc.gpsimd.tensor_tensor(WL[:, k, :, :], W[:, k, 0:3, :], WH[:, k, 0:3, :], ALU.subtract).then_inc(s_wl, 1)
            runs(pool, body)

        @block.tensor
        def _(pe):
            def three(out, k, w, hi, lo, start, stop):
                nc.tensor.matmul(out, WH[:, k, w, :], hi, start=start, stop=False, skip_group_check=True)
                nc.tensor.matmul(out, WH[:, k, w, :], lo, start=False, stop=False, skip_group_check=True)
                return nc.tensor.matmul(out, WL[:, k, w, :], hi, start=False, stop=stop, skip_group_check=True)

            def down(U, k, tb):
                j = (2 * k + tb) % 4
                pe.wait_ge(s_lo, U + 1)
                three(acc[:, tb, :], k, 2, HHh[:, j, :], HHl[:, j, :], False, False).then_inc(s_down, 1)

            def open_sums(half):
                if half == 0:
                    pe.wait_ge(s_z, 1)
                else:
                    pe.wait_ge(s_out, TBS)
                for tb in range(TBS):
                    nc.tensor.matmul(acc[:, tb, :], zero[:, 0:P], zero[:, :], start=True, stop=False, skip_group_check=True)

            def body(half, n, k, uses, c):
                for tb in range(TBS):
                    U = n * TBS + tb
                    if tb == 0:
                        pe.wait_ge(s_wh, n + 1)
                        pe.wait_ge(s_wl, n + 1)
                    hi, lo = g.Hh[:, cols(half, tb)], g.Hl[:, cols(half, tb)]
                    if not early(U, 2):
                        pe.wait_ge(s_silu, U - 1)
                    three(g_ps[:, tb, :], k, 0, hi, lo, True, True).then_inc(s_g, 1)
                    if not early(U, 2):
                        pe.wait_ge(s_t, U - 1)
                    three(u_ps[:, tb, :], k, 1, hi, lo, True, True).then_inc(s_u, 1)
                    if not shared(c):
                        if not early(U, 2):
                            pe.wait_ge(s_hh, U - 1)
                        nc.tensor.matmul(rb_ps[:, tb, :], WH[:, k, 3, :], g.RT[:, cols(half, tb)],
                                         start=True, stop=True).then_inc(s_rb, 1)
                    if c == 1 and tb == 0:
                        open_sums(half)
                    if not early(U, LAG):
                        down(U - LAG, (k - 1) % RING, tb)

            runs(pe, body)
            for tb in range(TBS):
                down((ALL - 1) * TBS + tb, (ALL - 1) % RING, tb)

        @block.scalar
        def _(act):
            nc.scalar.preload_act_table(ACT.Silu)

            def round_weights(n, k, uses):
                act.wait_ge(s_ld[k], (uses + 1) * 16)
                if not early(n, RING):
                    act.wait_ge(s_down, (n - (RING - 1)) * TBS)
                nc.scalar.activation(WH[:, k, :, :], W[:, k, :, :], ACT.Copy).then_inc(s_wh, 1)

            def high(U, j):
                act.wait_ge(s_hh, U + 1)
                if not early(U, 4):
                    act.wait_ge(s_down, U - 3)
                nc.scalar.activation(HHh[:, j, :], HH[:, j, :], ACT.Copy).then_inc(s_hi, 1)

            def take_sums(half):
                act.wait_ge(s_down, (half + 1) * CHUNKS * TBS)
                for tb in range(TBS):
                    nc.scalar.activation(g.Y[:, cols(half, tb)], acc[:, tb, :], ACT.Copy).then_inc(s_out, 1)

            def body(half, n, k, uses, c):
                for tb in range(TBS):
                    U, j = n * TBS + tb, (2 * k + tb) % 4
                    act.wait_ge(s_g, U + 1)
                    if not early(U, 2):
                        act.wait_ge(s_t, U - 1)
                    nc.scalar.activation(SG[:, tb, :], g_ps[:, tb, :], ACT.Silu).then_inc(s_silu, 1)
                    if not early(U, 1):
                        high(U - 1, (j - 1) % 4)
                    if tb == 0 and not (isinstance(n, int) and n >= ALL - AHEAD):
                        round_weights(n + AHEAD, (k + AHEAD) % RING, uses + (k + AHEAD) // RING)
                    if tb == 0 and c == 1 and half == 1:
                        take_sums(0)

            for n in range(AHEAD):
                round_weights(n, n, 0)
            runs(act, body)
            high(ALL * TBS - 1, 3)
            take_sums(1)

        @block.vector
        def _(dve):
            nc.vector.memset(zero[:, :], 0.0).then_inc(s_z, 1)

            def low(U, j):
                dve.wait_ge(s_hi, U + 1)
                if not early(U, 4):
                    dve.wait_ge(s_down, U - 3)
                nc.vector.tensor_tensor(HHl[:, j, :], HH[:, j, :], HHh[:, j, :], ALU.subtract).then_inc(s_lo, 1)

            def body(half, n, k, uses, c):
                for tb in range(TBS):
                    U, j = n * TBS + tb, (2 * k + tb) % 4
                    dve.wait_ge(s_silu, U + 1)
                    dve.wait_ge(s_u, U + 1)
                    nc.vector.tensor_tensor(TT[:, tb, :], SG[:, tb, :], u_ps[:, tb, :], ALU.mult).then_inc(s_t, 1)
                    if not early(U, 1):
                        low(U - 1, (j - 1) % 4)
                    dve.wait_ge(s_t, U + 1)
                    if shared(c):
                        nc.vector.tensor_copy(HH[:, j, :], TT[:, tb, :]).then_inc(s_hh, 1)
                    else:
                        dve.wait_ge(s_rb, U + 1 - half * SHARED_UNITS)
                        nc.vector.tensor_tensor(HH[:, j, :], TT[:, tb, :], rb_ps[:, tb, :], ALU.mult).then_inc(s_hh, 1)

            runs(dve, body)
            low(ALL * TBS - 1, 3)


def stage_moe(nc, d, g):
    with ExitStack() as ctx:
        sb, _, _ = alloc(nc, ctx)
        g.RT = sb("RT", [P, TOK], F32R)
        g.Hh, g.Hl = sb("Hh", [P, TOK], F32R), sb("Hl", [P, TOK], F32R)
        stage_route(nc, d, g)
        stage_experts(nc, d, g)


W2 = SEQ + CONVPAD
DIRS = 2


def stage_mamba_project(nc, d, g, m):
    with ExitStack() as ctx:
        sb, ps, sem = alloc(nc, ctx)
        U2 = sb("U2", [P, DIRS, BATCH, W2])
        wx = sb("wx", [P, DIRS, 3 * P])
        cw = sb("cw", [P, DIRS, 2, 3 * P])
        wc = sb("wc", [P, DIRS, 2, 3 * P])
        wz = sb("wz", [P, DIRS, P])
        wdt = sb("wdt", [P, 4])
        cb = sb("cb", [P, DIRS, 3])
        dtb, al = sb("dtb", [P, 4]), sb("al", [P, 4])
        A = sb("A", [P, 4])
        shape = [P, TILES, 4]
        VV, NV, E, W1, DD, IZ, LN = (sb(n, shape) for n in ("VV", "NV", "E", "W1", "DD", "IZ", "LN"))
        job_ps = ps("job_ps", [P, 4, BLK])
        dt_ps = ps("dt_ps", shape)
        sum_ps = ps("sum_ps", [P, 3, 4, TILES])
        s_w, s_u2, s_pad, s_wc, s_dt, s_v, s_act, s_job, s_ev, s_sum = (
            sem("p_" + n) for n in ("w", "u2", "pad", "wc", "dt", "v", "act", "job", "ev", "sum"))
        JOBS = 4 * DIRS
        SHIFT = (3, 0)
        FAR = (-2, 2)
        block = ctx.enter_context(nc.Block())

        def blocks(eng, body):
            with eng.Fori(0, BATCH) as b:
                with eng.Fori(0, SEQ // BLK) as h:
                    for j in range(JOBS):
                        body(b, h, j, (b * (SEQ // BLK) + h) * JOBS + j)

        @block.sync
        def _(sp):
            for dst, src in ((wx[:, :, :], d["wxbc"]), (cw[:, :, :, :], d["cw"]), (wz[:, :, :], d["wz"]), (wdt[:, :], d["wdt"]),
                             (cb[:, :, :], d["cb"]), (dtb[:, :], d["dtb"]), (al[:, :], d["alog"]), (m.tri[:, :, :], d["tri"])):
                sp.dma_start(dst, src).then_inc(s_w, 16)
            for b in range(BATCH):
                t0 = b * SEQ
                for dst, src in ((U2[0:HD, 0, b, 3:3 + SEQ], g.U[0:HD, t0:t0 + SEQ]),
                                 (U2[HD:P, 0, b, 4:3 + SEQ], g.U[0:HD, t0:t0 + SEQ - 1]),
                                 (U2[0:HD, 1, b, 0:SEQ], g.U[HD:P, t0:t0 + SEQ]),
                                 (U2[HD:P, 1, b, 0:SEQ - 1], g.U[HD:P, t0 + 1:t0 + SEQ])):
                    sp.dma_start(dst, src).then_inc(s_u2, 16)

        @block.gpsimd
        def _(pool):
            nc.gpsimd.memset(U2[0:HD, 0, :, 0:3], 0.0).then_inc(s_pad, 1)
            nc.gpsimd.memset(U2[HD:P, 0, :, 0:4], 0.0).then_inc(s_pad, 1)
            nc.gpsimd.memset(U2[0:HD, 1, :, SEQ:W2], 0.0).then_inc(s_pad, 1)
            nc.gpsimd.memset(U2[HD:P, 1, :, SEQ - 1:W2], 0.0).then_inc(s_pad, 1)

        @block.tensor
        def _(pe):
            pe.wait_ge(s_w, 128)
            for t in range(TILES):
                mm = nc.tensor.matmul(dt_ps[:, t, :], g.U[:, t * P:(t + 1) * P], wdt[:, :], start=True, stop=True)
            mm.then_inc(s_dt, 1)
            pe.wait_ge(s_pad, 4)
            pe.wait_ge(s_u2, 128)
            pe.wait_ge(s_wc, 1)

            def job(b, h, j, J):
                dr, c = j // 4, j % 4
                pe.wait_ge(s_ev, J + 1)
                base = dr * BATCH * W2 + SHIFT[dr]
                flat = U2[:, :, :, :].rearrange("p a b c -> p (a b c)")
                if c < 3:
                    for q in range(2):
                        mm = nc.tensor.matmul(job_ps[:, j % 4, :], wc[:, dr, q, c * P:(c + 1) * P],
                                              flat[:, bass.ds(b * W2 + h * BLK + (base + q * FAR[dr]), BLK)],
                                              start=(q == 0), stop=(q == 1))
                else:
                    mm = nc.tensor.matmul(job_ps[:, j % 4, :], wz[:, dr, :],
                                          flat[:, bass.ds(b * W2 + h * BLK + base, BLK)], start=True, stop=True)
                mm.then_inc(s_job, 1)

            blocks(pe, job)
            pe.wait_ge(s_v, PROJECT_STEPS)
            for k in range(2):
                for dr in range(DIRS):
                    nc.tensor.matmul(sum_ps[:, k, 2 * dr:2 * dr + 2, :], m.tri[:, 2 * dr + k, :],
                                     m.AA[:, :, 2 * dr:2 * dr + 2].rearrange("p t h -> p h t"), start=True, stop=True)
            nc.tensor.matmul(sum_ps[:, 2, :, :], g.ones[:, :], m.AA[:, :, :].rearrange("p t h -> p h t"),
                             start=True, stop=True).then_inc(s_sum, 1)

        @block.scalar
        def _(act):
            act.sem_inc(s_ev, 4)
            act.wait_ge(s_w, 128)
            nc.scalar.activation(A[:, :], al[:, :], ACT.Exp).then_inc(s_act, 1)
            act.wait_ge(s_v, 3)
            nc.scalar.activation(E[:, :, :], NV[:, :, :], ACT.Exp).then_inc(s_act, 1)
            act.wait_ge(s_v, 4)
            nc.scalar.activation(LN[:, :, :], W1[:, :, :], ACT.Ln).then_inc(s_act, 1)
            nc.scalar.preload_act_table(ACT.Silu)

            def job(b, h, j, J):
                dr, c = j // 4, j % 4
                act.wait_ge(s_job, J + 1)
                at = bass.ds(b * SEQ + h * BLK, BLK)
                if c < 3:
                    nc.scalar.activation(m.XBC[:, dr, c, at], job_ps[:, j % 4, :], ACT.Silu, bias=cb[:, dr, c:c + 1]).then_inc(s_ev, 1)
                else:
                    nc.scalar.activation(m.SZ[:, dr, at], job_ps[:, j % 4, :], ACT.Silu).then_inc(s_ev, 1)

            blocks(act, job)
            act.wait_ge(s_sum, 1)
            nc.scalar.activation(m.EX[:, :, :, :], sum_ps[:, :, :, :], ACT.Exp).then_inc(s_act, 1)

        @block.vector
        def _(dve):
            n = 0

            def step(ins):
                nonlocal n
                ins.then_inc(s_v, 1)
                n += 1
                dve.wait_ge(s_v, n)

            dve.wait_ge(s_w, 128)
            for dr in range(DIRS):
                mm = nc.vector.tensor_tensor(wc[:, dr, :, :], cw[:, dr, :, :],
                                             wx[:, dr, :].unsqueeze(1).broadcast_to([P, 2, 3 * P]), ALU.mult)
            mm.then_inc(s_wc, 1)
            dve.wait_ge(s_dt, 1)
            step(nc.vector.tensor_tensor(VV[:, :, :], dt_ps[:, :, :], dtb[:, :].unsqueeze(1).broadcast_to(shape), ALU.add))
            step(nc.vector.tensor_scalar(NV[:, :, :], VV[:, :, :], -1.0, None, ALU.mult))
            step(nc.vector.tensor_tensor(NV[:, :, :], NV[:, :, :], VV[:, :, :], ALU.min))
            dve.wait_ge(s_act, 2)
            step(nc.vector.tensor_scalar(W1[:, :, :], E[:, :, :], 1.0, None, ALU.add))
            step(nc.vector.tensor_scalar(DD[:, :, :], W1[:, :, :], -1.0, None, ALU.add))
            step(nc.vector.tensor_scalar(IZ[:, :, :], DD[:, :, :], 0.0, None, ALU.is_equal))
            step(nc.vector.tensor_tensor(DD[:, :, :], DD[:, :, :], IZ[:, :, :], ALU.add))
            step(nc.vector.reciprocal(DD[:, :, :], DD[:, :, :]))
            dve.wait_ge(s_act, 3)
            step(nc.vector.tensor_tensor(LN[:, :, :], LN[:, :, :], IZ[:, :, :], ALU.add))
            step(nc.vector.tensor_tensor(LN[:, :, :], LN[:, :, :], E[:, :, :], ALU.mult))
            step(nc.vector.tensor_tensor(LN[:, :, :], LN[:, :, :], DD[:, :, :], ALU.mult))
            step(nc.vector.scalar_tensor_tensor(out=m.DT[:, :, :], in0=VV[:, :, :], scalar=0.0, in1=LN[:, :, :],
                                                op0=ALU.max, op1=ALU.add))
            step(nc.vector.scalar_tensor_tensor(out=m.AA[:, :, :], in0=m.DT[:, :, :], scalar=-1.0,
                                                in1=A[:, :].unsqueeze(1).broadcast_to(shape), op0=ALU.mult, op1=ALU.mult))
            assert n == PROJECT_STEPS


PROJECT_STEPS = 13


def stage_mamba_scan(nc, g, m):
    SEQS, STEPS = DIRS * BATCH, SEQ // P
    with ExitStack() as ctx:
        sb, ps, sem = alloc(nc, ctx)
        CP = sb("CP", [P, 2, 3, P])
        AR = sb("AR", [P, 2, 2, P])
        ED = sb("ED", [P, 2, 2, P])
        BT = sb("BT", [P, 2, P])
        GM = sb("GMt", [P, 2, P])
        MT = sb("MT", [P, 2, 2, P])
        DX, DS = sb("DX", [P, 2, 2, HD]), sb("DS", [P, 2, 2, HD])
        YT = sb("YT", [P, 2, 2, HD])
        HST, HD1 = sb("HST", [P, SEQS, 2, HD]), sb("HD1", [P, 2, 2, HD])
        t_ps = ps("t_ps", [P, 2, 4, P])
        d_ps = ps("dd_ps", [P, 2, 4, P])
        y_ps = ps("y_ps", [P, 2, 4, P])
        yt_ps = ps("yt_ps", [P, 2, 4, P])
        (s_z, s_cp, s_ar, s_t, s_d, s_ed, s_bt, s_gm, s_dx, s_ds, s_mt, s_y, s_y1, s_y2, s_h1, s_h2, s_yt, s_yev) = (
            sem("s_" + n) for n in ("z", "cp", "ar", "t", "d", "ed", "bt", "gm", "dx", "ds", "mt", "y", "y1", "y2", "h1",
                                    "h2", "yt", "yev"))
        block = ctx.enter_context(nc.Block())

        def early(U, n=2):
            return isinstance(U, int) and U < n

        def tile(i, q):
            dr, b = q // BATCH, q % BATCH
            return i + b * STEPS if dr == 0 else i * -1 + (b * STEPS + STEPS - 1)

        def at(i, q, n=P):
            return bass.ds(tile(i, q) * n, n)

        def units(eng, body, tail):
            def step(i):
                for q in range(SEQS):
                    body(i, q, i * SEQS + q)
            step(0)
            with eng.Fori(1, STEPS) as i:
                step(i)
            tail()

        def back(i, q, n):
            return (i, q - n) if q >= n else (i - 1, q - n + SEQS)

        def heads(i, q, kind):
            dr = q // BATCH
            return m.EX[:, kind, 2 * dr:2 * dr + 2, bass.ds(tile(i, q), 1)].broadcast_to([P, 2, HD])

        LAST = (STEPS - 1, SEQS - 1)

        @block.scalar
        def _(act):
            nc.scalar.preload_act_table(ACT.Exp)

            def body(i, q, U):
                dr = q // BATCH
                if not early(U):
                    act.wait_ge(s_y, U - 1)
                nc.scalar.activation(CP[:, q % 2, :, :], m.XBC[:, dr, :, at(i, q)], ACT.Copy).then_inc(s_cp, 1)
                act.wait_ge(s_d, U + 1)
                if not early(U):
                    act.wait_ge(s_mt, U - 1)
                nc.scalar.activation(ED[:, q % 2, :, :], d_ps[:, q % 2, 0:2, :], ACT.Exp).then_inc(s_ed, 1)
                nc.scalar.activation(BT[:, q % 2, :], d_ps[:, q % 2, 2, :], ACT.Copy).then_inc(s_bt, 1)
                if not early(U):
                    take_y(*back(i, q, 2), U - 2)

            def take_y(i, q, U):
                act.wait_ge(s_yt, U + 1)
                nc.scalar.activation(m.YB[:, q // BATCH, at(i, q)], yt_ps[:, q % 2, 0, :], ACT.Copy).then_inc(s_yev, 1)

            def tail():
                for n in (1, 0):
                    i, q = back(*LAST, n)
                    take_y(i, q, i * SEQS + q)

            units(act, body, tail)

        @block.gpsimd
        def _(pool):
            def body(i, q, U):
                dr = q // BATCH
                if not early(U):
                    pool.wait_ge(s_d, U - 1)
                shape = [P, 2, P]
                nc.gpsimd.tensor_tensor(AR[:, q % 2, :, :], m.tri[:, 2 * dr, :].unsqueeze(1).broadcast_to(shape),
                                        m.AA[:, bass.ds(tile(i, q), 1), 2 * dr:2 * dr + 2].rearrange("p o h -> p h o")
                                        .broadcast_to(shape), ALU.mult).then_inc(s_ar, 1)
            units(pool, body, lambda: None)

        @block.tensor
        def _(pe):
            def phase1(i, q, U):
                dr, k = q // BATCH, q % 2
                pe.wait_ge(s_cp, U + 1)
                if not early(U):
                    pe.wait_ge(s_dx, U - 1)
                nc.tensor.transpose(t_ps[:, k, 0, :], CP[:, k, 0, :], g.ident[:, :])
                nc.tensor.matmul(t_ps[:, k, 1, :], CP[:, k, 1, :], CP[:, k, 2, :], start=True, stop=True).then_inc(s_t, 1)
                pe.wait_ge(s_ar, U + 1)
                if not early(U):
                    pe.wait_ge(s_bt, U - 1)
                nc.tensor.matmul(d_ps[:, k, 0:2, :], m.tri[:, 2 * dr + 1, :], AR[:, k, :, :], start=True, stop=True)
                nc.tensor.transpose(d_ps[:, k, 2, :], CP[:, k, 1, :], g.ident[:, :]).then_inc(s_d, 1)

            def phase2(i, q, U):
                k = q % 2
                pe.wait_ge(s_mt, U + 1)
                pe.wait_ge(s_ds, U + 1)
                pe.wait_ge(s_bt, U + 1)
                if early(U, SEQS):
                    pe.wait_ge(s_z, 1)
                if not early(U):
                    pe.wait_ge(s_h2, U - 1)
                for h in range(2):
                    nc.tensor.matmul(y_ps[:, k, 0, h * HD:(h + 1) * HD], MT[:, k, h, :], DX[:, k, h, :], start=True, stop=True)
                nc.tensor.matmul(y_ps[:, k, 1, :], CP[:, k, 2, :], HST[:, q, :, :], start=True, stop=True)
                nc.tensor.matmul(y_ps[:, k, 2, :], BT[:, k, :], DS[:, k, :, :], start=True, stop=True).then_inc(s_y, 1)

            def turn(i, q, U):
                k = q % 2
                pe.wait_ge(s_y2, U + 1)
                if not early(U):
                    pe.wait_ge(s_yev, U - 1)
                nc.tensor.transpose(yt_ps[:, k, 0, :], YT[:, k, :, :], g.ident[:, :]).then_inc(s_yt, 1)

            def body(i, q, U):
                phase1(i, q, U)
                if not early(U, 1):
                    phase2(*back(i, q, 1), U - 1)
                if not early(U):
                    turn(*back(i, q, 2), U - 2)

            def tail():
                i, q = LAST
                U = i * SEQS + q
                phase2(i, q, U)
                turn(*back(i, q, 1), U - 1)
                turn(i, q, U)

            units(pe, body, tail)

        @block.vector
        def _(dve):
            nc.vector.memset(HST[:, :, :, :], 0.0).then_inc(s_z, 1)

            def body(i, q, U):
                dr, k = q // BATCH, q % 2
                dve.wait_ge(s_t, U + 1)
                nc.vector.tensor_tensor(GM[:, k, :], t_ps[:, k, 1, :], m.tri[:, 2 * dr, :], ALU.mult).then_inc(s_gm, 1)
                if not early(U):
                    dve.wait_ge(s_y, U - 1)
                nc.vector.tensor_tensor(DX[:, k, :, :], t_ps[:, k, 0, :].rearrange("p (h c) -> p h c", h=2),
                                        m.DT[:, bass.ds(tile(i, q), 1), 2 * dr:2 * dr + 2].rearrange("p o h -> p h o")
                                        .broadcast_to([P, 2, HD]), ALU.mult).then_inc(s_dx, 1)
                dve.wait_ge(s_dx, U + 1)
                nc.vector.tensor_tensor(DS[:, k, :, :], DX[:, k, :, :], heads(i, q, 1), ALU.mult).then_inc(s_ds, 1)
                dve.wait_ge(s_ed, U + 1)
                dve.wait_ge(s_gm, U + 1)
                nc.vector.tensor_tensor(MT[:, k, :, :], ED[:, k, :, :], GM[:, k, :].unsqueeze(1).broadcast_to([P, 2, P]),
                                        ALU.mult).then_inc(s_mt, 1)
                if not early(U, 1):
                    result(*back(i, q, 1), U - 1)

            def result(i, q, U):
                k = q % 2
                dve.wait_ge(s_y, U + 1)
                if not early(U):
                    dve.wait_ge(s_yt, U - 1)
                two = lambda n: y_ps[:, k, n, :].rearrange("p (h c) -> p h c", h=2)
                nc.vector.tensor_tensor(YT[:, k, :, :], two(1), heads(i, q, 0), ALU.mult).then_inc(s_y1, 1)
                nc.vector.tensor_tensor(HD1[:, k, :, :], HST[:, q, :, :], heads(i, q, 2), ALU.mult).then_inc(s_h1, 1)
                dve.wait_ge(s_y1, U + 1)
                nc.vector.tensor_tensor(YT[:, k, :, :], two(0), YT[:, k, :, :], ALU.add).then_inc(s_y2, 1)
                dve.wait_ge(s_h1, U + 1)
                nc.vector.tensor_tensor(HST[:, q, :, :], two(2), HD1[:, k, :, :], ALU.add).then_inc(s_h2, 1)

            def tail():
                result(*LAST, STEPS * SEQS - 1)

            units(dve, body, tail)


def stage_mamba_output(nc, d, g, m):
    with ExitStack() as ctx:
        sb, ps, sem = alloc(nc, ctx)
        wp = sb("wp", [P, DIRS, HD])
        op = sb("op", [P, P])
        YG = sb("YG", [P, DIRS, TOK])
        SQ = sb("oSQ", [P, 2, BLK])
        ST, R = sb("oST", [P, 2, 4]), sb("oR", [P, 2, 4])
        DG = sb("oDG", [P, 2, 4, P])
        CAT = sb("CAT", [P, 2, BLK])
        eps = sb("oeps", [P, 1])
        ms_ps, r_ps = ps("oms", [P, 2, BLK]), ps("or", [P, 2, BLK])
        cat_ps, o_ps = ps("cat_ps", [P, 2, BLK]), ps("oo_ps", [P, 2, BLK])
        s_w, s_e, s_g1, s_g2, s_sq, s_ms, s_st, s_r, s_dg, s_b, s_yn, s_cat, s_cc, s_o, s_out = (
            sem("o_" + n) for n in ("w", "e", "g1", "g2", "sq", "ms", "st", "r", "dg", "b", "yn", "cat", "cc", "o", "out"))
        ITEMS = DIRS * BLKS
        GN, DS = (g.vec["gn_f"], g.vec["gn_b"]), (g.vec["D_f"], g.vec["D_b"])

        def cols(n):
            return slice((n // 2) * BLK, (n // 2 + 1) * BLK)
        block = ctx.enter_context(nc.Block())

        @block.sync
        def _(sp):
            sp.dma_start(wp[:, :, :], d["wp"]).then_inc(s_w, 16)
            sp.dma_start(op[:, :], d["opT"]).then_inc(s_w, 16)

        @block.tensor
        def _(pe):
            pe.wait_ge(s_w, 32)
            for n in range(ITEMS + 2):
                if n < ITEMS:
                    pe.wait_ge(s_sq, n + 1)
                    if n >= 2:
                        pe.wait_ge(s_st, n - 1)
                    for t in range(4):
                        mm = nc.tensor.matmul(ms_ps[:, n % 2, t:t + 1], SQ[:, n % 2, t * P:(t + 1) * P], g.mean_col[:, :],
                                              start=True, stop=True)
                    mm.then_inc(s_ms, 1)
                if 1 <= n <= ITEMS:
                    k = n - 1
                    pe.wait_ge(s_dg, k + 1)
                    if k >= 2:
                        pe.wait_ge(s_yn, k - 1)
                    nc.tensor.matmul(r_ps[:, k % 2, :], g.ones[:, :], DG[:, k % 2, :, :], start=True, stop=True).then_inc(s_b, 1)
                if n >= 2:
                    k = n - 2
                    blk, dr = k // 2, k % 2
                    pe.wait_ge(s_yn, k + 1)
                    if blk >= 2:
                        pe.wait_ge(s_cc, blk - 1)
                    nc.tensor.matmul(cat_ps[dr * HD:(dr + 1) * HD, blk % 2, :], wp[:, dr, :], YG[:, dr, cols(k)],
                                     start=True, stop=True).then_inc(s_cat, 1)
                    if dr == 1:
                        pe.wait_ge(s_cc, blk + 1)
                        if blk >= 2:
                            pe.wait_ge(s_out, blk - 1)
                        nc.tensor.matmul(o_ps[:, blk % 2, :], op[:, :], CAT[:, blk % 2, :], start=True, stop=True).then_inc(s_o, 1)

        @block.scalar
        def _(act):
            nc.scalar.preload_act_table(ACT.Sqrt)
            act.wait_ge(s_e, 1)
            for n in range(ITEMS + 2):
                if n < ITEMS:
                    act.wait_ge(s_g2, n + 1)
                    if n >= 2:
                        act.wait_ge(s_ms, n - 1)
                    nc.scalar.activation(SQ[:, n % 2, :], YG[:, n % 2, cols(n)], ACT.Square).then_inc(s_sq, 1)
                    act.wait_ge(s_ms, n + 1)
                    if n >= 2:
                        act.wait_ge(s_r, n - 1)
                    nc.scalar.activation(ST[:, n % 2, :], ms_ps[:, n % 2, 0:4], ACT.Sqrt, bias=eps[:, :]).then_inc(s_st, 1)
                if n >= 2 and n % 2:
                    blk = (n - 2) // 2
                    act.wait_ge(s_cat, 2 * blk + 2)
                    if blk >= 2:
                        act.wait_ge(s_o, blk - 1)
                    nc.scalar.activation(CAT[:, blk % 2, :], cat_ps[:, blk % 2, :], ACT.Copy).then_inc(s_cc, 1)

        @block.vector
        def _(dve):
            nc.vector.memset(eps[:, :], 1e-5).then_inc(s_e, 1)
            for n in range(ITEMS + 3):
                if n < ITEMS:
                    dr = n % 2
                    nc.vector.scalar_tensor_tensor(out=YG[:, dr, cols(n)], in0=m.XBC[:, dr, 0, cols(n)], scalar=DS[dr],
                                                   in1=m.YB[:, dr, cols(n)], op0=ALU.mult, op1=ALU.add).then_inc(s_g1, 1)
                    dve.wait_ge(s_g1, n + 1)
                    nc.vector.tensor_tensor(YG[:, dr, cols(n)], YG[:, dr, cols(n)], m.SZ[:, dr, cols(n)], ALU.mult).then_inc(s_g2, 1)
                if 1 <= n <= ITEMS:
                    k = n - 1
                    dve.wait_ge(s_st, k + 1)
                    nc.vector.reciprocal(R[:, k % 2, :], ST[:, k % 2, :]).then_inc(s_r, 1)
                    dve.wait_ge(s_r, k + 1)
                    if k >= 2:
                        dve.wait_ge(s_b, k - 1)
                    nc.vector.tensor_tensor(DG[:, k % 2, :, :], g.ident[:, :].unsqueeze(1).broadcast_to([P, 4, P]),
                                            R[:, k % 2, :].unsqueeze(2).broadcast_to([P, 4, P]), ALU.mult).then_inc(s_dg, 1)
                    dve.wait_ge(s_b, k + 1)
                    dve.wait_ge(s_g2, k + 1)
                    y = YG[:, k % 2, cols(k)]
                    nc.vector.scalar_tensor_tensor(out=y, in0=y, scalar=GN[k % 2], in1=r_ps[:, k % 2, :],
                                                   op0=ALU.mult, op1=ALU.mult).then_inc(s_yn, 1)
                if n >= 4 and n % 2 == 0:
                    blk = (n - 4) // 2
                    dve.wait_ge(s_o, blk + 1)
                    at = slice(blk * BLK, (blk + 1) * BLK)
                    nc.vector.scalar_tensor_tensor(out=g.Y[:, at], in0=o_ps[:, blk % 2, :], scalar=g.vec["op_b"],
                                                   in1=g.H[:, at], op0=ALU.add, op1=ALU.add).then_inc(s_out, 1)


def stage_mamba(nc, d, g):
    with ExitStack() as ctx:
        sb, _, _ = alloc(nc, ctx)
        m = Shared()
        m.XBC, m.SZ = sb("XBC", [P, DIRS, 3, TOK]), sb("SZ", [P, DIRS, TOK])
        m.DT, m.AA, m.EX = sb("DT", [P, TILES, 4]), sb("AA", [P, TILES, 4]), sb("EX", [P, 3, 4, TILES])
        m.tri = sb("tri", [P, 4, P])
        stage_mamba_project(nc, d, g, m)
        with ExitStack() as inner:
            m.YB = inner.enter_context(nc.sbuf_tensor("YB", [P, DIRS, TOK], F32))
            stage_mamba_scan(nc, g, m)
            stage_mamba_output(nc, d, g, m)


def stage_ffn(nc, d, g, out):
    CH = HID1 // P
    with ExitStack() as ctx:
        sb, ps, sem = alloc(nc, ctx)
        wr, br = sb("wr", [P, BLOCKS16]), sb("br", [P, BLOCKS16])
        w1, b1, w2 = sb("w1", [P, HID1]), sb("b1", [P, CH]), sb("w2", [P, CH, P])
        sel, identb = sb("fsel", [BLOCKS16, HID1], BF16), sb("fidentb", [P, P], BF16)
        shape = [P, TILES, BLOCKS16]
        V, MX, SM, RC = sb("fV", shape), sb("fMX", [P, TILES]), sb("fSM", [P, TILES]), sb("fRC", [P, TILES])
        PA, PR = sb("PA", [P, TILES, BLOCKS16 + FTOP]), sb("fPR", [P, TILES, BLOCKS16 + FTOP])
        T8, MK = sb("fT8", [P, TILES, 8]), sb("MK", shape, BF16)
        MKT = sb("MKT", [BLOCKS16, TOK], BF16)
        HR = sb("HR", [P, CH, TOK])
        lg = ps("flg", [P, 512])
        mt_ps = ps("mt_ps", [BLOCKS16, 8, P], BF16)
        h_ps, mb_ps, y_ps = ps("fh", [P, 2, BLK]), ps("fmb", [P, 2, BLK]), ps("fy", [P, 2, BLK])
        s_w, s_lg, s_v, s_exp, s_mt, s_mev, s_h, s_hr, s_mb, s_hm, s_y, s_yb, s_x, s_out = (
            sem("f_" + n) for n in ("w", "lg", "v", "exp", "mt", "mev", "h", "hr", "mb", "hm", "y", "yb", "x", "out"))
        JOBS = BLKS * CH

        def cols(b):
            return slice(b * BLK, (b + 1) * BLK)
        block = ctx.enter_context(nc.Block())

        @block.sync
        def _(sp):
            for dst, src in ((wr[:, :], d["wr"]), (br[:, :], d["br"]), (w1[:, :], d["w1T"]), (b1[:, :], d["b1"]), (w2[:, :, :], d["w2T"]),
                             (sel[:, :], d["self"]), (identb[:, :], d["identb"])):
                sp.dma_start(dst, src).then_inc(s_w, 16)
            for b in range(BLKS):
                sp.wait_ge(s_x, b + 1)
                sp.dma_start(out[:, cols(b)], g.X[:, cols(b)]).then_inc(s_out, 16)
            sp.wait_ge(s_out, 16 * BLKS)

        @block.tensor
        def _(pe):
            pe.wait_ge(s_w, 112)
            for t in range(TILES):
                mm = nc.tensor.matmul(lg[:, t * BLOCKS16:(t + 1) * BLOCKS16], g.H[:, t * P:(t + 1) * P], wr[:, :],
                                      start=True, stop=True)
            mm.then_inc(s_lg, 1)
            for J in range(JOBS):
                if J >= 2:
                    pe.wait_ge(s_hr, J - 1)
                nc.tensor.matmul(h_ps[:, J % 2, :], w1[:, (J % CH) * P:(J % CH + 1) * P], g.H[:, cols(J // CH)],
                                 start=True, stop=True).then_inc(s_h, 1)
            pe.wait_ge(s_v, FFN_STEPS)
            for half in range(2):
                if half:
                    pe.wait_ge(s_mev, 1)
                for t in range(8):
                    mm = nc.tensor.transpose(mt_ps[:, t, :], MK[:, 8 * half + t, :], identb[:, :])
                mm.then_inc(s_mt, 1)
            for J in range(JOBS + 1):
                if J < JOBS:
                    pe.wait_ge(s_mev, J // (JOBS // 2) + 1)
                    if J >= 2:
                        pe.wait_ge(s_hm, J - 1)
                    nc.tensor.matmul(mb_ps[:, J % 2, :], sel[:, (J % CH) * P:(J % CH + 1) * P], MKT[:, cols(J // CH)],
                                     start=True, stop=True).then_inc(s_mb, 1)
                if J >= 1:
                    K = J - 1
                    b, c = K // CH, K % CH
                    pe.wait_ge(s_hm, K + 1)
                    if b >= 2 and c == 0:
                        pe.wait_ge(s_yb, b - 1)
                    mm = nc.tensor.matmul(y_ps[:, b % 2, :], w2[:, c, :], HR[:, c, cols(b)], start=(c == 0), stop=(c == CH - 1))
                    if c == CH - 1:
                        mm.then_inc(s_y, 1)

        @block.scalar
        def _(act):
            nc.scalar.preload_act_table(ACT.Exp)
            act.wait_ge(s_w, 112)
            for J in range(JOBS):
                if J == 4:
                    act.wait_ge(s_v, 4)
                    nc.scalar.activation(V[:, :, :], V[:, :, :], ACT.Exp).then_inc(s_exp, 1)
                act.wait_ge(s_h, J + 1)
                nc.scalar.activation(HR[:, J % CH, cols(J // CH)], h_ps[:, J % 2, :], ACT.Relu,
                                     bias=b1[:, J % CH:J % CH + 1]).then_inc(s_hr, 1)
            for half in range(2):
                act.wait_ge(s_mt, half + 1)
                nc.scalar.activation(MKT[:, half * SEQ:(half + 1) * SEQ].rearrange("e (t k) -> e t k", t=8),
                                     mt_ps[:, :, :], ACT.Copy).then_inc(s_mev, 1)
            for b in range(BLKS):
                act.wait_ge(s_y, b + 1)
                nc.scalar.activation(g.Y[:, cols(b)], y_ps[:, b % 2, :], ACT.Identity, bias=g.vec["b2"]).then_inc(s_yb, 1)

        @block.vector
        def _(dve):
            n = 0

            def step(ins, wait=True):
                nonlocal n
                ins.then_inc(s_v, 1)
                n += 1
                if wait:
                    dve.wait_ge(s_v, n)

            over = lambda t: t[:, :].unsqueeze(2).broadcast_to(shape)
            dve.wait_ge(s_lg, 1)
            step(nc.vector.tensor_tensor(V[:, :, :], lg[:, 0:TILES * BLOCKS16].rearrange("p (t e) -> p t e", t=TILES),
                                         br[:, :].unsqueeze(1).broadcast_to(shape), ALU.add))
            step(nc.vector.tensor_reduce(MX[:, :], V[:, :, :], AX.X, ALU.max))
            step(nc.vector.tensor_tensor(V[:, :, :], V[:, :, :], over(MX), ALU.subtract))
            step(nc.vector.memset(PA[:, :, BLOCKS16:BLOCKS16 + 1], 2.0))
            for k in range(1, FTOP):
                step(nc.vector.memset(PA[:, :, BLOCKS16 + k:BLOCKS16 + k + 1], 2.0 + k))
            dve.wait_ge(s_exp, 1)
            step(nc.vector.tensor_reduce(SM[:, :], V[:, :, :], AX.X, ALU.add))
            step(nc.vector.reciprocal(RC[:, :], SM[:, :]))
            step(nc.vector.tensor_tensor(PA[:, :, 0:BLOCKS16], V[:, :, :], over(RC), ALU.mult))
            for t in range(TILES):
                step(nc.vector.max(T8[:, t, :], PA[:, t, :]), wait=(t == TILES - 1))
            for t in range(TILES):
                step(nc.vector.match_replace(PR[:, t, :], T8[:, t, :], PA[:, t, :], -1.0), wait=(t == TILES - 1))
            step(nc.vector.tensor_scalar(MK[:, :, :], PR[:, :, 0:BLOCKS16], -1.0, None, ALU.is_equal))
            assert n == FFN_STEPS, n
            for J in range(JOBS):
                at = HR[:, J % CH, cols(J // CH)]
                dve.wait_ge(s_mb, J + 1)
                dve.wait_ge(s_hr, J + 1)
                nc.vector.tensor_tensor(at, at, mb_ps[:, J % 2, :], ALU.mult).then_inc(s_hm, 1)
            for b in range(BLKS):
                batch = b * BLK // SEQ
                dve.wait_ge(s_yb, b + 1)
                nc.vector.scalar_tensor_tensor(out=g.X[:, cols(b)], in0=g.Y[:, cols(b)],
                                               scalar=g.mod[:, 1, 5, batch:batch + 1], in1=g.X[:, cols(b)],
                                               op0=ALU.mult, op1=ALU.add).then_inc(s_x, 1)


FFN_STEPS = 43


def stage_residual(nc, g, layer, which):
    with ExitStack() as ctx:
        block = ctx.enter_context(nc.Block())

        @block.vector
        def _(dve):
            for b in range(BATCH):
                cols = slice(b * SEQ, (b + 1) * SEQ)
                nc.vector.scalar_tensor_tensor(out=g.X[:, cols], in0=g.Y[:, cols], scalar=g.mod[:, layer, which, b:b + 1],
                                               in1=g.X[:, cols], op0=ALU.mult, op1=ALU.add)


VECS = ("g_norm", "norm_w", "op_b", "b2", "gn_f", "gn_b", "D_f", "D_b")


def program(nc, d, out):
    with ExitStack() as ctx:
        sb, _, _ = alloc(nc, ctx)
        g = Shared()
        g.X, g.H, g.U, g.Y = (sb(n, [P, TOK]) for n in ("X", "H", "U", "Y"))
        g.mod, g.vecs = sb("mod", [P, 2, 6, BATCH]), sb("vecs", [P, len(VECS)])
        g.ident, g.center, g.ones = (sb(n, [P, P]) for n in ("ident", "center", "ones"))
        g.mean_col, g.eps = sb("mean_col", [P, 1]), sb("eps", [P, 2])
        g.eps5, g.eps_machine = g.eps[:, 0:1], g.eps[:, 1:2]
        g.vec = {n: g.vecs[:, i:i + 1] for i, n in enumerate(VECS)}
        stage_modulation(nc, d, g)
        with ExitStack() as scope:
            a, loads = attention_loads(d, g, alloc(nc, scope)[0])
            stage_norm(nc, g, "n0", 0, 0, rms=(g.vec["g_norm"], g.eps_machine), loads=loads)
            stage_attention(nc, d, g, a)
        stage_residual(nc, g, 0, 2)
        stage_norm(nc, g, "n1", 0, 1)
        stage_moe(nc, d, g)
        stage_residual(nc, g, 0, 5)
        stage_norm(nc, g, "n2", 1, 0, rms=(g.vec["norm_w"], g.eps5))
        stage_mamba(nc, d, g)
        stage_residual(nc, g, 1, 2)
        stage_norm(nc, g, "n3", 1, 1)
        stage_ffn(nc, d, g, out)


def constants():
    def bits(a):
        return np.ascontiguousarray((np.ascontiguousarray(a, np.float32).view(np.uint32) >> 16).astype(np.uint16))
    inv = (1.0 / np.float32(10000.0) ** (np.arange(0, DH, 2, dtype=np.float32) / np.float32(DH))).astype(np.float32)
    ang = np.repeat(np.arange(SEQ, dtype=np.float32)[:, None] * inv, 2, axis=-1)
    sign = np.where(np.arange(DH) % 2 == 0, np.float32(-1), np.float32(1))
    cs = np.stack([np.cos(ang), np.sin(ang) * sign])
    cs = np.tile(cs.transpose(2, 1, 0), (2, BATCH, 1))
    cs = cs.reshape(P, ITERS, ITER, 2).transpose(1, 0, 3, 2).reshape(ITERS, P, 2 * ITER)
    i, j = np.arange(P)[:, None] % SEG, np.arange(KEYS)[None, :]
    mask = np.where((j >= SEG) | (j <= i), 0.0, -BIG)
    r, c = np.arange(P)[:, None], np.arange(P)[None, :]
    tri = np.stack([r <= c, r > c, r >= c, r < c], axis=1)
    sel = np.zeros((CHUNKS, P, P), np.float32)
    for ch in range(CHUNKS - 2):
        e = (ch * P + np.arange(P)) // FF
        sel[ch, e, np.arange(P)] = sel[ch, EXPERTS + e, np.arange(P)] = 1
    self_ = np.repeat(np.eye(BLOCKS16, dtype=np.float32), FBLK, axis=1)
    eye = np.eye(P, dtype=np.float32)
    f = lambda a: np.ascontiguousarray(a, np.float32)
    return {"cs": f(cs), "maskb": bits(np.tile(mask, (1, QG))), "identb": bits(eye), "ident": eye,
            "center": f(eye - np.float32(1 / P)), "tri": f(tri), "sel": f(sel),
            "self": bits(self_)}


def layouts(x, sel):
    a = {k: np.asarray(v) for k, v in x.items()}
    L = {}
    L["xT"] = a["L0_attn_seq"].reshape(TOK, P).T
    L["ct"] = np.stack([a["L0_c"].T, a["L1_c"].T], 1)
    L["wmod"] = np.stack([a["L0_wmod"], a["L1_wmod"]], 1)
    L["vecs"] = np.stack([a["L0_attn_g_norm"], a["L1_attn_norm_w"], a["L1_attn_op_b"], a["L1_ffn_b2"],
                          a["L1_attn_f_gnorm_w"], a["L1_attn_b_gnorm_w"],
                          np.repeat(a["L1_attn_f_D"], HD), np.repeat(a["L1_attn_b_D"], HD)], 1)
    w = a["L0_attn_W_qkv"]
    L["wqk"] = w[:, 0:2 * HEADS * DH].reshape(P, 2, 2, 4 * P).transpose(0, 2, 1, 3).reshape(P, 2 * HEADS * DH)
    L["wv"] = w[:, 2 * HEADS * DH:]
    L["wo"] = a["L0_attn_W_out"].reshape(PAIRS, P, P).transpose(1, 0, 2)
    pm = a["L0_attn_pm"]
    L["pmk"] = pm[0].reshape(PAIRS, 2, PM, DH).transpose(1, 3, 0, 2).reshape(P, PAIRS, PM)
    L["pmv"] = pm[1].transpose(1, 0, 2).reshape(PM, HEADS * DH)
    L["gateT"] = a["L0_ffn_gate_w"].T
    L["gbias"] = np.broadcast_to(a["L0_ffn_gate_bias"], (P, EXPERTS))

    def hidden(e, s):
        s = np.concatenate([s.reshape(2, FF, P), np.zeros((2, P - FF, P), s.dtype)], 1)
        return np.concatenate([e.reshape(-1, P), s.reshape(-1, P)]).reshape(CHUNKS, P, P)
    wg = hidden(a["L0_ffn_Wg"], a["L0_ffn_Sg"]).transpose(0, 2, 1)
    wu = hidden(a["L0_ffn_Wu"], a["L0_ffn_Su"]).transpose(0, 2, 1)
    wd = hidden(a["L0_ffn_Wd"].transpose(0, 2, 1), a["L0_ffn_Sd"].T)
    L["w4"] = np.stack([wg, wu, wd, sel], 2).reshape(CHUNKS, P, 4 * P)
    dirs = ("f", "b")
    inw = [a[f"L1_attn_{k}_in_w"].T for k in dirs]
    L["wxbc"] = np.stack([np.concatenate([m[:, P:4 * P]] * 2, 0) for m in inw], 1)
    L["wz"] = np.stack([np.concatenate([m[:, 0:P], np.zeros((HD, P), m.dtype)]) for m in inw], 1)
    wdt = np.zeros((P, 4), np.float32)
    wdt[0:HD, 0:2], wdt[HD:P, 2:4] = inw[0][:, 4 * P:], inw[1][:, 4 * P:]
    L["wdt"] = wdt
    cw = [a[f"L1_attn_{k}_conv_w"].T for k in dirs]
    L["cw"] = np.stack([np.stack([np.repeat(m[[3 - 2 * q, 2 - 2 * q]], HD, axis=0) for q in range(2)], 1) for m in cw], 1)
    L["cb"] = np.stack([a[f"L1_attn_{k}_conv_b"].reshape(3, P).T for k in dirs], 1)
    L["dtb"] = np.broadcast_to(np.concatenate([a[f"L1_attn_{k}_dt_bias"] for k in dirs]), (P, 4))
    L["alog"] = np.broadcast_to(np.concatenate([a[f"L1_attn_{k}_A_log"] for k in dirs]), (P, 4))
    L["wp"] = np.stack([a[f"L1_attn_{k}_outp_w"].T for k in dirs], 1)
    L["opT"] = a["L1_attn_op_w"].T
    L["wr"] = a["L1_ffn_w_router"]
    L["br"] = np.broadcast_to(a["L1_ffn_b_router"], (P, BLOCKS16))
    L["w1T"] = a["L1_ffn_w1"].T
    L["b1"] = a["L1_ffn_b1"].reshape(HID1 // P, P).T
    L["w2T"] = a["L1_ffn_w2"].T.reshape(HID1 // P, P, P).transpose(1, 0, 2)
    return {k: np.ascontiguousarray(v) for k, v in L.items()}


def kernel(**inputs):
    import concourse.bacc as bacc
    from concourse.bass_utils import run_bass_kernel_spmd

    tables = constants()
    arrays = {**layouts(inputs, tables.pop("sel")), **tables}
    nc = bacc.Bacc("TRN2", target_bir_lowering=False, num_devices=1)
    aps = {n: nc.dram_tensor(f"in_{n}", a.shape, mybir.dt.from_np(a.dtype), kind="ExternalInput").ap()
           for n, a in arrays.items()}
    d = {n: ap.bitcast(BF16) if arrays[n].dtype == np.uint16 else ap for n, ap in aps.items()}
    out = nc.dram_tensor("out_xT", (P, TOK), F32, kind="ExternalOutput").ap()
    program(nc, d, out)
    r = run_bass_kernel_spmd(nc, [{f"in_{n}": a for n, a in arrays.items()}], core_ids=[0])
    return np.ascontiguousarray(r.results[0]["out_xT"].T).reshape(BATCH, SEQ, P)
```

```python
from contextlib import ExitStack

import numpy as np

import concourse.bass as bass
from concourse import mybir

F32 = mybir.dt.float32
F32R = mybir.dt.float32r
BF16 = mybir.dt.bfloat16
ALU = mybir.AluOpType
ACT = mybir.ActivationFunctionType
AX = mybir.AxisListType

P = 128
BATCH, SEQ = 2, 1024
TOK = BATCH * SEQ
TILES = TOK // P
BLK = 512
BLKS = TOK // BLK
HEADS, DH, SEG, PM = 16, 64, 64, 16
PAIRS = HEADS // 2
KEYS = SEG + PM
ITER = 256
ITERS = TOK // ITER
SEGS = ITER // SEG
QG = 4
UNITS = (ITER // P) * HEADS // QG
EXPERTS, FF, GROUPS, TOPG = 64, 88, 8, 4
GSIZE = EXPERTS // GROUPS
CHUNKS = EXPERTS * FF // P + 2
HD = 64
CONVPAD = 6
BLOCKS16, FBLK, FTOP = 16, 32, 4
HID1 = BLOCKS16 * FBLK
BIG = 1e30


class Shared:
    pass


def alloc(nc, ctx):
    def sb(name, shape, dt=F32):
        return ctx.enter_context(nc.sbuf_tensor(name, shape, dt))

    def ps(name, shape, dt=F32):
        return ctx.enter_context(nc.psum_tensor(name, shape, dt))

    def sem(name):
        return ctx.enter_context(nc.semaphore(name))
    return sb, ps, sem


def stage_modulation(nc, d, g):
    with ExitStack() as ctx:
        sb, ps, sem = alloc(nc, ctx)
        ct = sb("ct", [P, 2, BATCH])
        st = sb("st", [P, 2, BATCH])
        wmod = sb("wmod", [P, 2, 6 * P])
        mag = sb("mag", [P, 2, 2, BATCH])
        sgn = sb("sgn", [P, 2, 2, BATCH])
        mp = ps("mp", [P, 2, 6, BATCH])
        s_c, s_x, s_silu, s_mod, s_dve = sem("m_c"), sem("m_x"), sem("m_silu"), sem("m_mod"), sem("m_dve")
        block = ctx.enter_context(nc.Block())

        @block.sync
        def _(sp):
            sp.dma_start(ct[:, :, :], d["ct"]).then_inc(s_c, 16)
            sp.dma_start(wmod[:, :, :], d["wmod"]).then_inc(s_c, 16)
            sp.dma_start(g.X[:, :], d["xT"]).then_inc(s_x, 16)
            sp.dma_start(g.ident[:, :], d["ident"]).then_inc(s_x, 16)
            sp.dma_start(g.center[:, :], d["center"]).then_inc(s_x, 16)
            sp.dma_start(g.vecs[:, :], d["vecs"]).then_inc(s_x, 16)
            sp.wait_ge(s_x, 64)

        @block.scalar
        def _(act):
            act.wait_ge(s_c, 32)
            nc.scalar.activation(st[:, :, :], ct[:, :, :], ACT.Silu).then_inc(s_silu, 1)
            act.wait_ge(s_x, 64)
            nc.scalar.activation(g.onesr[:, :], g.ident[:, :], ACT.Identity, scale=0.0, bias=1.0)

        @block.tensor
        def _(pe):
            pe.wait_ge(s_silu, 1)
            for layer in range(2):
                for v in range(6):
                    mm = nc.tensor.matmul(mp[:, layer, v, :], wmod[:, layer, v * P:(v + 1) * P],
                                          st[:, layer, :], start=True, stop=True)
            mm.then_inc(s_mod, 1)

        @block.vector
        def _(dve):
            nc.vector.memset(g.mean_col[:, :], 1.0 / P).then_inc(s_dve, 1)
            nc.vector.memset(g.ones[:, :], 1.0).then_inc(s_dve, 1)
            nc.vector.memset(g.U[:, TOK:], 0.0).then_inc(s_dve, 1)
            nc.vector.memset(g.eps[:, 0:1], 1e-5).then_inc(s_dve, 1)
            nc.vector.memset(g.eps[:, 1:2], float(np.finfo(np.float32).eps)).then_inc(s_dve, 1)
            dve.wait_ge(s_mod, 1)
            nc.vector.tensor_copy(g.mod[:, :, :, :], mp[:, :, :, :]).then_inc(s_dve, 1)
            dve.wait_ge(s_dve, 6)
            for n, v in enumerate((1, 4)):
                nc.vector.tensor_scalar(g.mod[:, :, v, :], g.mod[:, :, v, :], 1.0, None, ALU.add).then_inc(s_dve, 1)
            gates = g.mod[:, :, 2:6:3, :]
            nc.vector.tensor_scalar(mag[:, :, :, :], gates, -1.0, None, ALU.mult).then_inc(s_dve, 1)
            nc.vector.tensor_scalar(sgn[:, :, :, :], gates, 0.0, 2.0, ALU.is_ge, ALU.mult).then_inc(s_dve, 1)
            dve.wait_ge(s_dve, 10)
            nc.vector.tensor_tensor(mag[:, :, :, :], mag[:, :, :, :], gates, ALU.max).then_inc(s_dve, 1)
            nc.vector.tensor_scalar(sgn[:, :, :, :], sgn[:, :, :, :], -1.0, None, ALU.add).then_inc(s_dve, 1)
            dve.wait_ge(s_dve, 12)
            nc.vector.tensor_scalar(mag[:, :, :, :], mag[:, :, :, :], 0.25, None, ALU.max).then_inc(s_dve, 1)
            dve.wait_ge(s_dve, 13)
            nc.vector.tensor_tensor(gates, mag[:, :, :, :], sgn[:, :, :, :], ALU.mult).then_inc(s_dve, 1)


def stage_norm(nc, g, tag, layer, half, rms=None, residual=None, loads=(), splits=(), copies=()):
    norms = 2 if rms else 1
    scale, shift = (1, 0) if half == 0 else (4, 3)
    with ExitStack() as ctx:
        sb, ps, sem = alloc(nc, ctx)
        D, XN, SQ = (sb(tag + n, [P, TOK]) for n in ("D", "XN", "SQ"))
        ST, R = sb(tag + "ST", [P, norms, TILES]), sb(tag + "R", [P, norms, TILES])
        RH, RL = (sb(tag + n, [P, norms, TILES], F32R) for n in ("RH", "RL"))
        DH, DL = (sb(tag + n, [P, 2, BLK], F32R) for n in ("DH", "DL"))
        d_ps, ms_ps, r_ps = (ps(tag + n, [P, 2, BLK]) for n in ("d_ps", "ms_ps", "r_ps"))
        s_cent, s_d, s_sq, s_ms, s_root, s_inv = (sem(tag + n) for n in ("cent", "d", "sq", "ms", "root", "inv"))
        s_r, s_ap, s_h = (sem(tag + n) for n in ("r", "ap", "h"))
        s_dl = sem(tag + "dl")
        s_load = sem(tag + "load") if loads else None
        s_high = sem(tag + "high") if splits else None
        block = ctx.enter_context(nc.Block())
        TB = BLK // P
        SPLIT = 4 if rms else 2
        RES = BLKS if residual else 0
        ORDER = [(0, b) for b in range(BLKS)]
        if rms:
            ORDER = [(0, 0), (0, 1), (0, 2), (0, 3), (1, 0), (1, 1), (1, 2), (1, 3)]

        def cols(b):
            return slice(b * BLK, (b + 1) * BLK)

        @block.sync
        def _(sp):
            for dst, src in loads:
                sp.dma_start(dst, src).then_inc(s_load, 16)
            for blocks, dst, src, s_copied in copies:
                sp.wait_ge(s_ap, BLKS + blocks)
                sp.dma_start(dst, src).then_inc(s_copied, 16)
            if loads:
                sp.wait_ge(s_load, 16 * len(loads))

        @block.tensor
        def _(pe):
            def mean_square(n, b):
                i = ORDER.index((n, b))
                pe.wait_ge(s_sq, i + 1)
                if i >= 2:
                    pe.wait_ge(s_root, i - 1)
                for t in range(TB):
                    at = slice(b * BLK + t * P, b * BLK + (t + 1) * P)
                    mm = nc.tensor.matmul(ms_ps[:, i % 2, t:t + 1], SQ[:, at], g.mean_col[:, :], start=True, stop=True)
                mm.then_inc(s_ms, 1)

            def broadcast(n, b):
                i = ORDER.index((n, b))
                if i >= 2:
                    pe.wait_ge(s_ap, i - 1)
                pe.wait_ge(s_inv, 4 * (i + 1))
                nc.tensor.matmul(r_ps[:, i % 2, :], g.onesr[:, :], DH[:, i % 2, :], start=True, stop=False)
                pe.wait_ge(s_dl, i + 1)
                nc.tensor.matmul(r_ps[:, i % 2, :], g.onesr[:, :], DL[:, i % 2, :], start=False, stop=True).then_inc(s_r, 1)

            for b in range(BLKS):
                if residual:
                    pe.wait_ge(s_d, b + 1)
                if b >= 2:
                    pe.wait_ge(s_d, RES + b - 1)
                nc.tensor.matmul(d_ps[:, b % 2, :], g.center[:, :], g.X[:, cols(b)], start=True, stop=True).then_inc(s_cent, 1)
                if b >= 1:
                    mean_square(0, b - 1)
                if b >= 2:
                    broadcast(0, b - 2)
            for i in range(3, len(ORDER)):
                mean_square(*ORDER[i])
                broadcast(*ORDER[i - 1])
            broadcast(*ORDER[-1])

        @block.scalar
        def _(act):
            nc.scalar.preload_act_table(ACT.Sqrt)

            def root(n, b):
                i = ORDER.index((n, b))
                act.wait_ge(s_ms, i + 1)
                nc.scalar.activation(ST[:, n, TB * b:TB * (b + 1)], ms_ps[:, i % 2, 0:TB], ACT.Sqrt,
                                     bias=(rms[1] if n else g.eps5)).then_inc(s_root, 1)

            def modulate(b):
                batch = b * BLK // SEQ
                act.wait_ge(s_ap, b + 1)
                nc.scalar.activation(g.H[:, cols(b)], XN[:, cols(b)], ACT.Identity,
                                     scale=g.mod[:, layer, scale, batch:batch + 1],
                                     bias=g.mod[:, layer, shift, batch:batch + 1]).then_inc(s_h, 1)

            done = 0
            for i, (n, b) in enumerate(ORDER):
                if n == 0:
                    act.wait_ge(s_cent, b + 1)
                    nc.scalar.activation(SQ[:, cols(b)], d_ps[:, b % 2, :], ACT.Square).then_inc(s_sq, 1)
                else:
                    modulate(b)
                    done += 1
                    act.wait_ge(s_h, b + 1)
                    act.wait_ge(s_ms, ORDER.index((0, b)) + 1)
                    nc.scalar.activation(SQ[:, cols(b)], g.H[:, cols(b)], ACT.Square).then_inc(s_sq, 1)
                if i >= 1:
                    root(*ORDER[i - 1])
                if SPLIT <= i < SPLIT + len(splits):
                    if i == SPLIT:
                        act.wait_ge(s_load, 16 * len(loads))
                    raw, high, _ = splits[i - SPLIT]
                    nc.scalar.activation(high, raw, ACT.Copy).then_inc(s_high, 1)
            root(*ORDER[-1])
            for b in range(done, BLKS):
                modulate(b)

        @block.gpsimd
        def _(pool):
            for i, (n, b) in enumerate(ORDER):
                pool.wait_ge(s_inv, 4 * i + 3)
                if i >= 2:
                    pool.wait_ge(s_r, i - 1)
                nc.gpsimd.tensor_tensor(DL[:, i % 2, :].rearrange("p (t k) -> p t k", t=TB),
                                        g.ident[:, :].unsqueeze(1).broadcast_to([P, TB, P]),
                                        RL[:, n, TB * b:TB * (b + 1)].unsqueeze(2).broadcast_to([P, TB, P]),
                                        ALU.mult).then_inc(s_dl, 1)

        @block.vector
        def _(dve):
            def inverse(n, b):
                i, tiles = ORDER.index((n, b)), slice(TB * b, TB * (b + 1))
                dve.wait_ge(s_root, i + 1)
                nc.vector.reciprocal(R[:, n, tiles], ST[:, n, tiles]).then_inc(s_inv, 1)
                dve.wait_ge(s_inv, 4 * i + 1)
                nc.vector.tensor_copy(RH[:, n, tiles], R[:, n, tiles]).then_inc(s_inv, 1)
                dve.wait_ge(s_inv, 4 * i + 2)
                nc.vector.tensor_tensor(RL[:, n, tiles], R[:, n, tiles], RH[:, n, tiles], ALU.subtract).then_inc(s_inv, 1)
                if i >= 2:
                    dve.wait_ge(s_r, i - 1)
                nc.vector.tensor_tensor(DH[:, i % 2, :].rearrange("p (t k) -> p t k", t=TB),
                                        g.ident[:, :].unsqueeze(1).broadcast_to([P, TB, P]),
                                        RH[:, n, tiles].unsqueeze(2).broadcast_to([P, TB, P]), ALU.mult).then_inc(s_inv, 1)

            def apply(n, b):
                i = ORDER.index((n, b))
                dve.wait_ge(s_r, i + 1)
                if n == 0:
                    dve.wait_ge(s_d, RES + b + 1)
                    nc.vector.tensor_tensor(XN[:, cols(b)], D[:, cols(b)], r_ps[:, i % 2, :], ALU.mult).then_inc(s_ap, 1)
                else:
                    dve.wait_ge(s_h, b + 1)
                    nc.vector.scalar_tensor_tensor(out=g.U[:, cols(b)], in0=g.H[:, cols(b)], scalar=rms[0],
                                                   in1=r_ps[:, i % 2, :], op0=ALU.mult, op1=ALU.mult).then_inc(s_ap, 1)

            for i, (n, b) in enumerate(ORDER):
                if n == 0:
                    if residual and b == 0:
                        for c in range(BLKS):
                            batch = c * BLK // SEQ
                            nc.vector.scalar_tensor_tensor(out=g.X[:, cols(c)], in0=g.Y[:, cols(c)],
                                                           scalar=g.mod[:, residual[0], residual[1], batch:batch + 1],
                                                           in1=g.X[:, cols(c)], op0=ALU.mult, op1=ALU.add).then_inc(s_d, 1)
                    dve.wait_ge(s_sq, ORDER.index((0, b)) + 1)
                    nc.vector.tensor_copy(D[:, cols(b)], d_ps[:, b % 2, :]).then_inc(s_d, 1)
                if i >= 1:
                    inverse(*ORDER[i - 1])
                if i >= 2:
                    apply(*ORDER[i - 2])
                if SPLIT < i <= SPLIT + len(splits):
                    raw, high, low = splits[i - SPLIT - 1]
                    dve.wait_ge(s_high, i - SPLIT)
                    nc.vector.tensor_tensor(low, raw, high, ALU.subtract)
            inverse(*ORDER[-1])
            for n, b in ORDER[-2:]:
                apply(n, b)


NEIGHBOUR = [i ^ 1 for i in range(32)]


def attention_loads(d, g, sb):
    a = Shared()
    a.wv = sb("wv", [P, HEADS * DH])
    a.wo = sb("wo", [P, PAIRS, P])
    a.wqkh, a.wqkl = (sb(n, [P, 2 * PAIRS, P], F32R) for n in ("wqkh", "wqkl"))
    a.wvh, a.wvl = (sb(n, [P, HEADS * DH], F32R) for n in ("wvh", "wvl"))
    a.pmk = sb("pmk", [P, PAIRS, PM])
    a.maskb, a.identb = sb("maskb", [P, QG * KEYS], BF16), sb("identb", [P, P], BF16)
    a.V = sb("V", [KEYS, 2, SEGS, HEADS * DH])
    loads = [(g.Y[:, :], d["wqk"]), (a.wv[:, :], d["wv"]), (a.wo[:, :, :], d["wo"]),
             (a.pmk[:, :, :], d["pmk"]), (a.maskb[:, :], d["maskb"]), (a.identb[:, :], d["identb"])]
    for par in range(2):
        for seg in range(SEGS):
            loads.append((a.V[SEG:KEYS, par, seg, :], d["pmv"]))
    wqk = g.Y[:, :].rearrange("p (a b) -> p a b", b=P)
    halves = [slice(0, PAIRS), slice(PAIRS, 2 * PAIRS)]
    splits = [(a.wv[:, :], a.wvh[:, :], a.wvl[:, :])] + [(wqk[:, h, :], a.wqkh[:, h, :], a.wqkl[:, h, :]) for h in halves]
    return a, loads, splits


def stage_attention(nc, d, g, a):
    with ExitStack() as ctx:
        sb, ps, sem = alloc(nc, ctx)
        wqkh, wqkl, wvh, wvl = a.wqkh, a.wqkl, a.wvh, a.wvl
        Gh, Gl = (sb(n, [P, 2, ITER], F32R) for n in ("Gh", "Gl"))
        cs = sb("cs", [P, 2, 2, ITER])
        T = sb("T", [P, 2, 2, ITER])
        S = sb("S", [P, 2, 2, ITER])
        Q = sb("Q", [P, 2, PAIRS, ITER])
        K = sb("K", [P, 2, PAIRS, SEGS, KEYS])
        MX, NM = sb("MX", [P, 2, QG]), sb("NM", [P, 2, QG])
        SM = sb("SM", [P, 2, QG])
        RC = sb("RC", [P, 2, QG])
        PR = sb("PR", [P, 4, QG, KEYS])
        PT = sb("PT", [KEYS, 4, QG, P])
        OT = sb("OT", [P, 2, PAIRS, ITER])
        s_bank = ps("s_bank", [P, 2, 512])
        pt_bank = ps("pt_bank", [P, 2, QG, P])
        o_bank = ps("o_bank", [P, QG, P])
        qk_bank = ps("qk_bank", [P, 2, 2, ITER])
        v_bank = ps("v_bank", [P, 512])
        s_pm, s_gh, s_gl, s_cs = (sem("a_" + n) for n in ("pm", "gh", "gl", "cs"))
        s_qk, s_rot, s_sin, s_add = (sem("a_" + n) for n in ("qk", "rot", "sin", "add"))
        s_v, s_vev = sem("a_v"), sem("a_vev")
        s_sc, s_mx, s_nm, s_exp, s_sum, s_rc, s_pr = (sem("a_" + n) for n in ("sc", "mx", "nm", "exp", "sum", "rc", "pr"))
        s_tr, s_ptev, s_av, s_oev, s_y, s_yev = (sem("a_" + n) for n in ("tr", "ptev", "av", "oev", "y", "yev"))
        ROPES = PAIRS
        VH = 2 * SEGS

        def loops(eng, body, first, tail):
            first()
            body(0, 0, "first")
            with eng.Fori(0, (ITERS - 2) // 2) as i:
                body(i * 2 + 1, 1, "mid")
                body(i * 2 + 2, 0, "mid")
            body(ITERS - 1, 1, "last")
            tail()

        def noop():
            pass

        wo, pmk, maskb, identb, V = a.wo, a.pmk, a.maskb, a.identb, a.V

        block = ctx.enter_context(nc.Block())

        @block.sync
        def _(sp):
            def load(n, par):
                src = d["cs"][bass.ds(n, 1), :, :].rearrange("o p n -> (o p) n")
                if not (isinstance(n, int) and n < 1):
                    sp.wait_ge(s_add, (n - 1) * ROPES + 1)
                sp.dma_start(cs[:, par, :, :].rearrange("p a b -> p (a b)"), src).then_inc(s_cs, 16)

            def first():
                load(0, 0)

            def body(it, par, which):
                if which != "last":
                    load(it + 1, 1 - par)

            loops(sp, body, first, noop)

        @block.tensor
        def _(pe):
            def scores(it, par, u):
                sp_, hh, odd = u // 4, (u // 2) % 2, u % 2
                U = it * UNITS + u
                if not (isinstance(it, int) and U < 2):
                    pe.wait_ge(s_exp, U - 1)
                bank = s_bank[:, u % 2, 0:QG * KEYS]
                nc.tensor.matmul(bank, identb[:, :], maskb[:, :], start=True, stop=False, skip_group_check=True)
                for j in range(QG):
                    for s in range(2):
                        mm = nc.tensor.matmul(
                            s_bank[SEG * s:SEG * (s + 1), u % 2, j * KEYS:(j + 1) * KEYS],
                            Q[DH * odd:DH * (odd + 1), par, QG * hh + j, P * sp_ + SEG * s:P * sp_ + SEG * (s + 1)],
                            K[DH * odd:DH * (odd + 1), par, QG * hh + j, 2 * sp_ + s, :],
                            start=False, stop=True, skip_group_check=True)
                mm.then_inc(s_sc, 1)

            def transposes(U, u):
                pe.wait_ge(s_pr, U + 1)
                if not (isinstance(U, int) and U < 2):
                    pe.wait_ge(s_ptev, U - 1)
                for j in range(QG):
                    mm = nc.tensor.transpose(pt_bank[0:KEYS, u % 2, j, :], PR[:, u % 4, j, :], g.ident[:, :])
                mm.then_inc(s_tr, 1)

            def values(U, u, it, par):
                sp_, hh = u // 4, (u // 2) % 2
                pe.wait_ge(s_ptev, U + 1)
                if u % 4 == 1:
                    pe.wait_ge(s_vev, it * VH + 4 * (sp_ + 1))
                if not (isinstance(U, int) and U == 1):
                    pe.wait_ge(s_oev, it * (UNITS // 2) + u // 2)
                for j in range(QG):
                    for s in range(2):
                        for odd in range(2):
                            head = 2 * (QG * hh + j) + odd
                            mm = nc.tensor.matmul(o_bank[DH * odd:DH * (odd + 1), j, SEG * s:SEG * (s + 1)],
                                                  V[:, par, 2 * sp_ + s, head * DH:(head + 1) * DH],
                                                  PT[:, (u - 1 + odd) % 4, j, SEG * s:SEG * (s + 1)], start=True, stop=True)
                mm.then_inc(s_av, 1)

            def project_qk(n, par, i):
                if not (isinstance(n, int) and n == 0 and i < 2):
                    pe.wait_ge(s_rot, 2 * (n * ROPES + i - 1))
                for h in range(2):
                    out, c = qk_bank[:, i % 2, h, :], 2 * i + h
                    nc.tensor.matmul(out, wqkh[:, c, :], Gh[:, par, :], start=True, stop=False)
                    nc.tensor.matmul(out, wqkh[:, c, :], Gl[:, par, :], start=False, stop=False)
                    mm = nc.tensor.matmul(out, wqkl[:, c, :], Gh[:, par, :], start=False, stop=True)
                mm.then_inc(s_qk, 1)

            def project_v(n, par, v):
                if not (isinstance(n, int) and n == 0 and v == 0):
                    pe.wait_ge(s_vev, n * VH + 2 * v)
                cols, toks = slice(512 * (v % 2), 512 * (v % 2 + 1)), slice(P * (v // 2), P * (v // 2 + 1))
                nc.tensor.matmul(v_bank[:, :], Gh[:, par, toks], wvh[:, cols], start=True, stop=False)
                nc.tensor.matmul(v_bank[:, :], Gl[:, par, toks], wvh[:, cols], start=False, stop=False)
                nc.tensor.matmul(v_bank[:, :], Gh[:, par, toks], wvl[:, cols], start=False, stop=True).then_inc(s_v, 1)

            def project_out(it, par, vdone):
                pe.wait_ge(s_oev, (it + 1) * (UNITS // 2))
                pe.wait_ge(s_vev, vdone)
                for hp in range(PAIRS):
                    mm = nc.tensor.matmul(v_bank[:, 0:ITER], wo[:, hp, :], OT[:, par, hp, :],
                                          start=(hp == 0), stop=(hp == PAIRS - 1))
                mm.then_inc(s_y, 1)

            def first():
                pe.sem_inc(s_y, 2)
                pe.wait_ge(s_gl, 1)
                for i in range(ROPES):
                    project_qk(0, 0, i)
                    if i % 2:
                        project_v(0, 0, i // 2)

            def body(it, par, which):
                if which == "first":
                    pe.wait_ge(s_pm, 2 * SEGS)
                for u in range(UNITS):
                    if u == 0:
                        pe.wait_ge(s_add, it * ROPES + ROPES // 2)
                    if u == 2:
                        pe.wait_ge(s_add, (it + 1) * ROPES)
                    scores(it, par, u)
                    old = not (which == "first" and u < 2)
                    pu, pit, ppar = (u - 2, it, par) if u >= 2 else (u + UNITS - 2, it - 1, 1 - par)
                    if old:
                        transposes(pit * UNITS + pu, pu)
                    if u == 3 and which != "first":
                        project_out(it - 1, 1 - par, (it + 1) * VH + (4 if which != "last" else 0))
                    if which != "last":
                        if u == 0:
                            pe.wait_ge(s_gl, it + 2)
                        project_qk(it + 1, 1 - par, u)
                        if u == 4 and which != "first":
                            pe.wait_ge(s_yev, it)
                        if u % 2 == 0:
                            project_v(it + 1, 1 - par, u // 2)
                    if old and pu % 2:
                        values(pit * UNITS + pu, pu, pit, ppar)

            def tail():
                it = ITERS - 1
                for u in (UNITS - 2, UNITS - 1):
                    transposes(it * UNITS + u, u)
                values(it * UNITS + UNITS - 1, UNITS - 1, it, 1)
                pe.wait_ge(s_yev, it)
                project_out(it, 1, ITERS * VH)

            loops(pe, body, first, tail)

        @block.vector
        def _(dve):
            def low_block(n, par):
                dve.wait_ge(s_gh, n + 1)
                if not (isinstance(n, int) and n < 2):
                    dve.wait_ge(s_v, (n - 1) * (VH // 2))
                nc.vector.tensor_tensor(Gl[:, par, :], g.U[:, bass.ds(n * ITER, ITER)], Gh[:, par, :], ALU.subtract).then_inc(s_gl, 1)

            def rope(n, par, i):
                dve.wait_ge(s_qk, n * ROPES + i + 1)
                if not (isinstance(n, int) and n == 0 and i < 2):
                    dve.wait_ge(s_add, n * ROPES + i - 1)
                if i == 0:
                    dve.wait_ge(s_cs, (n + 1) * 16)
                nc.vector.tensor_tensor(T[:, i % 2, :, :], qk_bank[:, i % 2, :, :],
                                        cs[:, par, 0, :].unsqueeze(1).broadcast_to([P, 2, ITER]),
                                        ALU.mult).then_inc(s_rot, 1)
                nc.vector.stream_shuffle(S[:, i % 2, :, :], qk_bank[:, i % 2, :, :], NEIGHBOUR).then_inc(s_rot, 1)

            def softmax_a(it, u):
                U = it * UNITS + u
                S = s_bank[:, u % 2, 0:QG * KEYS].rearrange("p (j k) -> p j k", j=QG)
                dve.wait_ge(s_sc, U + 1)
                nc.vector.tensor_reduce(MX[:, u % 2, :], S, AX.X, ALU.max).then_inc(s_mx, 1)
                dve.wait_ge(s_mx, U + 1)
                if not (isinstance(it, int) and U < 2):
                    dve.wait_ge(s_exp, U - 1)
                nc.vector.tensor_scalar(NM[:, u % 2, :], MX[:, u % 2, :], -(DH ** -0.5), None, ALU.mult).then_inc(s_nm, 1)

            def softmax_b(it, u):
                U = it * UNITS + u
                dve.wait_ge(s_exp, U + 1)
                nc.vector.tensor_reduce(SM[:, u % 2, :], PR[:, u % 4, :, :], AX.X, ALU.add).then_inc(s_sum, 1)
                dve.wait_ge(s_sum, U + 1)
                if not (isinstance(it, int) and U < 2):
                    dve.wait_ge(s_pr, U - 1)
                nc.vector.reciprocal(RC[:, u % 2, :], SM[:, u % 2, :]).then_inc(s_rc, 1)

            def normalise(it, u):
                dve.wait_ge(s_rc, it * UNITS + u + 1)
                nc.vector.tensor_tensor(PR[:, u % 4, :, :], PR[:, u % 4, :, :],
                                        RC[:, u % 2, :].unsqueeze(2).broadcast_to([P, QG, KEYS]), ALU.mult).then_inc(s_pr, 1)

            def first():
                low_block(0, 0)
                low_block(1, 1)
                for i in range(ROPES):
                    rope(0, 0, i)
                    dve.wait_ge(s_rot, 2 * (i + 1))
                    nc.vector.tensor_tensor(S[:, i % 2, :, :], S[:, i % 2, :, :],
                                            cs[:, 0, 1, :].unsqueeze(1).broadcast_to([P, 2, ITER]), ALU.mult).then_inc(s_sin, 1)

            def body(it, par, which):
                for u in range(UNITS):
                    softmax_a(it, u)
                    if u == 6 and which != "last":
                        low_block(it + 2, par)
                    if which != "last":
                        rope(it + 1, 1 - par, u)
                    softmax_b(it, u)
                    normalise(it, u)
            loops(dve, body, first, noop)

        @block.gpsimd
        def _(pool):
            def turn(n, par, i):
                if i == 0:
                    pool.wait_ge(s_cs, (n + 1) * 16)
                pool.wait_ge(s_rot, 2 * (n * ROPES + i + 1))
                nc.gpsimd.tensor_tensor(S[:, i % 2, :, :], S[:, i % 2, :, :],
                                        cs[:, par, 1, :].unsqueeze(1).broadcast_to([P, 2, ITER]),
                                        ALU.mult).then_inc(s_sin, 1)

            def add(n, par, i):
                pool.wait_ge(s_sin, n * ROPES + i + 1)
                two = slice(4 * (i // 4) + 2 * (i % 2), 4 * (i // 4) + 2 * (i % 2) + 2)
                if i == 0 and not (isinstance(n, int) and n < 2):
                    pool.wait_ge(s_sc, (n - 1) * UNITS)
                if i % 4 < 2:
                    nc.gpsimd.tensor_tensor(Q[:, par, two, :], T[:, i % 2, :, :], S[:, i % 2, :, :], ALU.add).then_inc(s_add, 1)
                else:
                    nc.gpsimd.tensor_tensor(K[:, par, two, :, 0:SEG], T[:, i % 2, :, :].rearrange("p h (s k) -> p h s k", s=SEGS),
                                            S[:, i % 2, :, :].rearrange("p h (s k) -> p h s k", s=SEGS), ALU.add).then_inc(s_add, 1)

            def first():
                for par in range(2):
                    for seg in range(SEGS):
                        nc.gpsimd.tensor_copy(K[:, par, :, seg, SEG:KEYS], pmk[:, :, :]).then_inc(s_pm, 1)
                for i in range(ROPES):
                    add(0, 0, i)

            def body(it, par, which):
                if which != "last":
                    for u in range(UNITS):
                        turn(it + 1, 1 - par, u)
                        add(it + 1, 1 - par, u)

            loops(pool, body, first, noop)

        @block.scalar
        def _(act):
            nc.scalar.preload_act_table(ACT.Exp)

            def exponent(it, u):
                U = it * UNITS + u
                act.wait_ge(s_nm, U + 1)
                if not (isinstance(it, int) and U < 4):
                    act.wait_ge(s_tr, U - 3)
                for j in range(QG):
                    ins = nc.scalar.activation(PR[:, u % 4, j, :], s_bank[:, u % 2, j * KEYS:(j + 1) * KEYS], ACT.Exp,
                                               scale=DH ** -0.5, bias=NM[:, u % 2, j:j + 1])
                ins.then_inc(s_exp, 1)

            def take_pt(U, u, it):
                act.wait_ge(s_tr, U + 1)
                if not (isinstance(U, int) and U < 4):
                    act.wait_ge(s_av, it * (UNITS // 2) + u // 2 - 1)
                nc.scalar.activation(PT[:, u % 4, :, :], pt_bank[0:KEYS, u % 2, :, :], ACT.Copy).then_inc(s_ptev, 1)

            def take_v(n, par, v):
                act.wait_ge(s_v, n * (VH // 2) + v + 1)
                if not (isinstance(n, int) and n < 2):
                    act.wait_ge(s_av, (n - 2) * (UNITS // 2) + (UNITS // 4) * (v // 2 + 1))
                for s in range(2):
                    nc.scalar.activation(V[0:SEG, par, 2 * (v // 2) + s, 512 * (v % 2):512 * (v % 2 + 1)],
                                         v_bank[SEG * s:SEG * (s + 1), :], ACT.Copy).then_inc(s_vev, 1)

            def take_o(U, u, it, par):
                act.wait_ge(s_av, it * (UNITS // 2) + u // 2 + 1)
                act.wait_ge(s_y, it + 1)
                sp_, hh = u // 4, (u // 2) % 2
                nc.scalar.activation(OT[:, par, QG * hh:QG * (hh + 1), P * sp_:P * (sp_ + 1)], o_bank[:, :, :],
                                     ACT.Copy).then_inc(s_oev, 1)

            def take_y(it):
                act.wait_ge(s_y, it + 3)
                nc.scalar.activation(g.Y[:, bass.ds(it * ITER, ITER)], v_bank[:, 0:ITER], ACT.Copy).then_inc(s_yev, 1)

            def high_block(n, par):
                if not (isinstance(n, int) and n < 2):
                    act.wait_ge(s_v, (n - 1) * (VH // 2))
                nc.scalar.activation(Gh[:, par, :], g.U[:, bass.ds(n * ITER, ITER)], ACT.Copy).then_inc(s_gh, 1)

            def first():
                high_block(0, 0)
                high_block(1, 1)
                for v in range(VH // 2):
                    take_v(0, 0, v)

            def body(it, par, which):
                for u in range(UNITS):
                    old = not (which == "first" and u < 2)
                    pu, pit, ppar = (u - 2, it, par) if u >= 2 else (u + UNITS - 2, it - 1, 1 - par)
                    if old:
                        take_pt(pit * UNITS + pu, pu, pit)
                    exponent(it, u)
                    if u == 5 and which != "last":
                        high_block(it + 2, par)
                    if u == 3 and which != "first":
                        take_y(it - 1)
                    if which != "last" and u % 2 == 0:
                        take_v(it + 1, 1 - par, u // 2)
                    if old and pu % 2:
                        take_o(pit * UNITS + pu, pu, pit, ppar)

            def tail():
                it = ITERS - 1
                for u in (UNITS - 2, UNITS - 1):
                    take_pt(it * UNITS + u, u, it)
                take_o(it * UNITS + UNITS - 1, UNITS - 1, it, 1)
                take_y(it)

            loops(act, body, first, tail)


def route_loads(d, sb):
    r = Shared()
    r.gate, r.gbias = sb("gate", [P, EXPERTS]), sb("gbias", [P, EXPERTS])
    return r, [(r.gate[:, :], d["gateT"]), (r.gbias[:, :], d["gbias"])]


RING, AHEAD, TBS = 4, 2, 2
EARLY = RING * TBS


def three(nc, out, e, k, w, hi, lo, start, stop):
    nc.tensor.matmul(out, e.WH[:, k, w, :], hi, start=start, stop=False, skip_group_check=True)
    nc.tensor.matmul(out, e.WH[:, k, w, :], lo, start=False, stop=False, skip_group_check=True)
    return nc.tensor.matmul(out, e.WL[:, k, w, :], hi, start=False, stop=stop, skip_group_check=True)


def stage_route(nc, d, g, r, e):
    with ExitStack() as ctx:
        sb, ps, sem = alloc(nc, ctx)
        gate, gbias = r.gate, r.gbias
        shape = [P, TILES, EXPERTS]
        HALVES, half_shape = (slice(0, TILES // 2), slice(TILES // 2, TILES)), [P, TILES // 2, EXPERTS]
        SC, SF, EQ, LOW = sb("SC", shape), sb("SF", shape), sb("EQ", shape), sb("LOW", shape)
        M1, CNT, M2 = (sb(n, [P, TILES, GROUPS]) for n in ("M1", "CNT", "M2"))
        GA, GR = sb("GA", [P, TILES, GROUPS + 8 - TOPG]), sb("GR", [P, TILES, GROUPS + 8 - TOPG])
        T8 = sb("T8", [P, TILES, 8])
        GM = sb("GM", [P, TILES, GROUPS])
        WS, WR = sb("WS", [P, TILES]), sb("WR", [P, TILES])
        RH = sb("RH", [P, TILES, EXPERTS], F32R)
        SP = sb("SP", [P, TILES, 2, EXPERTS])
        lg = ps("lg", [P, 2, TILES // 2, EXPERTS])
        rt = ps("rt", [P, 2, 4, P])
        s_lg, s_sig, s_v, s_tr, s_ev, s_hl = (sem("r_" + n) for n in ("lg", "sig", "v", "tr", "ev", "hl"))
        block = ctx.enter_context(nc.Block())

        @block.sync
        def _(sp):
            for k in range(RING):
                sp.dma_start(e.W[:, k, :, :].rearrange("p a b -> p (a b)"), d["w4"][k]).then_inc(e.s_ld[k], 16)

        @block.tensor
        def _(pe):
            for t in range(TILES):
                mm = nc.tensor.matmul(lg[:, t // 8, t % 8, :], g.H[:, t * P:(t + 1) * P], gate[:, :], start=True, stop=True)
                if t % 8 == 7:
                    mm.then_inc(s_lg, 1)
            for U in range(EARLY):
                k, tb = U // TBS, U % TBS
                at = slice(tb * BLK, (tb + 1) * BLK)
                pe.wait_ge(e.s_wl, k + 1)
                pe.wait_ge(s_hl, tb + 1)
                if U >= 2:
                    pe.wait_ge(e.s_silu, U - 1)
                three(nc, e.g_ps[:, tb, :], e, k, 0, g.Hh[:, at], g.Hl[:, at], True, True).then_inc(e.s_g, 1)
                three(nc, e.u_ps[:, tb, :], e, k, 1, g.Hh[:, at], g.Hl[:, at], True, True).then_inc(e.s_u, 1)
            for q in range(TILES // 4):
                pe.wait_ge(s_v, ROUTE_STEPS - 4 if q < TILES // 8 else ROUTE_STEPS)
                if q >= 2:
                    pe.wait_ge(s_ev, q - 1)
                for t in range(4):
                    mm = nc.tensor.transpose(rt[:, q % 2, t, :], SP[:, 4 * q + t, :, :], g.ident[:, :])
                mm.then_inc(s_tr, 1)

        @block.gpsimd
        def _(pool):
            for b in range(BLKS):
                cols = slice(b * BLK, (b + 1) * BLK)
                pool.wait_ge(s_sig, 2 + b + 1)
                nc.gpsimd.tensor_tensor(g.Hl[:, cols], g.H[:, cols], g.Hh[:, cols], ALU.subtract).then_inc(s_hl, 1)
                n = b
                pool.wait_ge(e.s_wh, n + 1)
                nc.gpsimd.tensor_tensor(e.WL[:, n, :, :], e.W[:, n, 0:3, :], e.WH[:, n, 0:3, :], ALU.subtract).then_inc(e.s_wl, 1)
            for U in range(EARLY):
                pool.wait_ge(e.s_silu, U + 1)
                nc.gpsimd.tensor_tensor(e.TP[:, U, :], e.SG[:, U % 2, :], e.TP[:, U, :], ALU.mult).then_inc(e.s_t, 1)

        @block.scalar
        def _(act):
            nc.scalar.preload_act_table(ACT.Sigmoid)
            for h in range(2):
                act.wait_ge(s_lg, h + 1)
                nc.scalar.activation(SC[:, 8 * h:8 * h + 8, :], lg[:, h, :, :], ACT.Sigmoid).then_inc(s_sig, 1)
            for b in range(BLKS):
                cols = slice(b * BLK, (b + 1) * BLK)
                nc.scalar.activation(g.Hh[:, cols], g.H[:, cols], ACT.Copy).then_inc(s_sig, 1)
                n = b
                act.wait_ge(e.s_ld[n], 16)
                nc.scalar.activation(e.WH[:, n, :, :], e.W[:, n, :, :], ACT.Copy).then_inc(e.s_wh, 1)
            nc.scalar.preload_act_table(ACT.Silu)
            for U in range(EARLY):
                act.wait_ge(e.s_u, U + 1)
                nc.scalar.activation(e.TP[:, U, :], e.u_ps[:, U % 2, :], ACT.Copy)
                act.wait_ge(e.s_g, U + 1)
                if U >= 2:
                    act.wait_ge(e.s_t, U - 1)
                nc.scalar.activation(e.SG[:, U % 2, :], e.g_ps[:, U % 2, :], ACT.Silu).then_inc(e.s_silu, 1)
            for q in range(TILES // 4):
                act.wait_ge(s_tr, q + 1)
                nc.scalar.activation(g.RT[:, q * BLK:(q + 1) * BLK].rearrange("p (t k) -> p t k", t=4),
                                     rt[:, q % 2, :, :], ACT.Copy).then_inc(s_ev, 1)

        @block.vector
        def _(dve):
            n = 0

            def step(ins, wait=True):
                nonlocal n
                ins.then_inc(s_v, 1)
                n += 1
                if wait:
                    dve.wait_ge(s_v, n)

            def grouped(t, T=slice(0, TILES)):
                return t[:, T, :].rearrange("p t (a b) -> p (t a) b", b=GSIZE)

            def per_group(t, T=slice(0, TILES)):
                return t[:, T, :].rearrange("p t a -> p (t a)")

            def over_group(t, T=slice(0, TILES)):
                return per_group(t, T).unsqueeze(2).broadcast_to([P, (T.stop - T.start) * GROUPS, GSIZE])

            for k in range(8 - TOPG):
                step(nc.vector.memset(GA[:, :, GROUPS + k:GROUPS + k + 1], BIG * (k + 1)), wait=False)
            for h in range(2):
                T = HALVES[h]
                dve.wait_ge(s_sig, h + 1)
                step(nc.vector.tensor_tensor(SF[:, T, :], SC[:, T, :], gbias[:, :].unsqueeze(1).broadcast_to(half_shape), ALU.add))
                step(nc.vector.tensor_reduce(per_group(M1, T), grouped(SF, T), AX.X, ALU.max))
                step(nc.vector.tensor_tensor(grouped(EQ, T), grouped(SF, T), over_group(M1, T), ALU.is_equal))
                step(nc.vector.tensor_reduce(per_group(CNT, T), grouped(EQ, T), AX.X, ALU.add))
                step(nc.vector.scalar_tensor_tensor(out=LOW[:, T, :], in0=EQ[:, T, :], scalar=-BIG, in1=SF[:, T, :],
                                                    op0=ALU.mult, op1=ALU.add))
                step(nc.vector.tensor_reduce(per_group(M2, T), grouped(LOW, T), AX.X, ALU.max))
            step(nc.vector.tensor_scalar(CNT[:, :, :], CNT[:, :, :], 2.0, -BIG, ALU.is_lt, ALU.mult))
            step(nc.vector.tensor_tensor(CNT[:, :, :], CNT[:, :, :], M1[:, :, :], ALU.add))
            step(nc.vector.tensor_tensor(M2[:, :, :], M2[:, :, :], CNT[:, :, :], ALU.max))
            step(nc.vector.tensor_tensor(GA[:, :, 0:GROUPS], M1[:, :, :], M2[:, :, :], ALU.add))
            for t in range(TILES):
                step(nc.vector.max(T8[:, t, :], GA[:, t, :]), wait=(t == TILES - 1))
            for t in range(TILES):
                step(nc.vector.match_replace(GR[:, t, :], T8[:, t, :], GA[:, t, :], -4 * BIG), wait=(t == TILES - 1))
            step(nc.vector.tensor_scalar(GM[:, :, :], GR[:, :, 0:GROUPS], -4 * BIG, None, ALU.is_equal))
            step(nc.vector.tensor_tensor(grouped(LOW), grouped(SF), over_group(GM), ALU.mult))
            step(nc.vector.tensor_scalar(LOW[:, :, :], LOW[:, :, :], 0.0, None, ALU.add))
            for t in range(TILES):
                step(nc.vector.max(T8[:, t, :], LOW[:, t, :]), wait=(t == TILES - 1))
            for t in range(TILES):
                step(nc.vector.match_replace(EQ[:, t, :], T8[:, t, :], LOW[:, t, :], -4 * BIG), wait=(t == TILES - 1))
            step(nc.vector.scalar_tensor_tensor(out=SF[:, :, :], in0=EQ[:, :, :], scalar=-4 * BIG, in1=SC[:, :, :],
                                                op0=ALU.is_equal, op1=ALU.mult))
            step(nc.vector.tensor_reduce(WS[:, :], SF[:, :, :], AX.X, ALU.add))
            step(nc.vector.tensor_scalar(WS[:, :], WS[:, :], 1e-20, None, ALU.add))
            step(nc.vector.reciprocal(WR[:, :], WS[:, :]))
            step(nc.vector.tensor_scalar(WR[:, :], WR[:, :], 2.5, None, ALU.mult))
            for h in range(2):
                T = HALVES[h]
                step(nc.vector.tensor_tensor(SF[:, T, :], SF[:, T, :], WR[:, T].unsqueeze(2).broadcast_to(half_shape), ALU.mult))
                step(nc.vector.tensor_copy(RH[:, T, :], SF[:, T, :]))
                step(nc.vector.tensor_copy(SP[:, T, 0, :], RH[:, T, :]), wait=False)
                step(nc.vector.tensor_tensor(SP[:, T, 1, :], SF[:, T, :], RH[:, T, :], ALU.subtract), wait=(h == 1))
            assert n == ROUTE_STEPS, n


ROUTE_STEPS = 100


def stage_experts(nc, d, g, e):
    LAG = 2
    LOOPS, REST = CHUNKS // RING, CHUNKS % RING
    ALL = 2 * CHUNKS
    SHARED_UNITS = 2 * TBS
    with ExitStack() as ctx:
        sb, ps, sem = alloc(nc, ctx)
        W, WH, WL = e.W, e.WH, e.WL
        zero = sb("zero", [P, BLK], BF16)
        SG, TT = e.SG, sb("TT", [P, 2, BLK])
        HH = sb("HH", [P, 4, BLK])
        HHh, HHl = (sb(n, [P, 4, BLK], F32R) for n in ("HHh", "HHl"))
        g_ps, u_ps = e.g_ps, e.u_ps
        rb_ps, acc = ps("rb_ps", [P, 2, BLK]), ps("acc", [P, 2, BLK])
        s_ld, s_wh, s_wl = e.s_ld, e.s_wh, e.s_wl
        s_g, s_u, s_silu, s_t = e.s_g, e.s_u, e.s_silu, e.s_t
        s_z, s_rb, s_hh, s_hi, s_lo, s_down, s_out = (
            sem("e_" + n) for n in ("z", "rb", "hh", "hi", "lo", "down", "out"))

        def runs(eng, body):
            for half in range(2):
                n0 = half * CHUNKS

                def one(i, k):
                    body(half, i * RING + (n0 + k), (n0 + k) % RING, i + (n0 + k) // RING,
                         i * RING + k if isinstance(i, int) else None)
                for k in range(RING):
                    one(0, k)
                with eng.Fori(1, LOOPS) as i:
                    for k in range(RING):
                        one(i, k)
                for k in range(REST):
                    one(LOOPS, k)

        def cols(half, tb):
            return slice((half * TBS + tb) * BLK, (half * TBS + tb + 1) * BLK)

        def early(U, n):
            return isinstance(U, int) and U < n

        def shared(c):
            return c is not None and c >= CHUNKS - 2

        block = ctx.enter_context(nc.Block())

        @block.sync
        def _(sp):
            def body(half, n, k, uses, c):
                if early(n, RING):
                    return
                sp.wait_ge(s_wl, n - (RING - 1))
                sp.dma_start(W[:, k, :, :].rearrange("p a b -> p (a b)"),
                             d["w4"][bass.ds(n - half * CHUNKS, 1), :, :].rearrange("o p n -> (o p) n")).then_inc(s_ld[k], 16)
            runs(sp, body)

        @block.gpsimd
        def _(pool):
            def body(half, n, k, uses, c):
                if early(n, RING):
                    return
                pool.wait_ge(s_wh, n + 1)
                nc.gpsimd.tensor_tensor(WL[:, k, :, :], W[:, k, 0:3, :], WH[:, k, 0:3, :], ALU.subtract).then_inc(s_wl, 1)
            runs(pool, body)

        @block.tensor
        def _(pe):
            def down(U, k, tb):
                j = (2 * k + tb) % 4
                pe.wait_ge(s_lo, U + 1)
                three(nc, acc[:, tb, :], e, k, 2, HHh[:, j, :], HHl[:, j, :], False, False).then_inc(s_down, 1)

            def open_sums(half):
                if half == 0:
                    pe.wait_ge(s_z, 1)
                else:
                    pe.wait_ge(s_out, TBS)
                for tb in range(TBS):
                    nc.tensor.matmul(acc[:, tb, :], zero[:, 0:P], zero[:, :], start=True, stop=False, skip_group_check=True)

            def body(half, n, k, uses, c):
                for tb in range(TBS):
                    U = n * TBS + tb
                    if tb == 0:
                        pe.wait_ge(s_wh, n + 1)
                        pe.wait_ge(s_wl, n + 1)
                    hi, lo = g.Hh[:, cols(half, tb)], g.Hl[:, cols(half, tb)]
                    if not early(U, EARLY):
                        pe.wait_ge(s_silu, U - 1)
                        three(nc, g_ps[:, tb, :], e, k, 0, hi, lo, True, True).then_inc(s_g, 1)
                        pe.wait_ge(s_t, U - 1)
                        three(nc, u_ps[:, tb, :], e, k, 1, hi, lo, True, True).then_inc(s_u, 1)
                    if not shared(c):
                        if not early(U, 2):
                            pe.wait_ge(s_hh, U - 1)
                        nc.tensor.matmul(rb_ps[:, tb, :], WH[:, k, 3, :], g.RT[:, cols(half, tb)],
                                         start=True, stop=True).then_inc(s_rb, 1)
                    if c == 1 and tb == 0:
                        open_sums(half)
                    if not early(U, LAG):
                        down(U - LAG, (k - 1) % RING, tb)

            runs(pe, body)
            for tb in range(TBS):
                down((ALL - 1) * TBS + tb, (ALL - 1) % RING, tb)

        @block.scalar
        def _(act):
            nc.scalar.preload_act_table(ACT.Silu)

            def round_weights(n, k, uses):
                act.wait_ge(s_ld[k], (uses + 1) * 16)
                if not early(n, RING):
                    act.wait_ge(s_down, (n - (RING - 1)) * TBS)
                nc.scalar.activation(WH[:, k, :, :], W[:, k, :, :], ACT.Copy).then_inc(s_wh, 1)

            def high(U, j):
                act.wait_ge(s_hh, U + 1)
                if not early(U, 4):
                    act.wait_ge(s_down, U - 3)
                nc.scalar.activation(HHh[:, j, :], HH[:, j, :], ACT.Copy).then_inc(s_hi, 1)

            def take_sums(half):
                act.wait_ge(s_down, (half + 1) * CHUNKS * TBS)
                for tb in range(TBS):
                    nc.scalar.activation(g.Y[:, cols(half, tb)], acc[:, tb, :], ACT.Copy).then_inc(s_out, 1)

            def body(half, n, k, uses, c):
                for tb in range(TBS):
                    U, j = n * TBS + tb, (2 * k + tb) % 4
                    if not early(U, EARLY):
                        act.wait_ge(s_g, U + 1)
                        act.wait_ge(s_t, U - 1)
                        nc.scalar.activation(SG[:, tb, :], g_ps[:, tb, :], ACT.Silu).then_inc(s_silu, 1)
                    if not early(U, 1):
                        high(U - 1, (j - 1) % 4)
                    if tb == 0 and not (isinstance(n, int) and (n >= ALL - AHEAD or n < RING - AHEAD)):
                        round_weights(n + AHEAD, (k + AHEAD) % RING, uses + (k + AHEAD) // RING)
                    if tb == 0 and c == 1 and half == 1:
                        take_sums(0)

            runs(act, body)
            high(ALL * TBS - 1, 3)
            take_sums(1)

        @block.vector
        def _(dve):
            nc.vector.memset(zero[:, :], 0.0).then_inc(s_z, 1)

            def low(U, j):
                dve.wait_ge(s_hi, U + 1)
                if not early(U, 4):
                    dve.wait_ge(s_down, U - 3)
                nc.vector.tensor_tensor(HHl[:, j, :], HH[:, j, :], HHh[:, j, :], ALU.subtract).then_inc(s_lo, 1)

            def body(half, n, k, uses, c):
                for tb in range(TBS):
                    U, j = n * TBS + tb, (2 * k + tb) % 4
                    source = TT[:, tb, :]
                    if early(U, EARLY):
                        source = e.TP[:, U, :]
                    else:
                        dve.wait_ge(s_silu, U + 1)
                        dve.wait_ge(s_u, U + 1)
                        nc.vector.tensor_tensor(source, SG[:, tb, :], u_ps[:, tb, :], ALU.mult).then_inc(s_t, 1)
                    if not early(U, 1):
                        low(U - 1, (j - 1) % 4)
                    dve.wait_ge(s_t, U + 1)
                    if shared(c):
                        nc.vector.tensor_copy(HH[:, j, :], source).then_inc(s_hh, 1)
                    else:
                        dve.wait_ge(s_rb, U + 1 - half * SHARED_UNITS)
                        nc.vector.tensor_tensor(HH[:, j, :], source, rb_ps[:, tb, :], ALU.mult).then_inc(s_hh, 1)

            runs(dve, body)
            low(ALL * TBS - 1, 3)


def stage_moe(nc, d, g, r):
    with ExitStack() as ctx:
        sb, _, _ = alloc(nc, ctx)
        g.RT = sb("RT", [P, TOK], F32R)
        g.Hh, g.Hl = sb("Hh", [P, TOK], F32R), sb("Hl", [P, TOK], F32R)
        _, ps, sem = alloc(nc, ctx)
        e = Shared()
        e.W = sb("W", [P, RING, 4, P])
        e.WH, e.WL = sb("WH", [P, RING, 4, P], F32R), sb("WL", [P, RING, 3, P], F32R)
        e.s_ld = [sem(f"e_ld{k}") for k in range(RING)]
        e.s_wh, e.s_wl, e.s_g, e.s_u, e.s_silu, e.s_t = (sem("e_" + n) for n in ("wh", "wl", "g", "u", "silu", "t"))
        e.SG, e.TP = sb("SG", [P, 2, BLK]), sb("TP", [P, EARLY, BLK])
        e.g_ps, e.u_ps = ps("g_ps", [P, 2, BLK]), ps("u_ps", [P, 2, BLK])
        stage_route(nc, d, g, r, e)
        stage_experts(nc, d, g, e)


W2 = SEQ + CONVPAD
DIRS = 2


def mamba_loads(d, g, sb, sem):
    m = Shared()
    m.wx, m.cw = sb("wx", [P, DIRS, 3 * P]), sb("cw", [P, DIRS, 2, 3 * P])
    m.wz, m.wdt = sb("wz", [P, DIRS, P]), sb("wdt", [P, 4])
    m.wzh, m.wzl = (sb(n, [P, DIRS, P], F32R) for n in ("wzh", "wzl"))
    m.cb, m.dtb, m.al = sb("cb", [P, DIRS, 3]), sb("dtb", [P, 4]), sb("al", [P, 4])
    m.tri, m.wp, m.op = sb("tri", [P, 4, P]), sb("wp", [P, DIRS, HD]), sb("op", [P, P])
    m.U2l = sb("U2l", [P, DIRS, BATCH, W2], F32R)
    m.U2 = m.U2l[:, :, :, :].bitcast(F32)
    m.s_u2 = [sem(f"m_u2{b}") for b in range(BATCH)]
    m.copies = []
    for b in range(BATCH):
        t0, blocks = b * SEQ, (b + 1) * SEQ // BLK
        m.copies += [(blocks, m.U2[0:HD, 0, b, 3:3 + SEQ], g.U[0:HD, t0:t0 + SEQ], m.s_u2[b]),
                     (blocks, m.U2[HD:P, 0, b, 4:3 + SEQ], g.U[0:HD, t0:t0 + SEQ - 1], m.s_u2[b]),
                     (blocks, m.U2[0:HD, 1, b, 0:SEQ], g.U[HD:P, t0:t0 + SEQ], m.s_u2[b]),
                     (blocks, m.U2[HD:P, 1, b, 0:SEQ - 1], g.U[HD:P, t0 + 1:t0 + SEQ], m.s_u2[b])]
    return m, [(m.wx[:, :, :], d["wxbc"]), (m.cw[:, :, :, :], d["cw"]), (m.wz[:, :, :], d["wz"]), (m.wdt[:, :], d["wdt"]),
               (m.cb[:, :, :], d["cb"]), (m.dtb[:, :], d["dtb"]), (m.al[:, :], d["alog"]), (m.tri[:, :, :], d["tri"]),
               (m.wp[:, :, :], d["wp"]), (m.op[:, :], d["opT"])]


def stage_mamba_project(nc, g, m):
    with ExitStack() as ctx:
        sb, ps, sem = alloc(nc, ctx)
        U2h = sb("U2h", [P, DIRS, BATCH, W2], F32R)
        U2, U2l = m.U2, m.U2l
        wch, wcl = (sb(n, [P, DIRS, 2, 3 * P], F32R) for n in ("wch", "wcl"))
        wc = sb("wc", [P, DIRS, 2, 3 * P])
        wx, cw, wdt, cb, dtb, al = m.wx, m.cw, m.wdt, m.cb, m.dtb, m.al
        A = sb("A", [P, 4])
        shape = [P, TILES, 4]
        VV, NV, E, W1, DD, IZ, LN = (sb(n, shape) for n in ("VV", "NV", "E", "W1", "DD", "IZ", "LN"))
        job_ps = ps("job_ps", [P, 4, BLK])
        dt_ps = ps("dt_ps", shape)
        sum_ps = ps("sum_ps", [P, 3, 4, TILES])
        s_u2h, s_u2l, s_wch, s_wcl = (sem("p_" + n) for n in ("u2h", "u2l", "wch", "wcl"))
        s_pad, s_wc, s_dt, s_v, s_act, s_job, s_ev, s_sum = (
            sem("p_" + n) for n in ("pad", "wc", "dt", "v", "act", "job", "ev", "sum"))
        JOBS = 4 * DIRS
        SHIFT = (3, 0)
        FAR = (-2, 2)
        block = ctx.enter_context(nc.Block())

        def blocks(eng, body):
            with eng.Fori(0, BATCH) as b:
                with eng.Fori(0, SEQ // BLK) as h:
                    for j in range(JOBS):
                        body(b, h, j, (b * (SEQ // BLK) + h) * JOBS + j)

        @block.gpsimd
        def _(pool):
            nc.gpsimd.memset(U2[0:HD, 0, :, 0:3], 0.0).then_inc(s_pad, 1)
            nc.gpsimd.memset(U2[HD:P, 0, :, 0:4], 0.0).then_inc(s_pad, 1)
            nc.gpsimd.memset(U2[0:HD, 1, :, SEQ:W2], 0.0).then_inc(s_pad, 1)
            nc.gpsimd.memset(U2[HD:P, 1, :, SEQ - 1:W2], 0.0).then_inc(s_pad, 1)
            pool.wait_ge(s_pad, 4)
            nc.gpsimd.memset(U2[:, 0, :, 3 + SEQ:W2], 0.0).then_inc(s_pad, 1)

        @block.tensor
        def _(pe):
            for t in range(TILES):
                mm = nc.tensor.matmul(dt_ps[:, t, :], g.U[:, t * P:(t + 1) * P], wdt[:, :], start=True, stop=True)
            mm.then_inc(s_dt, 1)
            pe.wait_ge(s_wcl, 1)

            def job(b, h, j, J):
                dr, c = j // 4, j % 4
                if j == 0:
                    pe.wait_ge(s_u2l, b * DIRS + DIRS)
                pe.wait_ge(s_ev, J + 1)
                base = dr * BATCH * W2 + SHIFT[dr]
                high, low = (t[:, :, :, :].rearrange("p a b c -> p (a b c)") for t in (U2h, U2l))
                pairs = 2 if c < 3 else 1
                for q in range(pairs):
                    wh, wl = ((wch[:, dr, q, c * P:(c + 1) * P], wcl[:, dr, q, c * P:(c + 1) * P]) if c < 3 else
                              (m.wzh[:, dr, :], m.wzl[:, dr, :]))
                    at = bass.ds(b * W2 + h * BLK + (base + q * FAR[dr]), BLK)
                    nc.tensor.matmul(job_ps[:, j % 4, :], wh, high[:, at], start=(q == 0), stop=False)
                    nc.tensor.matmul(job_ps[:, j % 4, :], wh, low[:, at], start=False, stop=False)
                    mm = nc.tensor.matmul(job_ps[:, j % 4, :], wl, high[:, at], start=False, stop=(q == pairs - 1))
                mm.then_inc(s_job, 1)

            blocks(pe, job)
            pe.wait_ge(s_v, PROJECT_STEPS)
            for k in range(2):
                for dr in range(DIRS):
                    nc.tensor.matmul(sum_ps[:, k, 2 * dr:2 * dr + 2, :], m.tri[:, 2 * dr + k, :],
                                     m.AA[:, :, 2 * dr:2 * dr + 2].rearrange("p t h -> p h t"), start=True, stop=True)
            nc.tensor.matmul(sum_ps[:, 2, :, :], g.ones[:, :], m.AA[:, :, :].rearrange("p t h -> p h t"),
                             start=True, stop=True).then_inc(s_sum, 1)

        @block.scalar
        def _(act):
            act.sem_inc(s_ev, 4)
            act.wait_ge(s_wc, 1)
            nc.scalar.activation(wch[:, :, :, :], wc[:, :, :, :], ACT.Copy).then_inc(s_wch, 1)
            act.wait_ge(s_pad, 5)
            for b in range(BATCH):
                act.wait_ge(m.s_u2[b], 64)
                for dr in range(DIRS):
                    nc.scalar.activation(U2h[:, dr, b, :], U2[:, dr, b, :], ACT.Copy).then_inc(s_u2h, 1)
            nc.scalar.activation(m.trir[:, :, :], m.tri[:, :, :], ACT.Copy)
            nc.scalar.activation(A[:, :], al[:, :], ACT.Exp).then_inc(s_act, 1)
            act.wait_ge(s_v, 3)
            nc.scalar.activation(E[:, :, :], NV[:, :, :], ACT.Exp).then_inc(s_act, 1)
            act.wait_ge(s_v, 4)
            nc.scalar.activation(LN[:, :, :], W1[:, :, :], ACT.Ln).then_inc(s_act, 1)
            nc.scalar.preload_act_table(ACT.Silu)

            def job(b, h, j, J):
                dr, c = j // 4, j % 4
                act.wait_ge(s_job, J + 1)
                at = bass.ds(b * SEQ + h * BLK, BLK)
                if c < 3:
                    nc.scalar.activation(m.XBC[:, dr, c, at], job_ps[:, j % 4, :], ACT.Silu, bias=cb[:, dr, c:c + 1]).then_inc(s_ev, 1)
                else:
                    nc.scalar.activation(m.SZ[:, dr, at], job_ps[:, j % 4, :], ACT.Silu).then_inc(s_ev, 1)

            blocks(act, job)
            act.wait_ge(s_sum, 1)
            nc.scalar.activation(m.EX[:, :, :, :], sum_ps[:, :, :, :], ACT.Exp).then_inc(s_act, 1)

        @block.vector
        def _(dve):
            n = 0

            def step(ins):
                nonlocal n
                ins.then_inc(s_v, 1)
                n += 1
                dve.wait_ge(s_v, n)

            for dr in range(DIRS):
                mm = nc.vector.tensor_tensor(wc[:, dr, :, :], cw[:, dr, :, :],
                                             wx[:, dr, :].unsqueeze(1).broadcast_to([P, 2, 3 * P]), ALU.mult)
            mm.then_inc(s_wc, 1)
            dve.wait_ge(s_wch, 1)
            nc.vector.tensor_tensor(wcl[:, :, :, :], wc[:, :, :, :], wch[:, :, :, :], ALU.subtract).then_inc(s_wcl, 1)
            for b in range(BATCH):
                for dr in range(DIRS):
                    dve.wait_ge(s_u2h, b * DIRS + dr + 1)
                    nc.vector.tensor_tensor(U2l[:, dr, b, :], U2[:, dr, b, :], U2h[:, dr, b, :], ALU.subtract).then_inc(s_u2l, 1)
            dve.wait_ge(s_dt, 1)
            step(nc.vector.tensor_tensor(VV[:, :, :], dt_ps[:, :, :], dtb[:, :].unsqueeze(1).broadcast_to(shape), ALU.add))
            step(nc.vector.tensor_scalar(NV[:, :, :], VV[:, :, :], -1.0, None, ALU.mult))
            step(nc.vector.tensor_tensor(NV[:, :, :], NV[:, :, :], VV[:, :, :], ALU.min))
            dve.wait_ge(s_act, 2)
            step(nc.vector.tensor_scalar(W1[:, :, :], E[:, :, :], 1.0, None, ALU.add))
            step(nc.vector.tensor_scalar(DD[:, :, :], W1[:, :, :], -1.0, None, ALU.add))
            step(nc.vector.tensor_scalar(IZ[:, :, :], DD[:, :, :], 0.0, None, ALU.is_equal))
            step(nc.vector.tensor_tensor(DD[:, :, :], DD[:, :, :], IZ[:, :, :], ALU.add))
            step(nc.vector.reciprocal(DD[:, :, :], DD[:, :, :]))
            dve.wait_ge(s_act, 3)
            step(nc.vector.tensor_tensor(LN[:, :, :], LN[:, :, :], IZ[:, :, :], ALU.add))
            step(nc.vector.tensor_tensor(LN[:, :, :], LN[:, :, :], E[:, :, :], ALU.mult))
            step(nc.vector.tensor_tensor(LN[:, :, :], LN[:, :, :], DD[:, :, :], ALU.mult))
            step(nc.vector.scalar_tensor_tensor(out=m.DT[:, :, :], in0=VV[:, :, :], scalar=0.0, in1=LN[:, :, :],
                                                op0=ALU.max, op1=ALU.add))
            step(nc.vector.scalar_tensor_tensor(out=m.AA[:, :, :], in0=m.DT[:, :, :], scalar=-1.0,
                                                in1=A[:, :].unsqueeze(1).broadcast_to(shape), op0=ALU.mult, op1=ALU.mult))
            step(nc.vector.tensor_copy(m.A2[:, :, 0, :], m.AA[:, :, :]))
            step(nc.vector.tensor_tensor(m.A2[:, :, 1, :], m.AA[:, :, :], m.A2[:, :, 0, :], ALU.subtract))
            assert n == PROJECT_STEPS


PROJECT_STEPS = 15


def stage_mamba_scan(nc, g, m):
    SEQS, STEPS = DIRS * BATCH, SEQ // P
    with ExitStack() as ctx:
        sb, ps, sem = alloc(nc, ctx)
        CP = sb("CP", [P, SEQS, 3, P])
        AR = sb("AR", [P, 2, 2, 2, P], F32R)
        ED = sb("ED", [P, SEQS, 2, P])
        BT = sb("BT", [P, SEQS, P])
        GM = sb("GMt", [P, 2, P])
        MT = sb("MT", [P, 2, 2, P])
        DX, DS = sb("DX", [P, 2, 2, HD]), sb("DS", [P, 2, 2, HD])
        YT = sb("YT", [P, 2, 2, HD])
        HST, HD1 = sb("HST", [P, SEQS, 2, HD]), sb("HD1", [P, 2, 2, HD])
        t_ps = ps("t_ps", [P, 2, 4, P])
        d_ps = ps("dd_ps", [P, 2, 4, P])
        y_ps = ps("y_ps", [P, 2, 4, P])
        yt_ps = ps("yt_ps", [P, 2, 4, P])
        (s_z, s_cp, s_ar, s_t, s_d, s_ed, s_bt, s_gm, s_dx, s_ds, s_mt, s_y, s_y1, s_y2, s_h1, s_h2, s_yt, s_yev) = (
            sem("s_" + n) for n in ("z", "cp", "ar", "t", "d", "ed", "bt", "gm", "dx", "ds", "mt", "y", "y1", "y2", "h1",
                                    "h2", "yt", "yev"))
        block = ctx.enter_context(nc.Block())

        def early(U, n=2):
            return isinstance(U, int) and U < n

        def tile(i, q):
            dr, b = q // BATCH, q % BATCH
            return i + b * STEPS if dr == 0 else i * -1 + (b * STEPS + STEPS - 1)

        def at(i, q, n=P):
            return bass.ds(tile(i, q) * n, n)

        def units(eng, body, tail):
            def step(i):
                for q in range(SEQS):
                    body(i, q, i * SEQS + q)
            step(0)
            with eng.Fori(1, STEPS) as i:
                step(i)
            tail()

        def ahead(i, q):
            return (i, q + 1) if q + 1 < SEQS else (i + 1, 0)

        def back(i, q, n):
            return (i, q - n) if q >= n else (i - 1, q - n + SEQS)

        def heads(i, q, kind):
            dr = q // BATCH
            return m.EX[:, kind, 2 * dr:2 * dr + 2, bass.ds(tile(i, q), 1)].broadcast_to([P, 2, HD])

        LAST = (STEPS - 1, SEQS - 1)

        @block.scalar
        def _(act):
            nc.scalar.preload_act_table(ACT.Exp)

            def copy(i, q, U):
                if not early(U, SEQS):
                    act.wait_ge(s_y, U - (SEQS - 1))
                nc.scalar.activation(CP[:, q, :, :], m.XBC[:, q // BATCH, :, at(i, q)], ACT.Copy).then_inc(s_cp, 1)

            def body(i, q, U):
                if early(U, 1):
                    copy(i, q, U)
                copy(*ahead(i, q), U + 1)
                if not early(U, 3):
                    take_y(*back(i, q, 3), U - 3)
                act.wait_ge(s_d, U + 1)
                if not early(U, SEQS):
                    act.wait_ge(s_mt, U - (SEQS - 1))
                    act.wait_ge(s_y, U - (SEQS - 1))
                nc.scalar.activation(ED[:, q, :, :], d_ps[:, q % 2, 0:2, :], ACT.Exp).then_inc(s_ed, 1)
                nc.scalar.activation(BT[:, q, :], d_ps[:, q % 2, 2, :], ACT.Copy).then_inc(s_bt, 1)

            def take_y(i, q, U):
                act.wait_ge(s_yt, U + 1)
                nc.scalar.activation(m.YB[:, q // BATCH, at(i, q)], yt_ps[:, q % 2, 0, :], ACT.Copy).then_inc(s_yev, 1)

            def tail():
                for n in (2, 1, 0):
                    i, q = back(*LAST, n)
                    take_y(i, q, i * SEQS + q)

            units(act, body, tail)

        @block.gpsimd
        def _(pool):
            def decays(i, q, U):
                dr = q // BATCH
                if not early(U):
                    pool.wait_ge(s_d, U - 1)
                shape = [P, 2, 2, P]
                nc.gpsimd.tensor_tensor(AR[:, q % 2, :, :, :], m.tri[:, 2 * dr, :].unsqueeze(1).unsqueeze(1).broadcast_to(shape),
                                        m.A2[:, bass.ds(tile(i, q), 1), :, 2 * dr:2 * dr + 2].rearrange("p o c h -> p c h o")
                                        .broadcast_to(shape), ALU.mult).then_inc(s_ar, 1)

            def body(i, q, U):
                if early(U, 1):
                    decays(i, q, U)
                decays(*ahead(i, q), U + 1)
                pool.wait_ge(s_dx, U + 1)
                if not early(U):
                    pool.wait_ge(s_y, U - 1)
                nc.gpsimd.tensor_tensor(DS[:, q % 2, :, :], DX[:, q % 2, :, :], heads(i, q, 1), ALU.mult).then_inc(s_ds, 1)
            units(pool, body, lambda: None)

        @block.tensor
        def _(pe):
            def phase1(i, q, U):
                dr, k = q // BATCH, q % 2
                pe.wait_ge(s_cp, U + 1)
                if not early(U):
                    pe.wait_ge(s_dx, U - 1)
                nc.tensor.transpose(t_ps[:, k, 0, :], CP[:, q, 0, :], g.ident[:, :])
                nc.tensor.matmul(t_ps[:, k, 1, :], CP[:, q, 1, :], CP[:, q, 2, :], start=True, stop=True).then_inc(s_t, 1)
                pe.wait_ge(s_ar, U + 1)
                if not early(U):
                    pe.wait_ge(s_bt, U - 1)
                for part in range(2):
                    nc.tensor.matmul(d_ps[:, k, 0:2, :], m.trir[:, 2 * dr + 1, :], AR[:, k, part, :, :],
                                     start=(part == 0), stop=(part == 1))
                nc.tensor.transpose(d_ps[:, k, 2, :], CP[:, q, 1, :], g.ident[:, :]).then_inc(s_d, 1)

            def phase2(i, q, U):
                k = q % 2
                pe.wait_ge(s_mt, U + 1)
                pe.wait_ge(s_ds, U + 1)
                pe.wait_ge(s_bt, U + 1)
                if early(U, SEQS):
                    pe.wait_ge(s_z, 1)
                if not early(U):
                    pe.wait_ge(s_h2, U - 1)
                for h in range(2):
                    nc.tensor.matmul(y_ps[:, k, 0, h * HD:(h + 1) * HD], MT[:, k, h, :], DX[:, k, h, :], start=True, stop=True)
                nc.tensor.matmul(y_ps[:, k, 1, :], CP[:, q, 2, :], HST[:, q, :, :], start=True, stop=True)
                nc.tensor.matmul(y_ps[:, k, 2, :], BT[:, q, :], DS[:, k, :, :], start=True, stop=True).then_inc(s_y, 1)

            def turn(i, q, U):
                k = q % 2
                pe.wait_ge(s_y2, U + 1)
                if not early(U):
                    pe.wait_ge(s_yev, U - 1)
                nc.tensor.transpose(yt_ps[:, k, 0, :], YT[:, k, :, :], g.ident[:, :]).then_inc(s_yt, 1)

            def body(i, q, U):
                phase1(i, q, U)
                if not early(U, 1):
                    phase2(*back(i, q, 1), U - 1)
                if not early(U):
                    turn(*back(i, q, 2), U - 2)

            def tail():
                i, q = LAST
                U = i * SEQS + q
                phase2(i, q, U)
                turn(*back(i, q, 1), U - 1)
                turn(i, q, U)

            units(pe, body, tail)

        @block.vector
        def _(dve):
            nc.vector.memset(HST[:, :, :, :], 0.0).then_inc(s_z, 1)

            def body(i, q, U):
                dr, k = q // BATCH, q % 2
                dve.wait_ge(s_t, U + 1)
                nc.vector.tensor_tensor(GM[:, k, :], t_ps[:, k, 1, :], m.tri[:, 2 * dr, :], ALU.mult).then_inc(s_gm, 1)
                if not early(U):
                    dve.wait_ge(s_y, U - 1)
                    dve.wait_ge(s_ds, U - 1)
                nc.vector.tensor_tensor(DX[:, k, :, :], t_ps[:, k, 0, :].rearrange("p (h c) -> p h c", h=2),
                                        m.DT[:, bass.ds(tile(i, q), 1), 2 * dr:2 * dr + 2].rearrange("p o h -> p h o")
                                        .broadcast_to([P, 2, HD]), ALU.mult).then_inc(s_dx, 1)
                dve.wait_ge(s_ed, U + 1)
                dve.wait_ge(s_gm, U + 1)
                nc.vector.tensor_tensor(MT[:, k, :, :], ED[:, q, :, :], GM[:, k, :].unsqueeze(1).broadcast_to([P, 2, P]),
                                        ALU.mult).then_inc(s_mt, 1)
                if not early(U, 1):
                    result(*back(i, q, 1), U - 1)

            def result(i, q, U):
                k = q % 2
                dve.wait_ge(s_y, U + 1)
                if not early(U):
                    dve.wait_ge(s_yt, U - 1)
                two = lambda n: y_ps[:, k, n, :].rearrange("p (h c) -> p h c", h=2)
                nc.vector.tensor_tensor(YT[:, k, :, :], two(1), heads(i, q, 0), ALU.mult).then_inc(s_y1, 1)
                nc.vector.tensor_tensor(HD1[:, k, :, :], HST[:, q, :, :], heads(i, q, 2), ALU.mult).then_inc(s_h1, 1)
                dve.wait_ge(s_y1, U + 1)
                nc.vector.tensor_tensor(YT[:, k, :, :], two(0), YT[:, k, :, :], ALU.add).then_inc(s_y2, 1)
                dve.wait_ge(s_h1, U + 1)
                nc.vector.tensor_tensor(HST[:, q, :, :], two(2), HD1[:, k, :, :], ALU.add).then_inc(s_h2, 1)

            def tail():
                result(*LAST, STEPS * SEQS - 1)

            units(dve, body, tail)


def stage_mamba_output(nc, g, m):
    with ExitStack() as ctx:
        sb, ps, sem = alloc(nc, ctx)
        wp, op = m.wp, m.op
        YG = sb("YG", [P, DIRS, TOK])
        SQ = sb("oSQ", [P, 2, BLK])
        CAT = sb("CAT", [P, 2, BLK])
        ms_ps, r_ps = ps("oms", [P, 2, BLK]), ps("or", [P, 2, BLK])
        cat_ps, o_ps = ps("cat_ps", [P, 2, BLK]), ps("oo_ps", [P, 2, BLK])
        s_dl = sem("o_dl")
        s_g1, s_g2, s_sq, s_ms, s_st, s_r, s_b, s_yn, s_cat, s_cc, s_o, s_out = (
            sem("o_" + n) for n in ("g1", "g2", "sq", "ms", "st", "r", "b", "yn", "cat", "cc", "o", "out"))
        ITEMS = DIRS * BLKS
        TB = BLK // P
        ST, R = sb("oST", [P, ITEMS, TB]), sb("oR", [P, ITEMS, TB])
        RH, RL = sb("oRH", [P, ITEMS, TB], F32R), sb("oRL", [P, ITEMS, TB], F32R)
        DH, DL = sb("oDH", [P, 2, TB, P], F32R), sb("oDL", [P, 2, TB, P], F32R)
        GN, DS = (g.vec["gn_f"], g.vec["gn_b"]), (g.vec["D_f"], g.vec["D_b"])

        def cols(n):
            return slice((n // 2) * BLK, (n // 2 + 1) * BLK)

        def steps(*jobs):
            for i in range(ITEMS + 6):
                for job, lag in jobs:
                    if 0 <= i - lag < ITEMS:
                        job(i - lag)
        block = ctx.enter_context(nc.Block())

        @block.tensor
        def _(pe):
            def mean_square(n):
                pe.wait_ge(s_sq, n + 1)
                if n >= 2:
                    pe.wait_ge(s_st, n - 1)
                for t in range(TB):
                    mm = nc.tensor.matmul(ms_ps[:, n % 2, t:t + 1], SQ[:, n % 2, t * P:(t + 1) * P], g.mean_col[:, :],
                                          start=True, stop=True)
                mm.then_inc(s_ms, 1)

            def broadcast(n):
                if n >= 2:
                    pe.wait_ge(s_yn, n - 1)
                pe.wait_ge(s_r, 4 * (n + 1))
                nc.tensor.matmul(r_ps[:, n % 2, :], g.onesr[:, :], DH[:, n % 2, :, :], start=True, stop=False)
                pe.wait_ge(s_dl, n + 1)
                nc.tensor.matmul(r_ps[:, n % 2, :], g.onesr[:, :], DL[:, n % 2, :, :], start=False, stop=True).then_inc(s_b, 1)

            def project(n):
                blk, dr = n // 2, n % 2
                pe.wait_ge(s_yn, n + 1)
                if blk >= 2 and dr == 0:
                    pe.wait_ge(s_cc, blk - 1)
                nc.tensor.matmul(cat_ps[dr * HD:(dr + 1) * HD, blk % 2, :], wp[:, dr, :], YG[:, dr, cols(n)],
                                 start=True, stop=True).then_inc(s_cat, 1)

            def combine(n):
                blk = n // 2
                if n % 2:
                    pe.wait_ge(s_cc, blk + 1)
                    if blk >= 2:
                        pe.wait_ge(s_out, blk - 1)
                    nc.tensor.matmul(o_ps[:, blk % 2, :], op[:, :], CAT[:, blk % 2, :], start=True, stop=True).then_inc(s_o, 1)

            steps((mean_square, 1), (broadcast, 2), (project, 3), (combine, 4))

        @block.scalar
        def _(act):
            nc.scalar.preload_act_table(ACT.Sqrt)

            def square(n):
                act.wait_ge(s_g2, n + 1)
                if n >= 2:
                    act.wait_ge(s_ms, n - 1)
                nc.scalar.activation(SQ[:, n % 2, :], YG[:, n % 2, cols(n)], ACT.Square).then_inc(s_sq, 1)

            def root(n):
                act.wait_ge(s_ms, n + 1)
                nc.scalar.activation(ST[:, n, :], ms_ps[:, n % 2, 0:TB], ACT.Sqrt, bias=g.eps5).then_inc(s_st, 1)

            def take_cat(n):
                blk = n // 2
                if n % 2:
                    act.wait_ge(s_cat, n + 1)
                    if blk >= 2:
                        act.wait_ge(s_o, blk - 1)
                    nc.scalar.activation(CAT[:, blk % 2, :], cat_ps[:, blk % 2, :], ACT.Copy).then_inc(s_cc, 1)

            steps((square, 0), (root, 1), (take_cat, 3))

        @block.gpsimd
        def _(pool):
            def gate(n):
                dr = n % 2
                pool.wait_ge(s_g1, n + 1)
                nc.gpsimd.tensor_tensor(YG[:, dr, cols(n)], YG[:, dr, cols(n)], m.SZ[:, dr, cols(n)], ALU.mult).then_inc(s_g2, 1)

            def diagonal(n):
                pool.wait_ge(s_r, 4 * n + 3)
                if n >= 2:
                    pool.wait_ge(s_b, n - 1)
                nc.gpsimd.tensor_tensor(DL[:, n % 2, :, :], g.ident[:, :].unsqueeze(1).broadcast_to([P, TB, P]),
                                        RL[:, n, :].unsqueeze(2).broadcast_to([P, TB, P]), ALU.mult).then_inc(s_dl, 1)

            steps((gate, 0), (diagonal, 2))

        @block.vector
        def _(dve):
            def skip(n):
                dr = n % 2
                nc.vector.scalar_tensor_tensor(out=YG[:, dr, cols(n)], in0=m.XBC[:, dr, 0, cols(n)], scalar=DS[dr],
                                               in1=m.YB[:, dr, cols(n)], op0=ALU.mult, op1=ALU.add).then_inc(s_g1, 1)

            def inverse(n):
                dve.wait_ge(s_st, n + 1)
                nc.vector.reciprocal(R[:, n, :], ST[:, n, :]).then_inc(s_r, 1)
                dve.wait_ge(s_r, 4 * n + 1)
                nc.vector.tensor_copy(RH[:, n, :], R[:, n, :]).then_inc(s_r, 1)
                dve.wait_ge(s_r, 4 * n + 2)
                nc.vector.tensor_tensor(RL[:, n, :], R[:, n, :], RH[:, n, :], ALU.subtract).then_inc(s_r, 1)
                if n >= 2:
                    dve.wait_ge(s_b, n - 1)
                nc.vector.tensor_tensor(DH[:, n % 2, :, :], g.ident[:, :].unsqueeze(1).broadcast_to([P, TB, P]),
                                        RH[:, n, :].unsqueeze(2).broadcast_to([P, TB, P]), ALU.mult).then_inc(s_r, 1)

            def normalise(n):
                dve.wait_ge(s_b, n + 1)
                dve.wait_ge(s_sq, n + 1)
                y = YG[:, n % 2, cols(n)]
                nc.vector.scalar_tensor_tensor(out=y, in0=y, scalar=GN[n % 2], in1=r_ps[:, n % 2, :],
                                               op0=ALU.mult, op1=ALU.mult).then_inc(s_yn, 1)

            def finish(n):
                blk = n // 2
                if n % 2:
                    dve.wait_ge(s_o, blk + 1)
                    nc.vector.scalar_tensor_tensor(out=g.Y[:, cols(n)], in0=o_ps[:, blk % 2, :], scalar=g.vec["op_b"],
                                                   in1=g.H[:, cols(n)], op0=ALU.add, op1=ALU.add).then_inc(s_out, 1)

            steps((skip, 0), (inverse, 2), (normalise, 3), (finish, 5))


def stage_mamba(nc, g, m):
    with ExitStack() as ctx:
        sb, _, _ = alloc(nc, ctx)
        m.XBC, m.SZ = sb("XBC", [P, DIRS, 3, TOK]), sb("SZ", [P, DIRS, TOK])
        m.A2, m.trir = sb("A2", [P, TILES, 2, 4], F32R), sb("trir", [P, 4, P], F32R)
        m.DT, m.AA, m.EX = sb("DT", [P, TILES, 4]), sb("AA", [P, TILES, 4]), sb("EX", [P, 3, 4, TILES])
        stage_mamba_project(nc, g, m)
        with ExitStack() as inner:
            m.YB = inner.enter_context(nc.sbuf_tensor("YB", [P, DIRS, TOK], F32))
            stage_mamba_scan(nc, g, m)
            stage_mamba_output(nc, g, m)


def ffn_loads(d, sb):
    f = Shared()
    f.wr, f.br = sb("wr", [P, BLOCKS16]), sb("br", [P, BLOCKS16])
    f.w1, f.b1, f.w2 = sb("w1", [P, HID1]), sb("b1", [P, HID1 // P]), sb("w2", [P, HID1 // P, P])
    f.w1h, f.w1l = (sb(n, [P, HID1], F32R) for n in ("w1h", "w1l"))
    f.sel, f.identb = sb("fsel", [BLOCKS16, HID1], BF16), sb("fidentb", [P, P], BF16)
    return f, [(f.wr[:, :], d["wr"]), (f.br[:, :], d["br"]), (f.w1[:, :], d["w1T"]), (f.b1[:, :], d["b1"]),
               (f.w2[:, :, :], d["w2T"]), (f.sel[:, :], d["self"]), (f.identb[:, :], d["identb"])]


def stage_ffn(nc, g, f, out):
    CH = HID1 // P
    with ExitStack() as ctx:
        sb, ps, sem = alloc(nc, ctx)
        wr, br, b1, w2, sel, identb = f.wr, f.br, f.b1, f.w2, f.sel, f.identb
        Hh, Hl = sb("fHh", [P, TOK], F32R), sb("fHl", [P, TOK], F32R)
        shape = [P, TILES, BLOCKS16]
        V, MX, SM, RC = sb("fV", shape), sb("fMX", [P, TILES]), sb("fSM", [P, TILES]), sb("fRC", [P, TILES])
        PA, PR = sb("PA", [P, TILES, BLOCKS16 + FTOP]), sb("fPR", [P, TILES, BLOCKS16 + FTOP])
        T8, MK = sb("fT8", [P, TILES, 8]), sb("MK", shape, BF16)
        MKT = sb("MKT", [BLOCKS16, TOK], BF16)
        HR = sb("HR", [P, CH, TOK])
        lg = ps("flg", [P, 512])
        mt_ps = ps("mt_ps", [BLOCKS16, 8, P], BF16)
        h_ps, y_ps = ps("fh", [P, 4, BLK]), ps("fy", [P, 2, BLK])
        s_lg, s_v, s_exp, s_mt, s_mev, s_h, s_hr, s_mb, s_hm, s_y, s_yb, s_x, s_out = (
            sem("f_" + n) for n in ("lg", "v", "exp", "mt", "mev", "h", "hr", "mb", "hm", "y", "yb", "x", "out"))
        JOBS = BLKS * CH

        def cols(b):
            return slice(b * BLK, (b + 1) * BLK)
        block = ctx.enter_context(nc.Block())

        @block.sync
        def _(sp):
            for b in range(BLKS):
                sp.wait_ge(s_x, b + 1)
                sp.dma_start(out[:, cols(b)], g.X[:, cols(b)]).then_inc(s_out, 16)
            sp.wait_ge(s_out, 16 * BLKS)

        @block.tensor
        def _(pe):
            for t in range(TILES):
                mm = nc.tensor.matmul(lg[:, t * BLOCKS16:(t + 1) * BLOCKS16], g.H[:, t * P:(t + 1) * P], wr[:, :],
                                      start=True, stop=True)
            mm.then_inc(s_lg, 1)
            for J in range(JOBS):
                if J >= 4:
                    pe.wait_ge(s_hr, BLKS + J - 3)
                pe.wait_ge(s_v, J // CH + 1)
                rows, at = slice((J % CH) * P, (J % CH + 1) * P), cols(J // CH)
                nc.tensor.matmul(h_ps[:, J % 4, :], f.w1h[:, rows], Hh[:, at], start=True, stop=False)
                nc.tensor.matmul(h_ps[:, J % 4, :], f.w1h[:, rows], Hl[:, at], start=False, stop=False)
                nc.tensor.matmul(h_ps[:, J % 4, :], f.w1l[:, rows], Hh[:, at], start=False, stop=True).then_inc(s_h, 1)
            pe.wait_ge(s_v, FFN_STEPS)
            for half in range(2):
                if half:
                    pe.wait_ge(s_mev, 1)
                for t in range(8):
                    mm = nc.tensor.transpose(mt_ps[:, t, :], MK[:, 8 * half + t, :], identb[:, :])
                mm.then_inc(s_mt, 1)
            for J in range(JOBS + 1):
                if J < JOBS:
                    pe.wait_ge(s_mev, J // (JOBS // 2) + 1)
                    if J == 0:
                        pe.wait_ge(s_hr, BLKS + JOBS)
                    if J >= 2:
                        pe.wait_ge(s_hm, J - 1)
                    nc.tensor.matmul(h_ps[:, 2 + J % 2, :], sel[:, (J % CH) * P:(J % CH + 1) * P], MKT[:, cols(J // CH)],
                                     start=True, stop=True).then_inc(s_mb, 1)
                if J >= 1:
                    K = J - 1
                    b, c = K // CH, K % CH
                    pe.wait_ge(s_hm, K + 1)
                    if b >= 2 and c == 0:
                        pe.wait_ge(s_yb, b - 1)
                    mm = nc.tensor.matmul(y_ps[:, b % 2, :], w2[:, c, :], HR[:, c, cols(b)], start=(c == 0), stop=(c == CH - 1))
                    if c == CH - 1:
                        mm.then_inc(s_y, 1)

        @block.scalar
        def _(act):
            nc.scalar.preload_act_table(ACT.Exp)
            for b in range(BLKS):
                nc.scalar.activation(Hh[:, cols(b)], g.H[:, cols(b)], ACT.Copy).then_inc(s_hr, 1)
            for J in range(JOBS):
                if J == 4:
                    act.wait_ge(s_v, BLKS + 3)
                    nc.scalar.activation(V[:, :, :], V[:, :, :], ACT.Exp).then_inc(s_exp, 1)
                act.wait_ge(s_h, J + 1)
                nc.scalar.activation(HR[:, J % CH, cols(J // CH)], h_ps[:, J % 4, :], ACT.Relu,
                                     bias=b1[:, J % CH:J % CH + 1]).then_inc(s_hr, 1)
            for half in range(2):
                act.wait_ge(s_mt, half + 1)
                nc.scalar.activation(MKT[:, half * SEQ:(half + 1) * SEQ].rearrange("e (t k) -> e t k", t=8),
                                     mt_ps[:, :, :], ACT.Copy).then_inc(s_mev, 1)
            for b in range(BLKS):
                act.wait_ge(s_y, b + 1)
                nc.scalar.activation(g.Y[:, cols(b)], y_ps[:, b % 2, :], ACT.Identity, bias=g.vec["b2"]).then_inc(s_yb, 1)

        @block.vector
        def _(dve):
            n = 0

            def step(ins, wait=True):
                nonlocal n
                ins.then_inc(s_v, 1)
                n += 1
                if wait:
                    dve.wait_ge(s_v, n)

            for b in range(BLKS):
                dve.wait_ge(s_hr, b + 1)
                step(nc.vector.tensor_tensor(Hl[:, cols(b)], g.H[:, cols(b)], Hh[:, cols(b)], ALU.subtract), wait=False)
            over = lambda t: t[:, :].unsqueeze(2).broadcast_to(shape)
            dve.wait_ge(s_lg, 1)
            step(nc.vector.tensor_tensor(V[:, :, :], lg[:, 0:TILES * BLOCKS16].rearrange("p (t e) -> p t e", t=TILES),
                                         br[:, :].unsqueeze(1).broadcast_to(shape), ALU.add))
            step(nc.vector.tensor_reduce(MX[:, :], V[:, :, :], AX.X, ALU.max))
            step(nc.vector.tensor_tensor(V[:, :, :], V[:, :, :], over(MX), ALU.subtract))
            step(nc.vector.memset(PA[:, :, BLOCKS16:BLOCKS16 + 1], 2.0))
            for k in range(1, FTOP):
                step(nc.vector.memset(PA[:, :, BLOCKS16 + k:BLOCKS16 + k + 1], 2.0 + k))
            dve.wait_ge(s_exp, 1)
            step(nc.vector.tensor_reduce(SM[:, :], V[:, :, :], AX.X, ALU.add))
            step(nc.vector.reciprocal(RC[:, :], SM[:, :]))
            step(nc.vector.tensor_tensor(PA[:, :, 0:BLOCKS16], V[:, :, :], over(RC), ALU.mult))
            for t in range(TILES):
                step(nc.vector.max(T8[:, t, :], PA[:, t, :]), wait=(t == TILES - 1))
            for t in range(TILES):
                step(nc.vector.match_replace(PR[:, t, :], T8[:, t, :], PA[:, t, :], -1.0), wait=(t == TILES - 1))
            step(nc.vector.tensor_scalar(MK[:, :, :], PR[:, :, 0:BLOCKS16], -1.0, None, ALU.is_equal))
            assert n == FFN_STEPS, n
            for J in range(JOBS):
                at = HR[:, J % CH, cols(J // CH)]
                dve.wait_ge(s_mb, J + 1)
                dve.wait_ge(s_hr, BLKS + J + 1)
                nc.vector.tensor_tensor(at, at, h_ps[:, 2 + J % 2, :], ALU.mult).then_inc(s_hm, 1)
            for b in range(BLKS):
                batch = b * BLK // SEQ
                dve.wait_ge(s_yb, b + 1)
                nc.vector.scalar_tensor_tensor(out=g.X[:, cols(b)], in0=g.Y[:, cols(b)],
                                               scalar=g.mod[:, 1, 5, batch:batch + 1], in1=g.X[:, cols(b)],
                                               op0=ALU.mult, op1=ALU.add).then_inc(s_x, 1)


FFN_STEPS = BLKS + 43


VECS = ("g_norm", "norm_w", "op_b", "b2", "gn_f", "gn_b", "D_f", "D_b")


def program(nc, d, out):
    with ExitStack() as ctx:
        sb, _, _ = alloc(nc, ctx)
        g = Shared()
        g.X, g.H, g.Y = (sb(n, [P, TOK]) for n in ("X", "H", "Y"))
        g.U = sb("U", [P, TOK + ITER])
        g.mod, g.vecs = sb("mod", [P, 2, 6, BATCH]), sb("vecs", [P, len(VECS)])
        g.ident, g.center, g.ones = (sb(n, [P, P]) for n in ("ident", "center", "ones"))
        g.onesr = sb("onesr", [P, P], F32R)
        g.mean_col, g.eps = sb("mean_col", [P, 1]), sb("eps", [P, 2])
        g.eps5, g.eps_machine = g.eps[:, 0:1], g.eps[:, 1:2]
        g.vec = {n: g.vecs[:, i:i + 1] for i, n in enumerate(VECS)}
        stage_modulation(nc, d, g)
        with ExitStack() as scope:
            a, loads, splits = attention_loads(d, g, alloc(nc, scope)[0])
            stage_norm(nc, g, "n0", 0, 0, rms=(g.vec["g_norm"], g.eps_machine), loads=loads, splits=splits)
            stage_attention(nc, d, g, a)
        with ExitStack() as scope:
            r, loads = route_loads(d, alloc(nc, scope)[0])
            stage_norm(nc, g, "n1", 0, 1, residual=(0, 2), loads=loads)
            stage_moe(nc, d, g, r)
        with ExitStack() as scope:
            sb, _, sem = alloc(nc, scope)
            m, loads = mamba_loads(d, g, sb, sem)
            stage_norm(nc, g, "n2", 1, 0, rms=(g.vec["norm_w"], g.eps5), residual=(0, 5), loads=loads,
                       splits=[(m.wz[:, :, :], m.wzh[:, :, :], m.wzl[:, :, :])], copies=m.copies)
            stage_mamba(nc, g, m)
        with ExitStack() as scope:
            f, loads = ffn_loads(d, alloc(nc, scope)[0])
            stage_norm(nc, g, "n3", 1, 1, residual=(1, 2), loads=loads, splits=[(f.w1[:, :], f.w1h[:, :], f.w1l[:, :])])
            stage_ffn(nc, g, f, out)


def constants():
    def bits(a):
        return np.ascontiguousarray((np.ascontiguousarray(a, np.float32).view(np.uint32) >> 16).astype(np.uint16))
    inv = (1.0 / np.float32(10000.0) ** (np.arange(0, DH, 2, dtype=np.float32) / np.float32(DH))).astype(np.float32)
    ang = np.repeat(np.arange(SEQ, dtype=np.float32)[:, None] * inv, 2, axis=-1)
    sign = np.where(np.arange(DH) % 2 == 0, np.float32(-1), np.float32(1))
    cs = np.stack([np.cos(ang), np.sin(ang) * sign])
    cs = np.tile(cs.transpose(2, 1, 0), (2, BATCH, 1))
    cs = cs.reshape(P, ITERS, ITER, 2).transpose(1, 0, 3, 2).reshape(ITERS, P, 2 * ITER)
    i, j = np.arange(P)[:, None] % SEG, np.arange(KEYS)[None, :]
    mask = np.where((j >= SEG) | (j <= i), 0.0, -BIG)
    r, c = np.arange(P)[:, None], np.arange(P)[None, :]
    tri = np.stack([r <= c, r > c, r >= c, r < c], axis=1)
    sel = np.zeros((CHUNKS, P, P), np.float32)
    for ch in range(CHUNKS - 2):
        e = (ch * P + np.arange(P)) // FF
        sel[ch, e, np.arange(P)] = sel[ch, EXPERTS + e, np.arange(P)] = 1
    self_ = np.repeat(np.eye(BLOCKS16, dtype=np.float32), FBLK, axis=1)
    eye = np.eye(P, dtype=np.float32)
    f = lambda a: np.ascontiguousarray(a, np.float32)
    return {"cs": f(cs), "maskb": bits(np.tile(mask, (1, QG))), "identb": bits(eye), "ident": eye,
            "center": f(eye - np.float32(1 / P)), "tri": f(tri), "sel": f(sel),
            "self": bits(self_)}


def layouts(x, sel):
    a = {k: np.asarray(v) for k, v in x.items()}
    L = {}
    L["xT"] = a["L0_attn_seq"].reshape(TOK, P).T
    L["ct"] = np.stack([a["L0_c"].T, a["L1_c"].T], 1)
    L["wmod"] = np.stack([a["L0_wmod"], a["L1_wmod"]], 1)
    L["vecs"] = np.stack([a["L0_attn_g_norm"], a["L1_attn_norm_w"], a["L1_attn_op_b"], a["L1_ffn_b2"],
                          a["L1_attn_f_gnorm_w"], a["L1_attn_b_gnorm_w"],
                          np.repeat(a["L1_attn_f_D"], HD), np.repeat(a["L1_attn_b_D"], HD)], 1)
    w = a["L0_attn_W_qkv"]
    L["wqk"] = w[:, 0:2 * HEADS * DH].reshape(P, 2, 2, 4 * P).transpose(0, 2, 1, 3).reshape(P, 2 * HEADS * DH)
    L["wv"] = w[:, 2 * HEADS * DH:]
    L["wo"] = a["L0_attn_W_out"].reshape(PAIRS, P, P).transpose(1, 0, 2)
    pm = a["L0_attn_pm"]
    L["pmk"] = pm[0].reshape(PAIRS, 2, PM, DH).transpose(1, 3, 0, 2).reshape(P, PAIRS, PM)
    L["pmv"] = pm[1].transpose(1, 0, 2).reshape(PM, HEADS * DH)
    L["gateT"] = a["L0_ffn_gate_w"].T
    L["gbias"] = np.broadcast_to(a["L0_ffn_gate_bias"], (P, EXPERTS))

    def hidden(e, s):
        s = np.concatenate([s.reshape(2, FF, P), np.zeros((2, P - FF, P), s.dtype)], 1)
        return np.concatenate([e.reshape(-1, P), s.reshape(-1, P)]).reshape(CHUNKS, P, P)
    wg = hidden(a["L0_ffn_Wg"], a["L0_ffn_Sg"]).transpose(0, 2, 1)
    wu = hidden(a["L0_ffn_Wu"], a["L0_ffn_Su"]).transpose(0, 2, 1)
    wd = hidden(a["L0_ffn_Wd"].transpose(0, 2, 1), a["L0_ffn_Sd"].T)
    L["w4"] = np.stack([wg, wu, wd, sel], 2).reshape(CHUNKS, P, 4 * P)
    dirs = ("f", "b")
    inw = [a[f"L1_attn_{k}_in_w"].T for k in dirs]
    L["wxbc"] = np.stack([np.concatenate([m[:, P:4 * P]] * 2, 0) for m in inw], 1)
    L["wz"] = np.stack([np.concatenate([m[:, 0:P], np.zeros((HD, P), m.dtype)]) for m in inw], 1)
    wdt = np.zeros((P, 4), np.float32)
    wdt[0:HD, 0:2], wdt[HD:P, 2:4] = inw[0][:, 4 * P:], inw[1][:, 4 * P:]
    L["wdt"] = wdt
    cw = [a[f"L1_attn_{k}_conv_w"].T for k in dirs]
    L["cw"] = np.stack([np.stack([np.repeat(m[[3 - 2 * q, 2 - 2 * q]], HD, axis=0) for q in range(2)], 1) for m in cw], 1)
    L["cb"] = np.stack([a[f"L1_attn_{k}_conv_b"].reshape(3, P).T for k in dirs], 1)
    L["dtb"] = np.broadcast_to(np.concatenate([a[f"L1_attn_{k}_dt_bias"] for k in dirs]), (P, 4))
    L["alog"] = np.broadcast_to(np.concatenate([a[f"L1_attn_{k}_A_log"] for k in dirs]), (P, 4))
    L["wp"] = np.stack([a[f"L1_attn_{k}_outp_w"].T for k in dirs], 1)
    L["opT"] = a["L1_attn_op_w"].T
    L["wr"] = a["L1_ffn_w_router"]
    L["br"] = np.broadcast_to(a["L1_ffn_b_router"], (P, BLOCKS16))
    L["w1T"] = a["L1_ffn_w1"].T
    L["b1"] = a["L1_ffn_b1"].reshape(HID1 // P, P).T
    L["w2T"] = a["L1_ffn_w2"].T.reshape(HID1 // P, P, P).transpose(1, 0, 2)
    return {k: np.ascontiguousarray(v) for k, v in L.items()}


def kernel(**inputs):
    import concourse.bacc as bacc
    from concourse.bass_utils import run_bass_kernel_spmd

    tables = constants()
    arrays = {**layouts(inputs, tables.pop("sel")), **tables}
    nc = bacc.Bacc("TRN2", target_bir_lowering=False, num_devices=1)
    aps = {n: nc.dram_tensor(f"in_{n}", a.shape, mybir.dt.from_np(a.dtype), kind="ExternalInput").ap()
           for n, a in arrays.items()}
    d = {n: ap.bitcast(BF16) if arrays[n].dtype == np.uint16 else ap for n, ap in aps.items()}
    out = nc.dram_tensor("out_xT", (P, TOK), F32, kind="ExternalOutput").ap()
    program(nc, d, out)
    r = run_bass_kernel_spmd(nc, [{f"in_{n}": a for n, a in arrays.items()}], core_ids=[0])
    return np.ascontiguousarray(r.results[0]["out_xT"].T).reshape(BATCH, SEQ, P)
```
